# Optimizing a Trainium2 kernel written in Bass

```python
import numpy as np
import jax
import jax.numpy as jnp

def _softmax(x, axis=-1):
    return jax.nn.softmax(x, axis=axis)

def _gelu(x):
    return jax.nn.gelu(x, approximate=True)

def _silu(x):
    return jax.nn.silu(x)

def _sigmoid(x):
    return jax.nn.sigmoid(x)

def _layernorm(x, axis=-1, eps=1e-05):
    m = jnp.mean(x, axis=axis, keepdims=True)
    v = jnp.var(x, axis=axis, keepdims=True)
    return (x - m) / jnp.sqrt(v + eps)

def _scatter_add(tgt, idx, src, axis=0):
    return tgt.at[idx].add(src)

def _segment_sum(src, seg, n):
    return jax.ops.segment_sum(src, seg, n)
kernel_name = 'mk_seq_preln_d4_jaxref_r8_b72d04'

def setup_inputs(seed: int=0):
    np.random.seed(seed)
    _w = jnp.asarray

    def _L0_attn_setup():
        import jax, jax.numpy as jnp
        import numpy as np
        B, L, D, H, K = (4, 256, 128, 16, 3)
        HEAD_DIM = D // H
        LN_EPS = 1e-05
        key = jax.random.key(seed)
        ks = jax.random.split(key, 12)
        w = lambda k, shp: jax.random.normal(k, shp, jnp.float32) * shp[-1] ** (-0.5)
        return {'x': jax.random.normal(ks[0], (B, L, D), jnp.float32), 'band_importance': jax.random.normal(ks[1], (1, L), jnp.float32) * 0.02, 'Wq': w(ks[2], (D, D)), 'bq': jnp.zeros((D,), jnp.float32), 'Wk': w(ks[3], (D, D)), 'bk': jnp.zeros((D,), jnp.float32), 'Wv': w(ks[4], (D, D)), 'bv': jnp.zeros((D,), jnp.float32), 'Wo': w(ks[5], (D, D)), 'bo': jnp.zeros((D,), jnp.float32), 'gamma': jnp.ones((D,), jnp.float32), 'beta': jnp.zeros((D,), jnp.float32)}
    _L0_attn_in = _L0_attn_setup()

    def _L0_ffn_setup():
        import jax, jax.numpy as jnp
        import numpy as np
        IN_DIM = 128
        OUT_DIM = 128
        NUM_EXPERTS = 8
        TOP_K = 2
        key = jax.random.key(seed)
        ks = jax.random.split(key, 5)
        s = 1.0 / np.sqrt(IN_DIM)
        x = jax.random.normal(ks[0], (4, 256, IN_DIM), dtype=jnp.float32)
        Wg = jax.random.uniform(ks[1], (IN_DIM, NUM_EXPERTS), jnp.float32, -s, s)
        bg = jnp.zeros((NUM_EXPERTS,), jnp.float32)
        We = jax.random.uniform(ks[2], (NUM_EXPERTS, OUT_DIM, IN_DIM), jnp.float32, -s, s)
        be = jax.random.uniform(ks[3], (NUM_EXPERTS, OUT_DIM), jnp.float32, -s, s)
        return {'x': x, 'Wg': Wg, 'bg': bg, 'We': We, 'be': be}
    _L0_ffn_in = _L0_ffn_setup()

    def _L1_attn_setup():
        import math
        import jax, jax.numpy as jnp
        import numpy as np
        D_MODEL = 128
        NHEAD = 16
        DK = D_MODEL // NHEAD
        FACTOR = 5
        B, L = (4, 1024)
        U = max(1, min(FACTOR * math.ceil(math.log(L + 1)), L))
        key = jax.random.key(seed)
        ks = jax.random.split(key, 10)
        s = 1.0 / math.sqrt(D_MODEL)
        inp = {'x': jax.random.normal(ks[0], (B, L, D_MODEL), dtype=jnp.float32), 'Wq': jax.random.normal(ks[1], (D_MODEL, D_MODEL), dtype=jnp.float32) * s, 'bq': jnp.zeros((D_MODEL,), dtype=jnp.float32), 'Wk': jax.random.normal(ks[2], (D_MODEL, D_MODEL), dtype=jnp.float32) * s, 'bk': jnp.zeros((D_MODEL,), dtype=jnp.float32), 'Wv': jax.random.normal(ks[3], (D_MODEL, D_MODEL), dtype=jnp.float32) * s, 'bv': jnp.zeros((D_MODEL,), dtype=jnp.float32), 'Wo': jax.random.normal(ks[4], (D_MODEL, D_MODEL), dtype=jnp.float32) * s, 'bo': jnp.zeros((D_MODEL,), dtype=jnp.float32), 'idx_k': jax.random.permutation(ks[5], L)[:U].astype(jnp.int32)}
        return inp
    _L1_attn_in = _L1_attn_setup()

    def _L1_ffn_setup():
        import jax, jax.numpy as jnp
        import numpy as np
        D_MODEL, FF_DIM = (128, 256)
        N_SHARED, N_ROUTED, TOP_K = (1, 8, 2)
        BATCH, SEQ = (2, 256)
        key = jax.random.key(seed)
        ks = jax.random.split(key, 8)
        init = lambda k, shape: jax.random.normal(k, shape, jnp.float32) * 0.02
        x = jax.random.normal(ks[0], (BATCH, SEQ, D_MODEL), jnp.float32)
        Wg = init(ks[1], (D_MODEL, N_ROUTED))
        Ws1 = init(ks[2], (D_MODEL, FF_DIM))
        Ws3 = init(ks[3], (D_MODEL, FF_DIM))
        Ws2 = init(ks[4], (FF_DIM, D_MODEL))
        We1 = init(ks[5], (N_ROUTED, D_MODEL, FF_DIM))
        We3 = init(ks[6], (N_ROUTED, D_MODEL, FF_DIM))
        We2 = init(ks[7], (N_ROUTED, FF_DIM, D_MODEL))
        return {'x': x, 'Wg': Wg, 'Ws1': Ws1, 'Ws3': Ws3, 'Ws2': Ws2, 'We1': We1, 'We3': We3, 'We2': We2}
    _L1_ffn_in = _L1_ffn_setup()

    def _L2_attn_setup():
        import jax, jax.numpy as jnp
        import numpy as np
        DT_MIN, DT_MAX = (0.001, 0.1)
        DT_RANK, D_STATE, D_CONV = (64, 16, 4)
        key = jax.random.key(seed)
        ks = jax.random.split(key, 8)
        B, T, Dm = (4, 512, 128)
        Dn = 2 * Dm
        s = lambda k, shape, scale=0.02: jax.random.normal(k, shape, jnp.float32) * scale
        return {'x': jax.random.normal(ks[0], (B, T, Dm), jnp.float32), 'W_in': s(ks[1], (2 * Dn, Dm)), 'conv_w': s(ks[2], (Dn, 1, D_CONV), 0.1), 'conv_b': jnp.zeros((Dn,), jnp.float32), 'W_x': s(ks[3], (DT_RANK + 2 * D_STATE, Dn)), 'W_dt': s(ks[4], (Dn, DT_RANK)), 'b_dt': jnp.zeros((Dn,), jnp.float32), 'log_A': jax.random.uniform(ks[5], (Dn, D_STATE), jnp.float32), 'D_param': jnp.ones((Dn,), jnp.float32), 'W_out': s(ks[6], (Dm, Dn)), 'ln_w': jnp.ones((Dm,), jnp.float32), 'ln_b': jnp.zeros((Dm,), jnp.float32)}
    _L2_attn_in = _L2_attn_setup()

    def _L2_ffn_setup():
        import jax, jax.numpy as jnp
        import numpy as np
        D = 128
        LW = 16
        DEPTH = 8
        NN = 2 ** DEPTH - 1
        NL = 2 ** DEPTH
        B, S = (2, 128)

        def _fff(x, nw, nb, w1, b1, w2, b2, act):
            node = jnp.zeros(x.shape[:2], dtype=jnp.int32)
            for _ in range(DEPTH):
                logit = jnp.einsum('bsd,bsd->bs', x, nw[node]) + nb[node]
                node = 2 * node + 1 + (logit > 0).astype(jnp.int32)
            leaf = node - NN
            h = act(jnp.einsum('bsd,bsdl->bsl', x, w1[leaf]) + b1[leaf])
            return jnp.einsum('bsl,bsld->bsd', h, w2[leaf]) + b2[leaf]

        def _forward(x, q_nw, q_nb, q_w1, q_b1, q_w2, q_b2, k_nw, k_nb, k_w1, k_b1, k_w2, k_b2, v_nw, v_nb, v_w1, v_b1, v_w2, v_b2, f_nw, f_nb, f_w1, f_b1, f_w2, f_b2):
            mu = jnp.mean(x, -1, keepdims=True)
            sd = jnp.std(x, -1, ddof=1, keepdims=True)
            xn = (x - mu) / jnp.sqrt(sd + 1e-05)
            relu = jax.nn.relu
            q = _fff(xn, q_nw, q_nb, q_w1, q_b1, q_w2, q_b2, relu)
            k = _fff(xn, k_nw, k_nb, k_w1, k_b1, k_w2, k_b2, relu)
            v = _fff(xn, v_nw, v_nb, v_w1, v_b1, v_w2, v_b2, relu)
            att = jax.nn.softmax(jnp.einsum('bqd,bkd->bqk', q, k) / jnp.sqrt(jnp.float32(D)), axis=-1)
            y = xn + jnp.einsum('bqk,bkd->bqd', att, v)
            gelu = lambda t: jax.nn.gelu(t, approximate=False)
            return y + _fff(y, f_nw, f_nb, f_w1, f_b1, f_w2, f_b2, gelu)

        def _make_fff_params(key, scale_in, scale_leaf):
            ks = jax.random.split(key, 4)
            nw = jax.random.normal(ks[0], (NN, D), jnp.float32) * scale_in
            nb = jnp.zeros((NN,), jnp.float32)
            w1 = jax.random.normal(ks[1], (NL, D, LW), jnp.float32) * scale_in
            b1 = jax.random.normal(ks[2], (NL, LW), jnp.float32) * 0.01
            w2 = jax.random.normal(ks[3], (NL, LW, D), jnp.float32) * scale_leaf
            b2 = jnp.zeros((NL, D), jnp.float32)
            return (nw, nb, w1, b1, w2, b2)
        key = jax.random.key(seed)
        kx, kq, kk, kv, kf = jax.random.split(key, 5)
        s_in = 1.0 / np.sqrt(D)
        s_lf = 1.0 / np.sqrt(LW)
        inp = {'x': jax.random.normal(kx, (B, S, D), jnp.float32)}
        for name, kk_ in (('q', kq), ('k', kk), ('v', kv), ('f', kf)):
            nw, nb, w1, b1, w2, b2 = _make_fff_params(kk_, s_in, s_lf)
            inp.update({f'{name}_nw': nw, f'{name}_nb': nb, f'{name}_w1': w1, f'{name}_b1': b1, f'{name}_w2': w2, f'{name}_b2': b2})
        return inp
    _L2_ffn_in = _L2_ffn_setup()

    def _L3_attn_setup():
        import jax, jax.numpy as jnp
        import numpy as np
        B, T, C = (2, 256, 128)
        NH = 16
        HD = C // NH

        def build_alibi_bias(n_head, max_len):
            slopes = jnp.arange(1, n_head + 1, dtype=jnp.float32) / n_head
            ar = jnp.arange(max_len, dtype=jnp.float32)
            return slopes[:, None, None] * (ar[None, None, :] - ar[None, :, None])
        key = jax.random.key(seed)
        ks = jax.random.split(key, 7)
        s = 0.02
        return {'x': jax.random.normal(ks[0], (B, T, C), dtype=jnp.float32), 'q_w': jax.random.normal(ks[1], (C, C), dtype=jnp.float32) * s, 'q_b': jnp.zeros((C,), dtype=jnp.float32), 'kv_w': jax.random.normal(ks[2], (C, 2 * C), dtype=jnp.float32) * s, 'kv_b': jnp.zeros((2 * C,), dtype=jnp.float32), 'o_w': jax.random.normal(ks[3], (C, C), dtype=jnp.float32) * s, 'o_b': jnp.zeros((C,), dtype=jnp.float32)}
    _L3_attn_in = _L3_attn_setup()

    def _L3_ffn_setup():
        import jax, jax.numpy as jnp
        import numpy as np
        TOP_K = 2
        TEMP = 0.9
        EPS = 1e-05
        B, S, D, F, E = (2, 256, 128, 512, 8)

        def _moe_forward(x, gate_w, gate_b, w1, b1, w2, b2, ln_g, ln_b):
            logits = (x @ gate_w + gate_b) / TEMP
            topk_vals, topk_idx = jax.lax.top_k(logits, TOP_K)
            keep = jax.nn.one_hot(topk_idx, E, dtype=jnp.bool_).any(-2)
            masked = jnp.where(keep, logits, -jnp.inf)
            gate_probs = jax.nn.softmax(masked, axis=-1)
            h = jnp.einsum('bsd,edf->bsef', x, w1) + b1
            h = jax.nn.gelu(h, approximate=False)
            expert_out = jnp.einsum('bsef,efd->bsed', h, w2) + b2
            out = jnp.einsum('bse,bsed->bsd', gate_probs, expert_out)
            mu = out.mean(-1, keepdims=True)
            var = out.var(-1, keepdims=True)
            out = (out - mu) / jnp.sqrt(var + EPS) * ln_g + ln_b
            return out
        key = jax.random.key(seed)
        ks = jax.random.split(key, 4)
        scale_in = 1.0 / np.sqrt(D)
        scale_ff = 1.0 / np.sqrt(F)
        return {'x': jax.random.normal(ks[0], (B, S, D), jnp.float32), 'gate_w': jax.random.normal(ks[1], (D, E), jnp.float32) * scale_in, 'gate_b': jnp.zeros((E,), jnp.float32), 'w1': jax.random.normal(ks[2], (E, D, F), jnp.float32) * scale_in, 'b1': jnp.zeros((E, F), jnp.float32), 'w2': jax.random.normal(ks[3], (E, F, D), jnp.float32) * scale_ff, 'b2': jnp.zeros((E, D), jnp.float32), 'ln_g': jnp.ones((D,), jnp.float32), 'ln_b': jnp.zeros((D,), jnp.float32)}
    _L3_ffn_in = _L3_ffn_setup()
    _d = {'L0_attn_x': _L0_attn_in['x'], 'L0_attn_band_importance': _L0_attn_in['band_importance'], 'L0_attn_Wq': _L0_attn_in['Wq'], 'L0_attn_bq': _L0_attn_in['bq'], 'L0_attn_Wk': _L0_attn_in['Wk'], 'L0_attn_bk': _L0_attn_in['bk'], 'L0_attn_Wv': _L0_attn_in['Wv'], 'L0_attn_bv': _L0_attn_in['bv'], 'L0_attn_Wo': _L0_attn_in['Wo'], 'L0_attn_bo': _L0_attn_in['bo'], 'L0_attn_gamma': _L0_attn_in['gamma'], 'L0_attn_beta': _L0_attn_in['beta'], 'L0_ffn_Wg': _L0_ffn_in['Wg'], 'L0_ffn_bg': _L0_ffn_in['bg'], 'L0_ffn_We': _L0_ffn_in['We'], 'L0_ffn_be': _L0_ffn_in['be'], 'L1_attn_Wq': _L1_attn_in['Wq'], 'L1_attn_bq': _L1_attn_in['bq'], 'L1_attn_Wk': _L1_attn_in['Wk'], 'L1_attn_bk': _L1_attn_in['bk'], 'L1_attn_Wv': _L1_attn_in['Wv'], 'L1_attn_bv': _L1_attn_in['bv'], 'L1_attn_Wo': _L1_attn_in['Wo'], 'L1_attn_bo': _L1_attn_in['bo'], 'L1_attn_idx_k': _L1_attn_in['idx_k'], 'L1_ffn_Wg': _L1_ffn_in['Wg'], 'L1_ffn_Ws1': _L1_ffn_in['Ws1'], 'L1_ffn_Ws3': _L1_ffn_in['Ws3'], 'L1_ffn_Ws2': _L1_ffn_in['Ws2'], 'L1_ffn_We1': _L1_ffn_in['We1'], 'L1_ffn_We3': _L1_ffn_in['We3'], 'L1_ffn_We2': _L1_ffn_in['We2'], 'L2_attn_W_in': _L2_attn_in['W_in'], 'L2_attn_conv_w': _L2_attn_in['conv_w'], 'L2_attn_conv_b': _L2_attn_in['conv_b'], 'L2_attn_W_x': _L2_attn_in['W_x'], 'L2_attn_W_dt': _L2_attn_in['W_dt'], 'L2_attn_b_dt': _L2_attn_in['b_dt'], 'L2_attn_log_A': _L2_attn_in['log_A'], 'L2_attn_D_param': _L2_attn_in['D_param'], 'L2_attn_W_out': _L2_attn_in['W_out'], 'L2_attn_ln_w': _L2_attn_in['ln_w'], 'L2_attn_ln_b': _L2_attn_in['ln_b'], 'L2_ffn_q_nw': _L2_ffn_in['q_nw'], 'L2_ffn_q_nb': _L2_ffn_in['q_nb'], 'L2_ffn_q_w1': _L2_ffn_in['q_w1'], 'L2_ffn_q_b1': _L2_ffn_in['q_b1'], 'L2_ffn_q_w2': _L2_ffn_in['q_w2'], 'L2_ffn_q_b2': _L2_ffn_in['q_b2'], 'L2_ffn_k_nw': _L2_ffn_in['k_nw'], 'L2_ffn_k_nb': _L2_ffn_in['k_nb'], 'L2_ffn_k_w1': _L2_ffn_in['k_w1'], 'L2_ffn_k_b1': _L2_ffn_in['k_b1'], 'L2_ffn_k_w2': _L2_ffn_in['k_w2'], 'L2_ffn_k_b2': _L2_ffn_in['k_b2'], 'L2_ffn_v_nw': _L2_ffn_in['v_nw'], 'L2_ffn_v_nb': _L2_ffn_in['v_nb'], 'L2_ffn_v_w1': _L2_ffn_in['v_w1'], 'L2_ffn_v_b1': _L2_ffn_in['v_b1'], 'L2_ffn_v_w2': _L2_ffn_in['v_w2'], 'L2_ffn_v_b2': _L2_ffn_in['v_b2'], 'L2_ffn_f_nw': _L2_ffn_in['f_nw'], 'L2_ffn_f_nb': _L2_ffn_in['f_nb'], 'L2_ffn_f_w1': _L2_ffn_in['f_w1'], 'L2_ffn_f_b1': _L2_ffn_in['f_b1'], 'L2_ffn_f_w2': _L2_ffn_in['f_w2'], 'L2_ffn_f_b2': _L2_ffn_in['f_b2'], 'L3_attn_q_w': _L3_attn_in['q_w'], 'L3_attn_q_b': _L3_attn_in['q_b'], 'L3_attn_kv_w': _L3_attn_in['kv_w'], 'L3_attn_kv_b': _L3_attn_in['kv_b'], 'L3_attn_o_w': _L3_attn_in['o_w'], 'L3_attn_o_b': _L3_attn_in['o_b'], 'L3_ffn_gate_w': _L3_ffn_in['gate_w'], 'L3_ffn_gate_b': _L3_ffn_in['gate_b'], 'L3_ffn_w1': _L3_ffn_in['w1'], 'L3_ffn_b1': _L3_ffn_in['b1'], 'L3_ffn_w2': _L3_ffn_in['w2'], 'L3_ffn_b2': _L3_ffn_in['b2'], 'L3_ffn_ln_g': _L3_ffn_in['ln_g'], 'L3_ffn_ln_b': _L3_ffn_in['ln_b']}
    _x0 = _d['L0_attn_x']
    _d['L0_attn_x'] = jax.random.normal(jax.random.fold_in(jax.random.key(seed), 1), (8, 512, 128), dtype=_x0.dtype)
    del _x0
    return _d

def reference(L0_attn_x, L0_attn_band_importance, L0_attn_Wq, L0_attn_bq, L0_attn_Wk, L0_attn_bk, L0_attn_Wv, L0_attn_bv, L0_attn_Wo, L0_attn_bo, L0_attn_gamma, L0_attn_beta, L0_ffn_Wg, L0_ffn_bg, L0_ffn_We, L0_ffn_be, L1_attn_Wq, L1_attn_bq, L1_attn_Wk, L1_attn_bk, L1_attn_Wv, L1_attn_bv, L1_attn_Wo, L1_attn_bo, L1_attn_idx_k, L1_ffn_Wg, L1_ffn_Ws1, L1_ffn_Ws3, L1_ffn_Ws2, L1_ffn_We1, L1_ffn_We3, L1_ffn_We2, L2_attn_W_in, L2_attn_conv_w, L2_attn_conv_b, L2_attn_W_x, L2_attn_W_dt, L2_attn_b_dt, L2_attn_log_A, L2_attn_D_param, L2_attn_W_out, L2_attn_ln_w, L2_attn_ln_b, L2_ffn_q_nw, L2_ffn_q_nb, L2_ffn_q_w1, L2_ffn_q_b1, L2_ffn_q_w2, L2_ffn_q_b2, L2_ffn_k_nw, L2_ffn_k_nb, L2_ffn_k_w1, L2_ffn_k_b1, L2_ffn_k_w2, L2_ffn_k_b2, L2_ffn_v_nw, L2_ffn_v_nb, L2_ffn_v_w1, L2_ffn_v_b1, L2_ffn_v_w2, L2_ffn_v_b2, L2_ffn_f_nw, L2_ffn_f_nb, L2_ffn_f_w1, L2_ffn_f_b1, L2_ffn_f_w2, L2_ffn_f_b2, L3_attn_q_w, L3_attn_q_b, L3_attn_kv_w, L3_attn_kv_b, L3_attn_o_w, L3_attn_o_b, L3_ffn_gate_w, L3_ffn_gate_b, L3_ffn_w1, L3_ffn_b1, L3_ffn_w2, L3_ffn_b2, L3_ffn_ln_g, L3_ffn_ln_b):

    def _L0_attn_ref(x, band_importance, Wq, bq, Wk, bk, Wv, bv, Wo, bo, gamma, beta):
        import jax, jax.numpy as jnp
        import numpy as np
        B, L, D, H, K = (4, 256, 128, 16, 3)
        HEAD_DIM = D // H
        LN_EPS = 1e-05
        Bx, Lx, Dx = x.shape
        hd = Dx // H
        imp = jax.nn.softmax(band_importance, axis=-1)[0]
        _, idx = jax.lax.top_k(imp, K)
        col_mask = jnp.zeros((Lx,), bool).at[idx].set(True)
        bias = jnp.where(col_mask, -jnp.inf, 0.0).astype(x.dtype)
        q = (x @ Wq.T + bq).reshape(Bx, Lx, H, hd)
        k_ = (x @ Wk.T + bk).reshape(Bx, Lx, H, hd)
        v = (x @ Wv.T + bv).reshape(Bx, Lx, H, hd)
        scale = 1.0 / np.sqrt(hd)
        scores = jnp.einsum('bqhd,bkhd->bhqk', q, k_) * scale + bias[None, None, None, :]
        attn = jax.nn.softmax(scores, axis=-1)
        ctx = jnp.einsum('bhqk,bkhd->bqhd', attn, v).reshape(Bx, Lx, Dx)
        attn_out = ctx @ Wo.T + bo
        y = x + attn_out
        mu = jnp.mean(y, axis=-1, keepdims=True)
        var = jnp.mean((y - mu) ** 2, axis=-1, keepdims=True)
        return (y - mu) * jax.lax.rsqrt(var + LN_EPS) * gamma + beta

    def _L0_ffn_ref(x, Wg, bg, We, be):
        import jax, jax.numpy as jnp
        import numpy as np
        IN_DIM = 128
        OUT_DIM = 128
        NUM_EXPERTS = 8
        TOP_K = 2
        gate = jax.nn.softmax(x @ Wg + bg, axis=-1)
        topk_vals, topk_idx = jax.lax.top_k(gate, TOP_K)
        onehot = jax.nn.one_hot(topk_idx, NUM_EXPERTS, dtype=gate.dtype)
        gate_sparse = jnp.einsum('bsk,bske->bse', topk_vals, onehot)
        gate_sparse = gate_sparse / jnp.sum(gate_sparse, axis=-1, keepdims=True)
        y = jnp.einsum('bsi,eoi->bseo', x, We) + be[None, None, :, :].transpose(0, 1, 2, 3)
        out = jnp.einsum('bseo,bse->bso', y, gate_sparse)
        return out

    def _L1_attn_ref(x, Wq, bq, Wk, bk, Wv, bv, Wo, bo, idx_k):
        import math
        import jax, jax.numpy as jnp
        import numpy as np
        D_MODEL = 128
        NHEAD = 16
        DK = D_MODEL // NHEAD
        FACTOR = 5
        B, L = (4, 1024)
        U = max(1, min(FACTOR * math.ceil(math.log(L + 1)), L))
        Bv, Lv, _ = x.shape
        H, dk = (NHEAD, DK)
        u = idx_k.shape[0]
        scale = 1.0 / math.sqrt(dk)
        Q = (x @ Wq.T + bq).reshape(Bv, Lv, H, dk).transpose(0, 2, 1, 3)
        K = (x @ Wk.T + bk).reshape(Bv, Lv, H, dk).transpose(0, 2, 1, 3)
        V = (x @ Wv.T + bv).reshape(Bv, Lv, H, dk).transpose(0, 2, 1, 3)
        K_samp = K[:, :, idx_k, :]
        scores = jnp.einsum('bhld,bhud->bhlu', Q, K_samp) * scale
        M = scores.max(-1) - scores.mean(-1)
        _, top_idx = jax.lax.top_k(M, u)
        Q_top = jnp.take_along_axis(Q, top_idx[..., None], axis=2)
        attn = jax.nn.softmax(jnp.einsum('bhud,bhld->bhul', Q_top, K) * scale, axis=-1)
        ctx_top = jnp.einsum('bhul,bhld->bhud', attn, V)
        ctx = jnp.broadcast_to(V.mean(axis=2, keepdims=True), (Bv, H, Lv, dk))
        bidx = jnp.arange(Bv)[:, None, None]
        hidx = jnp.arange(H)[None, :, None]
        ctx = ctx.at[bidx, hidx, top_idx].set(ctx_top)
        ctx = ctx.transpose(0, 2, 1, 3).reshape(Bv, Lv, H * dk)
        return ctx @ Wo.T + bo

    def _L1_ffn_ref(x, Wg, Ws1, Ws3, Ws2, We1, We3, We2):
        import jax, jax.numpy as jnp
        import numpy as np
        D_MODEL, FF_DIM = (128, 256)
        N_SHARED, N_ROUTED, TOP_K = (1, 8, 2)
        BATCH, SEQ = (2, 256)
        B, S, d = x.shape
        E = Wg.shape[1]
        xf = x.reshape(-1, d)
        T = xf.shape[0]
        gates = jax.nn.sigmoid(xf @ Wg)
        vals, idx = jax.lax.top_k(gates, TOP_K)
        vals = vals / vals.sum(axis=-1, keepdims=True)
        w = jnp.zeros((T, E), x.dtype).at[jnp.arange(T)[:, None], idx].add(vals)
        shared = jax.nn.silu(xf @ Ws1) * (xf @ Ws3) @ Ws2
        h = jax.nn.silu(jnp.einsum('td,edf->tef', xf, We1)) * jnp.einsum('td,edf->tef', xf, We3)
        routed = jnp.einsum('tef,efd,te->td', h, We2, w)
        out = (shared + routed) / (N_SHARED + TOP_K)
        return out.reshape(B, S, d)

    def _L2_attn_ref(x, W_in, conv_w, conv_b, W_x, W_dt, b_dt, log_A, D_param, W_out, ln_w, ln_b):
        import jax, jax.numpy as jnp
        import numpy as np
        DT_MIN, DT_MAX = (0.001, 0.1)
        DT_RANK, D_STATE, D_CONV = (64, 16, 4)
        B, T, Dm = x.shape
        Dn = W_dt.shape[0]
        residual = x
        mu = x.mean(-1, keepdims=True)
        var = x.var(-1, keepdims=True)
        xn = (x - mu) / jnp.sqrt(var + 1e-05) * ln_w + ln_b
        xz = xn @ W_in.T
        x_inner, z = jnp.split(xz, 2, axis=-1)
        xc = jnp.transpose(x_inner, (0, 2, 1))
        xc = jax.lax.conv_general_dilated(xc, conv_w, window_strides=(1,), padding=[(D_CONV - 1, 0)], dimension_numbers=('NCH', 'OIH', 'NCH'), feature_group_count=Dn)
        xc = xc + conv_b[None, :, None]
        u = jax.nn.silu(jnp.transpose(xc, (0, 2, 1)))
        xbc = u @ W_x.T
        dt_low, B_ssm, C_ssm = jnp.split(xbc, [DT_RANK, DT_RANK + D_STATE], axis=-1)
        dt = jax.nn.softplus(dt_low @ W_dt.T + b_dt) + DT_MIN
        dt = jnp.clip(dt, DT_MIN, DT_MAX)
        A = -jnp.exp(log_A)

        def step(h, inp):
            dt_t, u_t, B_t, C_t = inp
            dA = jnp.exp(dt_t[:, :, None] * A)
            h = dA * h + (dt_t * u_t)[:, :, None] * B_t[:, None, :]
            y = jnp.einsum('bdn,bn->bd', h, C_t)
            return (h, y)
        h0 = jnp.zeros((B, Dn, D_STATE), x.dtype)
        _, ys = jax.lax.scan(step, h0, (jnp.moveaxis(dt, 1, 0), jnp.moveaxis(u, 1, 0), jnp.moveaxis(B_ssm, 1, 0), jnp.moveaxis(C_ssm, 1, 0)))
        y = jnp.moveaxis(ys, 0, 1)
        y = y + u * D_param
        y = y * jax.nn.silu(z)
        return y @ W_out.T + residual

    def _L2_ffn_ref(x, q_nw, q_nb, q_w1, q_b1, q_w2, q_b2, k_nw, k_nb, k_w1, k_b1, k_w2, k_b2, v_nw, v_nb, v_w1, v_b1, v_w2, v_b2, f_nw, f_nb, f_w1, f_b1, f_w2, f_b2):
        import jax, jax.numpy as jnp
        import numpy as np
        D = 128
        LW = 16
        DEPTH = 8
        NN = 2 ** DEPTH - 1
        NL = 2 ** DEPTH
        B, S = (2, 128)

        def _fff(x, nw, nb, w1, b1, w2, b2, act):
            node = jnp.zeros(x.shape[:2], dtype=jnp.int32)
            for _ in range(DEPTH):
                logit = jnp.einsum('bsd,bsd->bs', x, nw[node]) + nb[node]
                node = 2 * node + 1 + (logit > 0).astype(jnp.int32)
            leaf = node - NN
            h = act(jnp.einsum('bsd,bsdl->bsl', x, w1[leaf]) + b1[leaf])
            return jnp.einsum('bsl,bsld->bsd', h, w2[leaf]) + b2[leaf]

        def _forward(x, q_nw, q_nb, q_w1, q_b1, q_w2, q_b2, k_nw, k_nb, k_w1, k_b1, k_w2, k_b2, v_nw, v_nb, v_w1, v_b1, v_w2, v_b2, f_nw, f_nb, f_w1, f_b1, f_w2, f_b2):
            mu = jnp.mean(x, -1, keepdims=True)
            sd = jnp.std(x, -1, ddof=1, keepdims=True)
            xn = (x - mu) / jnp.sqrt(sd + 1e-05)
            relu = jax.nn.relu
            q = _fff(xn, q_nw, q_nb, q_w1, q_b1, q_w2, q_b2, relu)
            k = _fff(xn, k_nw, k_nb, k_w1, k_b1, k_w2, k_b2, relu)
            v = _fff(xn, v_nw, v_nb, v_w1, v_b1, v_w2, v_b2, relu)
            att = jax.nn.softmax(jnp.einsum('bqd,bkd->bqk', q, k) / jnp.sqrt(jnp.float32(D)), axis=-1)
            y = xn + jnp.einsum('bqk,bkd->bqd', att, v)
            gelu = lambda t: jax.nn.gelu(t, approximate=False)
            return y + _fff(y, f_nw, f_nb, f_w1, f_b1, f_w2, f_b2, gelu)

        def _make_fff_params(key, scale_in, scale_leaf):
            ks = jax.random.split(key, 4)
            nw = jax.random.normal(ks[0], (NN, D), jnp.float32) * scale_in
            nb = jnp.zeros((NN,), jnp.float32)
            w1 = jax.random.normal(ks[1], (NL, D, LW), jnp.float32) * scale_in
            b1 = jax.random.normal(ks[2], (NL, LW), jnp.float32) * 0.01
            w2 = jax.random.normal(ks[3], (NL, LW, D), jnp.float32) * scale_leaf
            b2 = jnp.zeros((NL, D), jnp.float32)
            return (nw, nb, w1, b1, w2, b2)
        return _forward(x, q_nw, q_nb, q_w1, q_b1, q_w2, q_b2, k_nw, k_nb, k_w1, k_b1, k_w2, k_b2, v_nw, v_nb, v_w1, v_b1, v_w2, v_b2, f_nw, f_nb, f_w1, f_b1, f_w2, f_b2)

    def _L3_attn_ref(x, q_w, q_b, kv_w, kv_b, o_w, o_b):
        import jax, jax.numpy as jnp
        import numpy as np
        B, T, C = (2, 256, 128)
        NH = 16
        HD = C // NH

        def build_alibi_bias(n_head, max_len):
            slopes = jnp.arange(1, n_head + 1, dtype=jnp.float32) / n_head
            ar = jnp.arange(max_len, dtype=jnp.float32)
            return slopes[:, None, None] * (ar[None, None, :] - ar[None, :, None])
        Bx, Tx, Cx = x.shape
        q = (x @ q_w + q_b).reshape(Bx, Tx, NH, HD).transpose(0, 2, 1, 3)
        kv = (x @ kv_w + kv_b).reshape(Bx, Tx, 2, NH, HD).transpose(2, 0, 3, 1, 4)
        k, v = (kv[0], kv[1])
        att = jnp.einsum('bhqd,bhkd->bhqk', q, k) * (1.0 / np.sqrt(HD))
        att = att + build_alibi_bias(NH, Tx)[None]
        causal = jnp.tril(jnp.ones((Tx, Tx), dtype=bool))
        att = jnp.where(causal[None, None], att, -jnp.inf)
        att = jax.nn.softmax(att, axis=-1)
        y = jnp.einsum('bhqk,bhkd->bhqd', att, v)
        y = y.transpose(0, 2, 1, 3).reshape(Bx, Tx, Cx)
        return y @ o_w + o_b

    def _L3_ffn_ref(x, gate_w, gate_b, w1, b1, w2, b2, ln_g, ln_b):
        import jax, jax.numpy as jnp
        import numpy as np
        TOP_K = 2
        TEMP = 0.9
        EPS = 1e-05
        B, S, D, F, E = (2, 256, 128, 512, 8)

        def _moe_forward(x, gate_w, gate_b, w1, b1, w2, b2, ln_g, ln_b):
            logits = (x @ gate_w + gate_b) / TEMP
            topk_vals, topk_idx = jax.lax.top_k(logits, TOP_K)
            keep = jax.nn.one_hot(topk_idx, E, dtype=jnp.bool_).any(-2)
            masked = jnp.where(keep, logits, -jnp.inf)
            gate_probs = jax.nn.softmax(masked, axis=-1)
            h = jnp.einsum('bsd,edf->bsef', x, w1) + b1
            h = jax.nn.gelu(h, approximate=False)
            expert_out = jnp.einsum('bsef,efd->bsed', h, w2) + b2
            out = jnp.einsum('bse,bsed->bsd', gate_probs, expert_out)
            mu = out.mean(-1, keepdims=True)
            var = out.var(-1, keepdims=True)
            out = (out - mu) / jnp.sqrt(var + EPS) * ln_g + ln_b
            return out
        return _moe_forward(x, gate_w, gate_b, w1, b1, w2, b2, ln_g, ln_b)
    x = L0_attn_x
    x = x + _L0_attn_ref(_layernorm(x, axis=-1), L0_attn_band_importance, L0_attn_Wq, L0_attn_bq, L0_attn_Wk, L0_attn_bk, L0_attn_Wv, L0_attn_bv, L0_attn_Wo, L0_attn_bo, L0_attn_gamma, L0_attn_beta)
    x = x + _L0_ffn_ref(_layernorm(x, axis=-1), L0_ffn_Wg, L0_ffn_bg, L0_ffn_We, L0_ffn_be)
    x = x + _L1_attn_ref(_layernorm(x, axis=-1), L1_attn_Wq, L1_attn_bq, L1_attn_Wk, L1_attn_bk, L1_attn_Wv, L1_attn_bv, L1_attn_Wo, L1_attn_bo, L1_attn_idx_k)
    x = x + _L1_ffn_ref(_layernorm(x, axis=-1), L1_ffn_Wg, L1_ffn_Ws1, L1_ffn_Ws3, L1_ffn_Ws2, L1_ffn_We1, L1_ffn_We3, L1_ffn_We2)
    x = x + _L2_attn_ref(_layernorm(x, axis=-1), L2_attn_W_in, L2_attn_conv_w, L2_attn_conv_b, L2_attn_W_x, L2_attn_W_dt, L2_attn_b_dt, L2_attn_log_A, L2_attn_D_param, L2_attn_W_out, L2_attn_ln_w, L2_attn_ln_b)
    x = x + _L2_ffn_ref(_layernorm(x, axis=-1), L2_ffn_q_nw, L2_ffn_q_nb, L2_ffn_q_w1, L2_ffn_q_b1, L2_ffn_q_w2, L2_ffn_q_b2, L2_ffn_k_nw, L2_ffn_k_nb, L2_ffn_k_w1, L2_ffn_k_b1, L2_ffn_k_w2, L2_ffn_k_b2, L2_ffn_v_nw, L2_ffn_v_nb, L2_ffn_v_w1, L2_ffn_v_b1, L2_ffn_v_w2, L2_ffn_v_b2, L2_ffn_f_nw, L2_ffn_f_nb, L2_ffn_f_w1, L2_ffn_f_b1, L2_ffn_f_w2, L2_ffn_f_b2)
    x = x + _L3_attn_ref(_layernorm(x, axis=-1), L3_attn_q_w, L3_attn_q_b, L3_attn_kv_w, L3_attn_kv_b, L3_attn_o_w, L3_attn_o_b)
    x = x + _L3_ffn_ref(_layernorm(x, axis=-1), L3_ffn_gate_w, L3_ffn_gate_b, L3_ffn_w1, L3_ffn_b1, L3_ffn_w2, L3_ffn_b2, L3_ffn_ln_g, L3_ffn_ln_b)
    return x

_drawn_inputs = setup_inputs


def setup_inputs(seed=0):
    import zlib

    import numpy as np

    out = dict(_drawn_inputs(seed))
    spreads = {'L0_attn_bq': (0.0, 0.1),
     'L0_attn_bk': (0.0, 2.0),
     'L0_attn_bv': (0.0, 0.1),
     'L0_attn_bo': (0.0, 0.1),
     'L0_attn_gamma': (1.0, 0.2),
     'L0_attn_beta': (0.0, 0.1),
     'L0_ffn_bg': (0.0, 0.1),
     'L1_attn_bq': (0.0, 0.354),
     'L1_attn_bk': (0.0, 2.0),
     'L1_attn_bv': (0.0, 0.1),
     'L1_attn_bo': (0.0, 0.1),
     'L2_attn_conv_b': (0.0, 0.536),
     'L2_attn_b_dt': (0.0, 0.8),
     'L2_attn_D_param': (1.0, 0.6),
     'L2_attn_ln_w': (1.0, 0.6),
     'L2_attn_ln_b': (0.0, 0.8),
     'L2_ffn_q_nb': (0.0, 0.599),
     'L2_ffn_q_b2': (0.0, 1.773),
     'L2_ffn_k_nb': (0.0, 0.436),
     'L2_ffn_k_b2': (0.0, 2.0),
     'L2_ffn_v_nb': (0.0, 0.299),
     'L2_ffn_v_b2': (0.0, 0.502),
     'L2_ffn_f_nb': (0.0, 0.1),
     'L2_ffn_f_b2': (0.0, 0.659),
     'L3_attn_q_b': (0.0, 2.0),
     'L3_attn_kv_b': (0.0, 0.658),
     'L3_attn_o_b': (0.0, 0.587),
     'L3_ffn_gate_b': (0.0, 0.321),
     'L3_ffn_b1': (0.0, 0.309),
     'L3_ffn_b2': (0.0, 0.567),
     'L3_ffn_ln_g': (1.0, 0.6),
     'L3_ffn_ln_b': (0.0, 0.355)}
    factors = {'L1_ffn_Wg': 4.088,
     'L1_ffn_Ws1': 2.968,
     'L1_ffn_Ws3': 3.129,
     'L1_ffn_Ws2': 3.323,
     'L1_ffn_We1': 3.995,
     'L1_ffn_We3': 3.357,
     'L1_ffn_We2': 3.885,
     'L2_attn_W_in': 4.345,
     'L2_attn_conv_w': 4.453,
     'L2_attn_W_x': 8.0,
     'L2_attn_log_A': 8.0,
     'L2_attn_W_out': 3.995,
     'L2_ffn_q_b1': 64.0,
     'L2_ffn_k_b1': 64.0,
     'L2_ffn_v_b1': 53.322,
     'L2_ffn_f_b1': 62.069,
     'L3_attn_q_w': 8.0,
     'L3_attn_kv_w': 3.818,
     'L3_attn_o_w': 2.971,
     'L0_attn_band_importance': 2.676,
     'L2_attn_W_dt': 8.0,
     'L2_ffn_q_nw': 2.88,
     'L2_ffn_q_w1': 3.189,
     'L2_ffn_q_w2': 3.048,
     'L2_ffn_k_nw': 2.943,
     'L2_ffn_k_w1': 3.046,
     'L2_ffn_k_w2': 3.035}
    for name, (base, spread) in spreads.items():
        noise = np.random.default_rng([zlib.crc32(name.encode()), seed]).standard_normal(out[name].shape)
        drawn = base * np.exp(spread * noise) if base else spread * noise
        out[name] = jnp.asarray(drawn.astype(out[name].dtype))
    for name, factor in factors.items():
        out[name] = (out[name] * factor).astype(out[name].dtype)
    return out
```

```python
from contextlib import ExitStack

import numpy as np
import concourse.bass as bass
from concourse import mybir
from concourse.alu_op_type import AluOpType as ALU

F32, BF16 = mybir.dt.float32, mybir.dt.bfloat16
ACT = mybir.ActivationFunctionType
AX = mybir.AxisListType

PHASES = (0, 1, 2, 3, 4, 5, 6, 7)

P = 128
D = 128
NB, L = 8, 512
TQ = L // P
H, HD = 16, 8
HG = 4
EPS = 1e-5
BIG = 1e30
DMA = 16

Q_PART = (0, 0, 1, 1, 0, 2)
K_PART = (0, 1, 0, 1, 2, 0)
NSLOT = len(Q_PART)
R_EXT = 64
R_MAX = 68
R_ALL = 71


class Steps:

    def __init__(self, eng, sem, per_turn):
        self.eng, self.sem, self.per_turn, self.n, self.base = eng, sem, per_turn, 0, 0

    def turn(self, t):
        self.base, self.n = t * self.per_turn, 0

    def did(self, ins):
        ins.then_inc(self.sem, 1)
        self.n += 1

    def wait(self):
        self.eng.wait_ge(self.sem, self.base + self.n)

    def link(self, ins):
        self.did(ins)
        self.wait()

    def close(self):
        assert self.n == self.per_turn, (self.n, self.per_turn)


def batch_view(x_sb, t):
    return x_sb[:, bass.ds(t * (TQ * D), TQ * D)].rearrange("p (t d) -> p t d", d=D)


LN_STEPS = 12


NORM_STEPS = 9


def rsqrt_polish(dve, s, y, v, tmp):
    s.link(dve.tensor_tensor(tmp, y, y, ALU.mult))
    s.link(dve.tensor_tensor(tmp, tmp, v, ALU.mult))
    s.link(dve.tensor_scalar(tmp, tmp, -0.5, 1.5, ALU.mult, ALU.add))
    s.link(dve.tensor_tensor(y, y, tmp, ALU.mult))


def norm_dve(dve, s, src, xc, sq, st, out, var_ready, seed_ready, k, eps=EPS):
    s.link(dve.reduce_sum(st[:, 0, :], src, AX.X))
    s.link(dve.tensor_scalar(st[:, 0, :], st[:, 0, :], 1.0 / D, None, ALU.mult))
    s.link(dve.tensor_tensor(xc, src, st[:, 0, :].unsqueeze(2).to_broadcast([P, TQ, D]), ALU.subtract))
    s.link(dve.tensor_tensor(sq, xc, xc, ALU.mult))
    s.link(dve.reduce_sum(st[:, 1, :], sq, AX.X))
    dve.tensor_scalar(st[:, 1, :], st[:, 1, :], 1.0 / D, eps, ALU.mult, ALU.add).then_inc(var_ready, 1)
    dve.wait_ge(seed_ready, 2 * k)
    rsqrt_polish(dve, s, st[:, 2, :], st[:, 1, :], st[:, 3, :])
    return dve.tensor_tensor(out, xc, st[:, 2, :].unsqueeze(2).to_broadcast([P, TQ, D]), ALU.mult)


def norm_act(act, st, var_ready, seed_ready, k):
    act.wait_ge(var_ready, k)
    act.activation(st[:, 2, :], st[:, 1, :], ACT.Ln).then_inc(seed_ready, 1)
    act.wait_ge(seed_ready, 2 * k - 1)
    act.activation(st[:, 2, :], st[:, 2, :], ACT.Exp, scale=-0.5).then_inc(seed_ready, 1)


def over_tiles(row):
    return row.unsqueeze(1).to_broadcast([P, TQ, D])


def turns(eng, emit):
    emit(0, 0, True, False)
    with eng.Fori(0, NB // 2 - 1) as k:
        emit(2 * k + 1, 1, True, True)
        emit(2 * k + 2, 0, True, True)
    emit(NB - 1, 1, True, True)
    emit(NB, 0, False, True)


class Stage:

    def __init__(self, nc, ctx, name):
        self.nc, self.ctx, self.name, self.sems = nc, ctx, name, []

    def sb(self, name, shape, dt=F32):
        return self.ctx.enter_context(self.nc.sbuf_tensor(f"{self.name}_{name}", shape, dt))

    def ps(self, name, shape, dt=F32):
        return self.ctx.enter_context(self.nc.psum_tensor(f"{self.name}_{name}", shape, dt))

    def sem(self, name):
        self.sems.append(self.ctx.enter_context(self.nc.semaphore(f"{self.name}_{name}")))
        return self.sems[-1]

    def block(self):
        self.ctx.callback(self.clear)
        return self.ctx.enter_context(self.nc.Block())

    def clear(self):
        with self.nc.Block() as block:
            @block.gpsimd
            def _(pool):
                for sem in self.sems:
                    pool.sem_clear(sem)


def attention_stage(nc, name, x_sb, ident, w, qk_scratch, mx_scratch, causal):
    with ExitStack() as ctx:
        m = Stage(nc, ctx, name)
        wq, wk, wv, wo = (m.sb(n, [P, D]) for n in ("wq", "wk", "wv", "wo"))
        bqk = m.sb("bqk", [P, 2])
        bv, bo = m.sb("bv", [P, D]), m.sb("bo", [P, D])
        xc, sq, xn = (m.sb(n, [P, TQ, D]) for n in ("xc", "sq", "xn"))
        st = m.sb("st", [P, 4, TQ])
        xnT = m.sb("xnT", [P, L])
        zeros = m.sb("zeros", [P, TQ * HG * (HD + 1)])
        qk32, rest = m.sb("qk32", [P, 2, L]), m.sb("rest", [P, 2, L])
        parts = m.sb("parts", [P, 3, 2, L], BF16)
        QS = m.sb("QS", [R_ALL, 2, H, L], BF16)
        KS = m.sb("KS", [R_ALL, 2, H, L], BF16)
        vaug = m.sb("vaug", [P, 2, TQ, H, HD + 1])
        mxs, mx = m.sb("mxs", [P, HG, TQ]), m.sb("mx", [P, P])
        mneg, mrest = m.sb("mneg", [64, P]), m.sb("mrest", [64, P])
        mparts = m.sb("mparts", [64, 3, P], BF16)
        probs = m.sb("probs", [P, 2, TQ, L])
        vstage = m.sb("vstage", [P, TQ, HG, 32])
        oT = m.sb("oT", [P, L])
        rden = m.sb("rden", [P, TQ, HG])
        cx = m.sb("cx", [P, TQ, D])
        cxT = m.sb("cxT", [P, L])
        if causal:
            identb = m.sb("identb", [P, P], BF16)
            above = m.sb("above", [P, 2, P], BF16)
        else:
            yres = m.sb("yres", [P, 2, TQ, D])
            gamma, beta = m.sb("gamma", [P, D]), m.sb("beta", [P, D])
            band = m.sb("band", [1, 256])
            btop, bsel, beq, bcum = m.sb("btop", [1, 16]), m.sb("bsel", [1, 256]), m.sb("beq", [1, 256]), m.sb("bcum", [1, 256])
            bzero = m.sb("bzero", [1, 256])
            brow = m.sb("brow", [1, H, L], BF16)
        psT, psU = m.ps("psT", [P, L]), m.ps("psU", [P, L])
        psM = [m.ps(f"psM{i}", [P, L]) for i in range(2)]
        psS = [m.ps(f"psS{i}", [P, L]) for i in range(3)]
        psO = m.ps("psO", [P, L])

        (
            loaded, ones_set, norm_steps, m_steps, out_steps, xn_ready, yres_ready, var_ready, seed_ready,
            var2_ready, seed2_ready, xnT_ps, xnT_ready, q_ps, k_ps, qk_evac, v_ps, v_ready, hi_ready, rest_ready,
            mid_ready, parts_ready, parts_stored, qk_loaded, sc_ready, sc_used, mx_ready, mT_ps, mparts_ready,
            mrow_stored, mrow_loaded, s_ready, p_ready, pv_done, oT_ps, o_used, cx_ready, cxT_ps, cxT_ready, y_ps,
            x_done, mask_row, band_steps, rden_ready, vstage_ready
        ) = (m.sem(n) for n in (
            "loaded", "ones_set", "norm_steps", "m_steps", "out_steps", "xn_ready", "yres_ready", "var_ready",
            "seed_ready", "var2_ready", "seed2_ready", "xnT_ps", "xnT_ready", "q_ps", "k_ps", "qk_evac", "v_ps",
            "v_ready", "hi_ready", "rest_ready", "mid_ready", "parts_ready", "parts_stored", "qk_loaded",
            "sc_ready", "sc_used", "mx_ready", "mT_ps", "mparts_ready", "mrow_stored", "mrow_loaded", "s_ready",
            "p_ready", "pv_done", "oT_ps", "o_used", "cx_ready", "cxT_ps", "cxT_ready", "y_ps", "x_done",
            "mask_row", "band_steps", "rden_ready", "vstage_ready"))

        loads = [(wq[:], w["wq"]), (wk[:], w["wk"]), (wv[:], w["wv"]), (wo[:], w["wo"]), (bqk[:], w["bqk"]),
                 (bv[:], w["bv"]), (bo[:], w["bo"])]
        for par in range(2):
            loads += [(QS[NSLOT * HD:R_MAX, par], w["qext"]), (KS[NSLOT * HD:R_ALL, par], w["kext"])]
        if causal:
            loads += [(identb[:], w["identb"]), (above[:], w["above"])]
        else:
            loads += [(gamma[:], w["gamma"]), (beta[:], w["beta"]), (band[:], w["band"])]
        n_loaded = DMA * len(loads)
        norms = 1 if causal else 2
        width = [(q + 1) * P if causal else L for q in range(TQ)]
        NG = H // HG
        first_q = [k * P if causal else 0 for k in range(TQ)]

        block = m.block()

        @block.sync
        def _(sp):
            for dst, src in loads:
                sp.dma_start(dst, src).then_inc(loaded, DMA)
            if not causal:
                sp.wait_ge(loaded, n_loaded)
                sp.wait_ge(band_steps, 12)
                for par in range(2):
                    sp.dma_start(KS[R_EXT:R_EXT + 1, par], brow[:]).then_inc(mask_row, DMA)

            def emit(t, par, ahead, behind):
                if ahead:
                    sp.wait_ge(parts_ready, t + 1)
                    sp.dma_start(qk_scratch.rearrange("a b p l -> p a b l"), parts[:]).then_inc(parts_stored, DMA)
                    sp.wait_ge(parts_stored, t * DMA + DMA)
                    for dst, side, part in ((QS, 0, Q_PART), (KS, 1, K_PART)):
                        for slot in range(NSLOT):
                            sp.dma_start(dst[slot * HD:(slot + 1) * HD, par],
                                         qk_scratch[part[slot], side].rearrange("(h e) l -> e h l", e=HD)
                                         ).then_inc(qk_loaded, DMA)
                    sp.wait_ge(mparts_ready, t + 1)
                    sp.dma_start(mx_scratch.rearrange("a p l -> p a l"), mparts[:]).then_inc(mrow_stored, DMA)
                    sp.wait_ge(mrow_stored, t * DMA + DMA)
                    sp.dma_start(QS[R_MAX:R_ALL, par].rearrange("e h l -> e (h l)"),
                                 mx_scratch.rearrange("a p l -> a (p l)")).then_inc(mrow_loaded, DMA)
            turns(sp, emit)

        @block.tensor
        def _(pe):
            pe.wait_ge(loaded, n_loaded)
            pe.wait_ge(ones_set, 4)
            pe.sem_inc(pv_done, 2)

            def emit(t, par, ahead, behind):
                if ahead:
                    pe.wait_ge(xn_ready, t + 1)
                    for q in range(TQ):
                        ins = pe.transpose(psT[:, q * P:(q + 1) * P], xn[:, q], ident[:])
                    ins.then_inc(xnT_ps, 1)
                    pe.wait_ge(xnT_ready, t + 1)
                    pe.matmul(psU[:], wq[:], xnT[:], start=True, stop=True).then_inc(q_ps, 1)
                    pe.matmul(psT[:], wk[:], xnT[:], start=True, stop=True).then_inc(k_ps, 1)
                    pe.wait_ge(qk_evac, 2 * t + 1)
                    for q in range(TQ):
                        ins = pe.matmul(psU[:, q * P:(q + 1) * P], xnT[:, q * P:(q + 1) * P], wv[:], start=True, stop=True)
                    ins.then_inc(v_ps, 1)
                if not causal:
                    pe.wait_ge(mask_row, 2 * DMA)
                u = t - 1

                def scores(g, j):
                    if j == 0:
                        pe.wait_ge(mrow_loaded, t * DMA)
                    for k in range(TQ):
                        i = j * TQ + k
                        bank = psS[i % 3]
                        pe.wait_ge(p_ready, 1 + (u * H + g * HG) * TQ + max(i - 2, 0))
                        if causal:
                            pe.matmul(bank[:, k * P:(k + 1) * P], identb[:], above[:, 0], start=True, stop=False,
                                      skip_group_check=True)
                        pe.matmul(bank[:, first_q[k]:L], KS[:, 1 - par, bass.ds(g * HG + j, 1), k * P:(k + 1) * P].rearrange("e h l -> e (h l)"),
                                  QS[:, 1 - par, bass.ds(g * HG + j, 1), first_q[k]:L].rearrange("e h l -> e (h l)"),
                                  start=not causal, stop=True, skip_group_check=True).then_inc(s_ready, 1)

                def for_maxima(g, j):
                    if j == 0:
                        pe.wait_ge(qk_loaded, (t + 1) * (2 * NSLOT * DMA))
                    for q in range(TQ):
                        i = j * TQ + q
                        bank = psM[i % 2]
                        pe.wait_ge(sc_used, 1 + (t * H + g * HG) * TQ + max(i - 1, 0))
                        if causal:
                            pe.matmul(bank[:, q * P:(q + 1) * P], identb[:], above[:, 1], start=True, stop=False,
                                      skip_group_check=True)
                        pe.matmul(bank[:, 0:width[q]], QS[0:R_MAX, par, bass.ds(g * HG + j, 1), q * P:(q + 1) * P].rearrange("e h l -> e (h l)"),
                                  KS[0:R_MAX, par, bass.ds(g * HG + j, 1), 0:width[q]].rearrange("e h l -> e (h l)"),
                                  start=not causal, stop=True, skip_group_check=True).then_inc(sc_ready, 1)

                def contexts(g, j):
                    pe.wait_ge(p_ready, 1 + (u * H + g * HG + j + 1) * TQ)
                    if j == 0:
                        pe.wait_ge(o_used, 1 + u * NG + g)
                        pe.wait_ge(vstage_ready, u * NG + g + 1)
                    for k in range(TQ):
                        ins = pe.matmul(psO[32 * j:32 * (j + 1), first_q[k]:L], vstage[:, k, j], probs[:, j % 2, k, first_q[k]:L],
                                        start=(k == 0), stop=(k == TQ - 1))
                    ins.then_inc(pv_done, 1)

                with pe.Fori(0, NG) as g:
                    for j in range(HG):
                        if behind:
                            scores(g, j)
                            if j:
                                contexts(g, j - 1)
                        if ahead:
                            for_maxima(g, j)
                    if behind:
                        contexts(g, HG - 1)
                        pe.wait_ge(o_used, 1 + u * NG + g + 1)
                        for q in range(TQ):
                            ins = pe.transpose(psT[:, q * P:(q + 1) * P], oT[:, q * P:(q + 1) * P], ident[:])
                        ins.then_inc(oT_ps, 1)
                if behind:
                    pe.wait_ge(cx_ready, t * NG)
                if ahead:
                    pe.wait_ge(mx_ready, 1 + t * NG + NG)
                    pe.transpose(psT[:, 0:P], mx[:], ident[:]).then_inc(mT_ps, 1)
                if behind:
                    if ahead:
                        pe.wait_ge(mparts_ready, t + 1)
                    for q in range(TQ):
                        ins = pe.transpose(psT[:, q * P:(q + 1) * P], cx[:, q], ident[:])
                    ins.then_inc(cxT_ps, 1)
                    pe.wait_ge(cxT_ready, t)
                    for q in range(TQ):
                        ins = pe.matmul(psU[:, q * P:(q + 1) * P], cxT[:, q * P:(q + 1) * P], wo[:], start=True, stop=True)
                    ins.then_inc(y_ps, 1)

            turns(pe, emit)

        @block.vector
        def _(dve):
            dve.memset(vaug[:], 1.0).then_inc(ones_set, 1)
            dve.memset(mx[:], 0.0).then_inc(ones_set, 1)
            dve.memset(vstage[:], 0.0).then_inc(ones_set, 1)
            dve.memset(zeros[:], 0.0).then_inc(ones_set, 1)
            dve.wait_ge(ones_set, 4)
            for started in (sc_used, mx_ready, o_used):
                dve.sem_inc(started, 1)
            dve.wait_ge(loaded, n_loaded)
            if not causal:
                b = Steps(dve, band_steps, 12)
                b.link(dve.memset(bzero[:], 0.0))
                b.link(dve.memset(brow[:], 0.0))
                b.link(dve.max(btop[:, 0:8], band[:]))
                b.link(dve.tensor_scalar(bsel[:], band[:], btop[:, 2:3], None, ALU.is_gt))
                b.link(dve.tensor_scalar(beq[:], band[:], btop[:, 2:3], None, ALU.is_equal))
                b.link(dve.reduce_sum(btop[:, 8:9], bsel[:], AX.X))
                b.link(dve.tensor_scalar(btop[:, 8:9], btop[:, 8:9], -1.0, 3.0, ALU.mult, ALU.add))
                b.link(dve.tensor_tensor_scan(bcum[:], beq[:], bzero[:], 0.0, ALU.add, ALU.add))
                b.link(dve.tensor_scalar(bcum[:], bcum[:], btop[:, 8:9], None, ALU.is_le))
                b.link(dve.tensor_tensor(beq[:], beq[:], bcum[:], ALU.mult))
                b.link(dve.tensor_tensor(bsel[:], bsel[:], beq[:], ALU.add))
                b.link(dve.tensor_scalar(brow[:, :, 0:256], bsel[:].unsqueeze(1).to_broadcast([1, H, 256]), -BIG, None, ALU.mult))
                b.close()
            a = Steps(dve, norm_steps, NORM_STEPS)
            mm = Steps(dve, m_steps, 4)
            o = Steps(dve, out_steps, 1 if causal else 4 + NORM_STEPS)

            def emit(t, par, ahead, behind):
                if ahead:
                    a.turn(t)
                    norm_dve(dve, a, batch_view(x_sb, t), xc[:], sq[:], st[:], xn[:], var_ready, seed_ready, t + 1).then_inc(xn_ready, 1)
                    a.close()
                    dve.wait_ge(xn_ready, t + 1)
                    if not causal:
                        dve.tensor_tensor(yres[:, par], xn[:],
                                          over_tiles(bo[:]), ALU.add).then_inc(yres_ready, 1)
                    dve.wait_ge(q_ps, t + 1)
                    dve.tensor_scalar(qk32[:, 0], psU[:], bqk[:, 0:1], float(HD ** -0.5), ALU.add, ALU.mult).then_inc(qk_evac, 1)
                    dve.wait_ge(k_ps, t + 1)
                    dve.tensor_scalar(qk32[:, 1], psT[:], bqk[:, 1:2], None, ALU.add).then_inc(qk_evac, 1)
                    dve.wait_ge(v_ps, t + 1)
                    dve.tensor_tensor(vaug[:, par, :, :, 0:HD],
                                      psU[:].rearrange("p (t h e) -> p t h e", t=TQ, h=H),
                                      bv[:].rearrange("p (h e) -> p h e", h=H).unsqueeze(1).to_broadcast([P, TQ, H, HD]),
                                      ALU.add).then_inc(v_ready, 1)

                def group(g):
                    if ahead:
                        dve.wait_ge(mx_ready, 1 + t * NG + g)
                    for j in range(HG):
                        if ahead:
                            for q in range(TQ):
                                i = j * TQ + q
                                dve.wait_ge(sc_ready, (t * H + g * HG) * TQ + i + 1)
                                dve.reduce_max(mxs[:, j, q:q + 1], psM[i % 2][:, 0:width[q]], AX.X).then_inc(sc_used, 1)
                    if ahead:
                        dve.wait_ge(sc_used, 1 + (t * H + g * HG + HG) * TQ)
                        dve.tensor_scalar(mx[:, bass.ds(g * (HG * TQ), HG * TQ)], mxs[:].rearrange("p a b -> p (a b)"),
                                          1.0, None, ALU.mult).then_inc(mx_ready, 1)
                    if behind:
                        dve.wait_ge(pv_done, 2 + (t - 1) * H + g * HG + HG)
                        dve.tensor_copy(oT[:], psO[:]).then_inc(o_used, 1)
                        dve.wait_ge(oT_ps, (t - 1) * NG + g + 1)
                        turned = psT[:].rearrange("p (t j e) -> p t j e", t=TQ, j=HG)
                        dve.reciprocal(rden[:], turned[:, :, :, HD]).then_inc(rden_ready, 1)
                        dve.wait_ge(rden_ready, (t - 1) * NG + g + 1)
                        dve.tensor_tensor(cx[:, :, bass.ds(g * (HG * HD), HG * HD)].rearrange("p t (j e) -> p t j e", j=HG),
                                          turned[:, :, :, 0:HD], rden[:].unsqueeze(3).to_broadcast([P, TQ, HG, HD]),
                                          ALU.mult).then_inc(cx_ready, 1)
                        dve.wait_ge(cx_ready, (t - 1) * NG + g + 1)
                with dve.Fori(0, NG) as g:
                    group(g)
                if ahead:
                    mm.turn(t)
                    dve.wait_ge(mT_ps, t + 1)
                    mm.link(dve.tensor_scalar(mneg[:], psT[0:64, 0:P], -1.0, None, ALU.mult))
                    mm.link(dve.tensor_copy(mparts[:, 0], mneg[:]))
                    mm.link(dve.tensor_tensor(mrest[:], mneg[:], mparts[:, 0], ALU.subtract))
                    mm.link(dve.tensor_copy(mparts[:, 1], mrest[:]))
                    dve.tensor_tensor(mparts[:, 2], mrest[:], mparts[:, 1], ALU.subtract).then_inc(mparts_ready, 1)
                    dve.wait_ge(mparts_ready, t + 1)
                    mm.close()
                if behind:
                    o.turn(t - 1)
                    dve.wait_ge(y_ps, t)
                    xb = batch_view(x_sb, t - 1)
                    y3 = psU[:].rearrange("p (t d) -> p t d", t=TQ)
                    if causal:
                        o.link(dve.tensor_tensor(xc[:], y3, over_tiles(bo[:]), ALU.add))
                        dve.tensor_tensor(xb, xb, xc[:], ALU.add).then_inc(x_done, 1)
                    else:
                        o.link(dve.tensor_tensor(cx[:], y3, yres[:, 1 - par], ALU.add))
                        o.link(norm_dve(dve, o, cx[:], xc[:], sq[:], st[:], cx[:], var2_ready, seed2_ready, t))
                        o.link(dve.tensor_tensor(cx[:], cx[:], over_tiles(gamma[:]), ALU.mult))
                        o.link(dve.tensor_tensor(cx[:], cx[:], over_tiles(beta[:]), ALU.add))
                        dve.tensor_tensor(xb, xb, cx[:], ALU.add).then_inc(x_done, 1)
                    dve.wait_ge(x_done, t)
                    o.close()
            turns(dve, emit)

        @block.gpsimd
        def _(pool):
            pool.wait_ge(ones_set, 4)

            def emit(t, par, ahead, behind):
                if ahead:
                    pool.wait_ge(hi_ready, t + 1)
                    pool.tensor_tensor(rest[:], qk32[:], parts[:, 0], ALU.subtract).then_inc(rest_ready, 1)
                    pool.wait_ge(mid_ready, t + 1)
                    pool.tensor_tensor(parts[:, 2], rest[:], parts[:, 1], ALU.subtract).then_inc(parts_ready, 1)
                if behind:
                    with pool.Fori(0, NG) as g:
                        pool.wait_ge(v_ready, t)
                        pool.wait_ge(pv_done, 2 + (t - 1) * H + g * HG)
                        pool.tensor_tensor(vstage[:, :, :, 0:HD + 1], vaug[:, 1 - par, :, bass.ds(g * HG, HG), :],
                                           zeros[:].rearrange("p (a b c) -> p a b c", a=TQ, b=HG),
                                           ALU.add).then_inc(vstage_ready, 1)
            turns(pool, emit)

        @block.scalar
        def _(act):
            act.sem_inc(p_ready, 1)

            act.preload_act_table_set("natural_log_exp_and_others")

            def emit(t, par, ahead, behind):
                if ahead:
                    norm_act(act, st, var_ready, seed_ready, t + 1)
                    act.wait_ge(xnT_ps, t + 1)
                    act.activation(xnT[:], psT[:], ACT.Copy).then_inc(xnT_ready, 1)
                    act.wait_ge(qk_evac, 2 * t + 2)
                    if behind:
                        act.wait_ge(parts_stored, t * DMA)
                    act.activation(parts[:, 0], qk32[:], ACT.Copy).then_inc(hi_ready, 1)
                    act.wait_ge(rest_ready, t + 1)
                    act.activation(parts[:, 1], rest[:], ACT.Copy).then_inc(mid_ready, 1)
                if behind:
                    u = t - 1

                    with act.Fori(0, NG) as g:
                        for j in range(HG):
                            for k in range(TQ):
                                act.wait_ge(s_ready, (u * H + g * HG + j) * TQ + k + 1)
                                if k == 0:
                                    act.wait_ge(pv_done, u * H + g * HG + j + 1)
                                act.activation(probs[:, j % 2, k, first_q[k]:L], psS[(j * TQ + k) % 3][:, first_q[k]:L],
                                               ACT.Exp).then_inc(p_ready, 1)
                    act.wait_ge(cxT_ps, t)
                    act.activation(cxT[:], psT[:], ACT.Copy).then_inc(cxT_ready, 1)
                    if not causal:
                        norm_act(act, st, var2_ready, seed2_ready, t)
            turns(act, emit)


NEG = 8


def experts_stage(nc, name, x_sb, ident, w, kind):
    shared = kind == "swiglu"
    NE = NEG + shared
    F = {"linear": P, "swiglu": 256, "gelu": 512}[kind]
    NF = F // P
    post_norm = kind == "gelu"
    has_bias = kind != "swiglu"
    out_scale = 1.0 / 3.0 if shared else 1.0
    gate_scale = 1.0 / 0.9 if kind == "gelu" else 1.0
    with ExitStack() as ctx:
        m = Stage(nc, ctx, name)
        wg, bg = m.sb("wg", [P, NEG]), m.sb("bg", [P, NEG])
        w_down = m.sb("w_down", [P, NE, NF, D])
        select = m.sb("select", [3 * NE, NE, P], BF16)
        before = m.sb("before", [P, NEG, NEG])
        identb = m.sb("identb", [P, P], BF16)
        xc, sq, xn = (m.sb(n, [P, TQ, D]) for n in ("xc", "sq", "xn"))
        st = m.sb("st", [P, 4, TQ])
        xnT = m.sb("xnT", [P, 2, L])
        logit, rank, gexp, gate = (m.sb(n, [P, TQ, NEG]) for n in ("logit", "rank", "gexp", "gate"))
        above, equal = m.sb("above", [P, TQ * NEG, NEG]), m.sb("equal", [P, TQ * NEG, NEG])
        gsum = m.sb("gsum", [P, TQ])
        gparts = m.sb("gparts", [P, TQ, 3, NE], BF16)
        gT = m.sb("gT", [3 * NE, 2, L], BF16)
        hw = m.sb("hw", [P, 2, NF, L])
        outT = m.sb("outT", [P, L])
        y = m.sb("y", [P, TQ, D])
        loads = [(wg[:], w["wg"]), (bg[:], w["bg"]), (select[:], w["select"]), (before[:], w["before"]),
                 (identb[:], w["identb"]), (w_down[:], w["w_down"])]
        if kind != "linear":
            h = m.sb("h", [P, NF, L])
            w_up = m.sb("w_up", [P, NE, (2 if shared else 1) * NF, P])
            loads.append((w_up[:], w["w_up"]))
        if kind == "swiglu":
            hh = m.sb("hh", [P, NF, L])
        if kind == "gelu":
            b_up, gamma, beta = m.sb("b_up", [P, NE, NF]), m.sb("gamma", [P, D]), m.sb("beta", [P, D])
            loads += [(b_up[:], w["b_up"]), (gamma[:], w["gamma"]), (beta[:], w["beta"])]
        if has_bias:
            b_down = m.sb("b_down", [3 * NE, 3, D], BF16)
            b32, brest = m.sb("b32", [3 * NE, D]), m.sb("brest", [3 * NE, D])
            loads.append((b32[:], w["b_down"]))
        n_loaded = DMA * len(loads)
        psT, psO = m.ps("psT", [P, L]), m.ps("psO", [P, L])
        psW = [m.ps(f"psW{i}", [P, L]) for i in range(2)]
        psF = [m.ps(f"psF{i}", [P, L]) for i in range(4)]
        gT_bank = psT[:].bitcast(BF16)[0:3 * NE, 0:L]

        (
            loaded, bias_steps, norm_steps, gate_steps, out_steps, var_ready, seed_ready, xn_ready, xnT_ps, xnT_ready,
            logit_ps, top_ready, exp_ready, gparts_ready, gT_ps, gT_ready, w_ps, up_ps, act_done, first_mult, hw_ready,
            down_done, out_ps, outT_ready, out_tok, var2_ready, seed2_ready, x_done, ones_set
        ) = (m.sem(n) for n in (
            "loaded", "bias_steps", "norm_steps", "gate_steps", "out_steps", "var_ready", "seed_ready", "xn_ready", "xnT_ps",
            "xnT_ready", "logit_ps", "top_ready", "exp_ready", "gparts_ready", "gT_ps", "gT_ready", "w_ps", "up_ps",
            "act_done", "first_mult", "hw_ready", "down_done", "out_ps", "outT_ready", "out_tok", "var2_ready",
            "seed2_ready", "x_done", "ones_set"))
        BIAS_STEPS = 5 if has_bias else 0

        block = m.block()

        @block.sync
        def _(sp):
            for dst, src in loads:
                sp.dma_start(dst, src).then_inc(loaded, DMA)

        @block.tensor
        def _(pe):
            pe.wait_ge(loaded, n_loaded)
            pe.sem_inc(down_done, 1)
            if has_bias:
                pe.wait_ge(bias_steps, BIAS_STEPS)

            def emit(t, par, ahead, behind):
                u = t - 1

                def up(e):
                    if e == 0:
                        pe.wait_ge(gT_ready, u + 1)
                    pe.wait_ge(hw_ready, 1 + u * (NE * NF) + max(e - 1, 0) * NF)
                    pe.matmul(psW[e % 2][:], select[:, e], gT[:, 1 - par], start=True, stop=True).then_inc(w_ps, 1)
                    for f in range(NF if kind != "linear" else 0):
                        if kind == "gelu":
                            pe.wait_ge(act_done, 1 + u * (NE * NF) + ((e - 1) * NF + f + 1 if e else 0))
                            pe.matmul(psF[f][:], w_up[:, e, f], xnT[:, 1 - par], start=True, stop=True).then_inc(up_ps, 1)
                        else:
                            pe.wait_ge(first_mult, 1 + u * (NE * NF) + ((e - 1) * NF + f + 1 if e else 0))
                            pe.matmul(psF[2 * f][:], w_up[:, e, f], xnT[:, 1 - par], start=True, stop=True)
                            pe.matmul(psF[2 * f + 1][:], w_up[:, e, NF + f], xnT[:, 1 - par], start=True, stop=True).then_inc(up_ps, 1)

                def down(e):
                    if e == 0:
                        pe.wait_ge(outT_ready, 1 + u)
                        for i in range(3 if has_bias else 0):
                            pe.matmul(psO[:], b_down[:, i], gT[:, 1 - par], start=(i == 0), stop=False)
                    for f in range(NF):
                        pe.wait_ge(hw_ready, 1 + u * (NE * NF) + e * NF + f + 1)
                        ins = pe.matmul(psO[:], w_down[:, e, f], hw[:, e % 2, f], start=(e == f == 0 and not has_bias),
                                        stop=(e == NE - 1 and f == NF - 1))
                    ins.then_inc(down_done, 1)

                for e in range(NE):
                    if behind:
                        up(e)
                        if e:
                            down(e - 1)
                    if ahead and e == 2:
                        pe.wait_ge(xn_ready, t + 1)
                        if behind:
                            pe.wait_ge(x_done, t)
                        for q in range(TQ):
                            ins = pe.transpose(psT[:, q * P:(q + 1) * P], xn[:, q], ident[:])
                        ins.then_inc(xnT_ps, 1)
                    if ahead and e == 4:
                        pe.wait_ge(xnT_ready, t + 1)
                        for q in range(TQ):
                            ins = pe.matmul(psT[:, q * NEG:(q + 1) * NEG], xnT[:, par, q * P:(q + 1) * P], wg[:], start=True, stop=True)
                        ins.then_inc(logit_ps, 1)
                    if ahead and e == 7:
                        pe.wait_ge(gparts_ready, t + 1)
                        for q in range(TQ):
                            ins = pe.transpose(gT_bank[:, q * P:(q + 1) * P], gparts[:, q].rearrange("p a b -> p (a b)"), identb[:])
                        ins.then_inc(gT_ps, 1)
                if behind:
                    down(NE - 1)
                    if ahead:
                        pe.wait_ge(gT_ready, t + 1)
                    pe.wait_ge(outT_ready, 2 + u)
                    for q in range(TQ):
                        ins = pe.transpose(psT[:, q * P:(q + 1) * P], outT[:, q * P:(q + 1) * P], ident[:])
                    ins.then_inc(out_tok, 1)
            turns(pe, emit)

        @block.scalar
        def _(act):
            act.wait_ge(loaded, n_loaded)
            act.sem_inc(outT_ready, 1)
            act.sem_inc(act_done, 1)

            def emit(t, par, ahead, behind):
                u = t - 1
                for e in range(NE):
                    if behind and kind != "linear":
                        for f in range(NF):
                            n = u * (NE * NF) + e * NF + f
                            act.wait_ge(up_ps, n + 1)
                            if kind == "gelu":
                                act.wait_ge(hw_ready, 1 + u * (NE * NF) + ((e - 1) * NF + f + 1 if e else 0))
                                act.activation(h[:, f], psF[f][:], ACT.Gelu, bias=b_up[:, e, f:f + 1]).then_inc(act_done, 1)
                            else:
                                act.wait_ge(first_mult, 1 + u * (NE * NF) + ((e - 1) * NF + f + 1 if e else 0))
                                act.activation(h[:, f], psF[2 * f][:], ACT.Silu).then_inc(act_done, 1)
                    if ahead and e == 0:
                        norm_act(act, st, var_ready, seed_ready, t + 1)
                    if ahead and e == 3:
                        act.wait_ge(xnT_ps, t + 1)
                        act.activation(xnT[:, par], psT[:], ACT.Copy).then_inc(xnT_ready, 1)
                    if ahead and e == 5:
                        act.wait_ge(top_ready, t + 1)
                        act.activation(gexp[:], logit[:], ACT.Exp, scale=-1.0 if shared else 1.0).then_inc(exp_ready, 1)
                if behind:
                    act.wait_ge(down_done, 1 + t * NE)
                    act.activation(outT[:], psO[:], ACT.Copy, scale=out_scale).then_inc(outT_ready, 1)
                    if post_norm:
                        norm_act(act, st, var2_ready, seed2_ready, t)
            turns(act, emit)

        @block.vector
        def _(dve):
            dve.wait_ge(loaded, n_loaded)
            for started in (hw_ready, first_mult, x_done):
                dve.sem_inc(started, 1)
            if shared:
                dve.memset(gparts[:], 0.0).then_inc(ones_set, 1)
                dve.wait_ge(ones_set, 1)
                dve.memset(gparts[:, :, 0, NEG], 1.0).then_inc(ones_set, 1)
            if has_bias:
                b = Steps(dve, bias_steps, BIAS_STEPS)
                b.link(dve.tensor_copy(b_down[:, 0], b32[:]))
                b.link(dve.tensor_tensor(brest[:], b32[:], b_down[:, 0], ALU.subtract))
                b.link(dve.tensor_copy(b_down[:, 1], brest[:]))
                b.link(dve.tensor_tensor(brest[:], brest[:], b_down[:, 1], ALU.subtract))
                b.link(dve.tensor_copy(b_down[:, 2], brest[:]))
                b.close()
            a = Steps(dve, norm_steps, NORM_STEPS)
            g = Steps(dve, gate_steps, 21 if shared else 22)
            o = Steps(dve, out_steps, 3 + NORM_STEPS)

            def per_token(v):
                return v.unsqueeze(2).to_broadcast([P, TQ, NEG])

            def prepare(t, par, slot):
                if slot == 0:
                    a.turn(t)
                    norm_dve(dve, a, batch_view(x_sb, t), xc[:], sq[:], st[:], xn[:], var_ready, seed_ready, t + 1).then_inc(xn_ready, 1)
                    dve.wait_ge(xn_ready, t + 1)
                    a.close()
                if slot == 4:
                    g.turn(t)
                    dve.wait_ge(logit_ps, t + 1)
                    g.link(dve.tensor_tensor(logit[:], psT[:, 0:TQ * NEG].rearrange("p (t e) -> p t e", t=TQ),
                                             bg[:].unsqueeze(1).to_broadcast([P, TQ, NEG]), ALU.add))
                    flat = logit[:].rearrange("p t e -> p (t e)")
                    mine = flat.unsqueeze(2).to_broadcast([P, TQ * NEG, NEG])
                    for q in range(TQ):
                        part = slice(q * NEG, (q + 1) * NEG)
                        other = logit[:, q].unsqueeze(1).to_broadcast([P, NEG, NEG])
                        g.did(dve.tensor_tensor(above[:, part], other, mine[:, part], ALU.is_gt))
                        g.did(dve.tensor_tensor(equal[:, part], other, mine[:, part], ALU.is_equal))
                    g.wait()
                    for q in range(TQ):
                        part = slice(q * NEG, (q + 1) * NEG)
                        ins = dve.tensor_tensor(equal[:, part], equal[:, part], before[:], ALU.mult)
                    g.link(ins)
                    g.link(dve.tensor_tensor(above[:], above[:], equal[:], ALU.add))
                    g.link(dve.reduce_sum(rank[:].rearrange("p t e -> p (t e)"), above[:], AX.X))
                    if shared:
                        dve.tensor_scalar(rank[:], rank[:], 2.0, None, ALU.is_lt).then_inc(top_ready, 1)
                    else:
                        g.link(dve.tensor_scalar(rank[:], rank[:], 2.0, None, ALU.is_lt))
                        g.link(dve.reduce_max(gsum[:], logit[:], AX.X))
                        g.link(dve.tensor_tensor(logit[:], logit[:], per_token(gsum[:]), ALU.subtract))
                        dve.tensor_scalar(logit[:], logit[:], gate_scale, None, ALU.mult).then_inc(top_ready, 1)
                if slot == 6:
                    dve.wait_ge(exp_ready, t + 1)
                    if shared:
                        g.link(dve.tensor_scalar(gexp[:], gexp[:], 1.0, None, ALU.add))
                        g.link(dve.reciprocal(gexp[:], gexp[:]))
                    g.link(dve.tensor_tensor(gate[:], gexp[:], rank[:], ALU.mult))
                    g.link(dve.reduce_sum(gsum[:], gate[:], AX.X))
                    g.link(dve.reciprocal(gsum[:], gsum[:]))
                    g.link(dve.tensor_tensor(gate[:], gate[:], per_token(gsum[:]), ALU.mult))
                    g.link(dve.tensor_copy(gparts[:, :, 0, 0:NEG], gate[:]))
                    g.link(dve.tensor_tensor(gate[:], gate[:], gparts[:, :, 0, 0:NEG], ALU.subtract))
                    g.link(dve.tensor_copy(gparts[:, :, 1, 0:NEG], gate[:]))
                    dve.tensor_tensor(gparts[:, :, 2, 0:NEG], gate[:], gparts[:, :, 1, 0:NEG], ALU.subtract).then_inc(gparts_ready, 1)
                    dve.wait_ge(gparts_ready, t + 1)
                if slot == 7:
                    dve.wait_ge(gT_ps, t + 1)
                    dve.tensor_copy(gT[:, par], gT_bank).then_inc(gT_ready, 1)

            def emit(t, par, ahead, behind):
                u = t - 1
                for e in range(NE):
                    if behind:
                        dve.wait_ge(w_ps, u * NE + e + 1)
                        for f in range(NF):
                            n = u * (NE * NF) + e * NF + f
                            if f == 0:
                                dve.wait_ge(down_done, 1 + u * NE + max(e - 1, 0))
                            if kind == "linear":
                                src = xnT[:, 1 - par]
                            elif kind == "gelu":
                                dve.wait_ge(act_done, 1 + n + 1)
                                src = h[:, f]
                            else:
                                dve.wait_ge(act_done, 1 + n + 1)
                                dve.wait_ge(hw_ready, 1 + u * (NE * NF) + ((e - 1) * NF + f + 1 if e else 0))
                                dve.tensor_tensor(hh[:, f], h[:, f], psF[2 * f + 1][:], ALU.mult).then_inc(first_mult, 1)
                                dve.wait_ge(first_mult, 1 + n + 1)
                                src = hh[:, f]
                            dve.tensor_tensor(hw[:, e % 2, f], src, psW[e % 2][:], ALU.mult).then_inc(hw_ready, 1)
                    if ahead:
                        prepare(t, par, e)
                if ahead:
                    g.close()
                if behind:
                    xb = batch_view(x_sb, u)
                    tok = psT[:].rearrange("p (t d) -> p t d", t=TQ)
                    dve.wait_ge(out_tok, t)
                    if post_norm:
                        o.turn(u)
                        o.link(dve.tensor_copy(y[:], tok))
                        o.link(norm_dve(dve, o, y[:], xc[:], sq[:], st[:], y[:], var2_ready, seed2_ready, t))
                        o.link(dve.tensor_tensor(y[:], y[:], over_tiles(gamma[:]), ALU.mult))
                        dve.tensor_tensor(y[:], y[:], over_tiles(beta[:]), ALU.add).then_inc(ones_set, 1)
                        dve.wait_ge(ones_set, t)
                        dve.tensor_tensor(xb, xb, y[:], ALU.add).then_inc(x_done, 1)
                        dve.wait_ge(x_done, 1 + t)
                        o.close()
                    else:
                        dve.tensor_tensor(xb, xb, tok, ALU.add).then_inc(x_done, 1)
            turns(dve, emit)


U = 35
HU = H * U
NC, CU = 5, HU // 5
assert NC * CU == HU and CU <= P


def sparse_attention_stage(nc, name, x_sb, ident, w, m_scratch):
    with ExitStack() as ctx:
        m = Stage(nc, ctx, name)
        wq, wk, wv, wo = (m.sb(n, [P, D]) for n in ("wq", "wk", "wv", "wo"))
        bqk = m.sb("bqk", [P, 2])
        bq, bv, bo = (m.sb(n, [P, D]) for n in ("bq", "bv", "bo"))
        idx_i, idx, key_no, sample = m.sb("idx_i", [P, U], mybir.dt.int32), m.sb("idx", [P, U]), m.sb("key_no", [P, TQ]), m.sb("sample", [P, TQ, U])
        head_cols = m.sb("head_cols", [P, H])
        count_up = m.sb("count_up", [P, U])
        row_rank = m.sb("row_rank", [P, NC])
        block_mask = m.sb("block_mask", [P, NC, D])
        spread = m.sb("spread", [P, NB, HU], BF16)
        mean_w, ones = m.sb("mean_w", [P, P]), m.sb("ones", [1, L])
        xc, sq, xn = (m.sb(n, [P, TQ, D]) for n in ("xc", "sq", "xn"))
        st = m.sb("st", [P, 4, TQ])
        xnT, qT, kT = m.sb("xnT", [P, L]), m.sb("qT", [P, L]), m.sb("kT", [P, L])
        xsT, ksT, ks_blocks = m.sb("xsT", [P, U]), m.sb("ksT", [P, U]), m.sb("ks_blocks", [P, H, U])
        kT_all, q_all, v_all = (m.sb(n, [P, NB * L]) for n in ("kT_all", "q_all", "v_all"))
        top, tot, meas = m.sb("top", [P, TQ, H]), m.sb("tot", [P, TQ, H]), m.sb("meas", [P, TQ, H])
        measT = m.sb("measT", [H, L])
        chosen, eq, cum, best = m.sb("chosen", [P, L]), m.sb("eq", [P, L]), m.sb("cum", [P, L]), m.sb("best", [P, 8])
        m_all, m_left, need = m.sb("m_all", [P, L]), m.sb("m_left", [P, L]), m.sb("need", [P, 1])
        nil = m.sb("nil", [P, L])
        rank, rank_b = m.sb("rank", [P, L]), m.sb("rank_b", [P, L], BF16)
        rankT = m.sb("rankT", [P, TQ, P])
        q_st, hot, hotT = m.sb("q_st", [P, L]), m.sb("hot", [P, TQ, HU]), m.sb("hotT", [CU, NC, L])
        q_blocks = m.sb("q_blocks", [P, H, U])
        vmean = m.sb("vmean", [P, D])
        smax, ssum, probs = m.sb("smax", [CU, NC]), m.sb("ssum", [CU, NC]), m.sb("probs", [CU, 2, L])
        probsT, cxd, cx = m.sb("probsT", [P, TQ, CU]), m.sb("cxd", [CU, D]), m.sb("cx", [CU, NC, D])
        cxT = m.sb("cxT", [P, L])
        y = m.sb("y", [P, TQ, D])
        bank = [m.ps(f"bank{i}", [P, L]) for i in range(8)]
        loads = [(t[:], w[n]) for t, n in (
            (wq, "wq"), (wk, "wk"), (wv, "wv"), (wo, "wo"), (bqk, "bqk"), (bq, "bq"), (bv, "bv"), (bo, "bo"), (idx_i, "idx"),
            (key_no, "key_no"), (head_cols, "head_cols"), (count_up, "count_up"), (row_rank, "row_rank"),
            (block_mask, "block_mask"), (spread, "spread"), (mean_w, "mean_w"), (ones, "ones"))]
        n_loaded = DMA * len(loads)
        HALF = HU // 2
        HH = H // 2

        (
            loaded, idx_steps, sample_ready, norm_steps, var_ready, seed_ready, xn_ready, xnT_ps, xnT_ready, qk_ps, qT_ready,
            kT_ready, tok_ps, tok_ready, xs_ps, xs_ready, ks_ps, ks_steps, ks_ready, sc_ps, sc_used, meas_steps, meas_ready, mT_ps,
            mT_ready, m_stored, m_loaded, pick_steps, rank_ready, rankT_ps, rankT_ready, q_staged, hot_ready, hotT_ps,
            hotT_ready, qtop_ps, q_blocks_ready, vmean_ps, vmean_ready, s_ps, smax_ready, probs_ready, probsT_ps,
            probsT_ready, cx_ps, cxd_ready, cx_steps, cx_ready, cxT_ps, cxT_ready, y_ps, y_ready, x_done
        ) = (m.sem(n) for n in (
            "loaded", "idx_steps", "sample_ready", "norm_steps", "var_ready", "seed_ready", "xn_ready", "xnT_ps", "xnT_ready",
            "qk_ps", "qT_ready", "kT_ready", "tok_ps", "tok_ready", "xs_ps", "xs_ready", "ks_ps", "ks_steps", "ks_ready", "sc_ps",
            "sc_used", "meas_steps", "meas_ready", "mT_ps", "mT_ready", "m_stored", "m_loaded", "pick_steps",
            "rank_ready", "rankT_ps", "rankT_ready", "q_staged", "hot_ready", "hotT_ps", "hotT_ready", "qtop_ps",
            "q_blocks_ready", "vmean_ps", "vmean_ready", "s_ps", "smax_ready", "probs_ready", "probsT_ps",
            "probsT_ready", "cx_ps", "cxd_ready", "cx_steps", "cx_ready", "cxT_ps", "cxT_ready", "y_ps", "y_ready", "x_done"))

        def of(all_, b, q=None):
            return all_[:, bass.ds(b * L, L)] if q is None else all_[:, bass.ds(b * L + q * P, P)]

        block = m.block()

        @block.sync
        def _(sp):
            for dst, src in loads:
                sp.dma_start(dst, src).then_inc(loaded, DMA)
            sp.sem_inc(m_stored, DMA)
            with sp.Fori(0, NB) as b:
                sp.wait_ge(mT_ready, b + 1)
                sp.dma_start(m_scratch[bass.ds(b * H, H), :], measT[:]).then_inc(m_stored, DMA)
            sp.wait_ge(m_stored, DMA + NB * DMA)
            sp.dma_start(m_all[:], m_scratch).then_inc(m_loaded, DMA)

        @block.tensor
        def _(pe):
            pe.wait_ge(loaded, n_loaded)
            pe.wait_ge(sample_ready, 2)
            with pe.Fori(0, NB) as b:
                pe.wait_ge(xn_ready, b + 1)
                for q in range(TQ):
                    pe.transpose(bank[0][:, q * P:(q + 1) * P], xn[:, q], ident[:])
                for q in range(TQ):
                    ins = pe.matmul(bank[5][:, 0:U], xn[:, q], sample[:, q], start=(q == 0), stop=(q == TQ - 1))
                ins.then_inc(xnT_ps, 1)
                pe.wait_ge(xnT_ready, b + 1)
                pe.matmul(bank[1][:], wq[:], xnT[:], start=True, stop=True)
                pe.matmul(bank[2][:], wk[:], xnT[:], start=True, stop=True).then_inc(qk_ps, 1)
                for dst, wt in ((bank[3], wq), (bank[4], wv)):
                    for q in range(TQ):
                        ins = pe.matmul(dst[:, q * P:(q + 1) * P], xnT[:, q * P:(q + 1) * P], wt[:], start=True, stop=True)
                ins.then_inc(tok_ps, 1)
                pe.wait_ge(xs_ready, b + 1)
                pe.matmul(bank[5][:, 0:U], wk[:], xsT[:], start=True, stop=True).then_inc(ks_ps, 1)
                pe.wait_ge(ks_ready, b + 1)
                pe.wait_ge(qT_ready, b + 1)
                for q in range(TQ):
                    for half in range(2):
                        pe.wait_ge(sc_used, 1 + 8 * b + max(2 * q + half - 1, 0))
                        pe.matmul(bank[6 + half][:, 0:HALF], qT[:, q * P:(q + 1) * P],
                                  ks_blocks[:, half * HH:(half + 1) * HH].rearrange("p h u -> p (h u)"),
                                  start=True, stop=True).then_inc(sc_ps, 1)
                pe.wait_ge(meas_ready, b + 1)
                for q in range(TQ):
                    ins = pe.transpose(bank[0][0:H, q * P:(q + 1) * P], meas[:, q], ident[:])
                ins.then_inc(mT_ps, 1)

            pe.wait_ge(rank_ready, 1)
            for q in range(TQ):
                ins = pe.transpose(bank[0][:, q * P:(q + 1) * P], rank[:, q * P:(q + 1) * P], ident[:])
            ins.then_inc(rankT_ps, 1)

            with pe.Fori(0, NB) as b:
                pe.wait_ge(hot_ready, b + 1)
                pe.wait_ge(q_staged, b + 1)
                for half in range(2):
                    for q in range(TQ):
                        ins = pe.matmul(bank[half][:, 0:HALF], q_st[:, q * P:(q + 1) * P],
                                        hot[:, q, half * HALF:(half + 1) * HALF], start=(q == 0), stop=(q == TQ - 1))
                ins.then_inc(qtop_ps, 1)
                for q in range(TQ):
                    ins = pe.matmul(bank[5][:, 0:D], mean_w[:], of(v_all, b, q), start=(q == 0), stop=(q == TQ - 1))
                ins.then_inc(vmean_ps, 1)
                for c in range(NC):
                    pe.wait_ge(hotT_ready, 1 + NC * b + c)
                    pe.matmul(bank[6][0:CU, :], spread[:, bass.ds(b, 1), c * CU:(c + 1) * CU].rearrange("p a c -> p (a c)"),
                              rank_b[:], start=True, stop=True).then_inc(hotT_ps, 1)
                pe.wait_ge(q_blocks_ready, 2 * b + 2)
                pe.wait_ge(vmean_ready, b + 1)

                def scores(c):
                    if c >= 2:
                        pe.wait_ge(probs_ready, NC * b + c - 1)
                    flat = q_blocks[:].rearrange("p h u -> p (h u)")
                    pe.matmul(bank[2 + c % 2][0:CU, :], flat[:, c * CU:(c + 1) * CU], of(kT_all, b), start=True, stop=True).then_inc(s_ps, 1)

                scores(0)
                for c in range(NC):
                    if c + 1 < NC:
                        scores(c + 1)
                    pe.wait_ge(probs_ready, NC * b + c + 1)
                    if c:
                        pe.wait_ge(probsT_ready, NC * b + c)
                    for k in range(TQ):
                        ins = pe.transpose(bank[4][:, k * P:k * P + CU], probs[:, c % 2, k * P:(k + 1) * P], ident[0:CU, 0:CU])
                    ins.then_inc(probsT_ps, 1)
                    pe.wait_ge(probsT_ready, NC * b + c + 1)
                    if c:
                        pe.wait_ge(cxd_ready, NC * b + c)
                    for k in range(TQ):
                        ins = pe.matmul(bank[5][0:CU, 0:D], probsT[:, k], of(v_all, b, k), start=(k == 0), stop=(k == TQ - 1))
                    ins.then_inc(cx_ps, 1)
                pe.wait_ge(hotT_ready, 1 + NC * b + NC)
                pe.matmul(bank[7][:], vmean[0:1, :], ones[:], start=True, stop=False)
                for c in range(NC):
                    pe.wait_ge(cx_ready, NC * b + c + 1)
                    ins = pe.matmul(bank[7][:], cx[:, c], hotT[:, c], start=False, stop=(c == NC - 1))
                ins.then_inc(cxT_ps, 1)
                pe.wait_ge(cxT_ready, b + 1)
                for q in range(TQ):
                    ins = pe.matmul(bank[0][:, q * P:(q + 1) * P], cxT[:, q * P:(q + 1) * P], wo[:], start=True, stop=True)
                ins.then_inc(y_ps, 1)

        @block.scalar
        def _(act):
            act.preload_act_table_set("natural_log_exp_and_others")
            act.wait_ge(loaded, n_loaded)
            with act.Fori(0, NB) as b:
                norm_act(act, st, var_ready, seed_ready, b + 1)
                act.wait_ge(xnT_ps, b + 1)
                act.activation(xnT[:], bank[0][:], ACT.Copy).then_inc(xnT_ready, 1)
                act.activation(xsT[:], bank[5][:, 0:U], ACT.Copy).then_inc(xs_ready, 1)
                act.wait_ge(qk_ps, b + 1)
                act.activation(qT[:], bank[1][:], ACT.Identity, bias=bqk[:, 0:1]).then_inc(qT_ready, 1)
            with act.Fori(0, NB) as b:
                for c in range(NC):
                    n = NC * b + c
                    act.wait_ge(smax_ready, n + 1)
                    if c >= 1:
                        act.wait_ge(probsT_ps, n)
                    act.activation(probs[:, c % 2], bank[2 + c % 2][0:CU, :], ACT.Exp, bias=smax[:, c:c + 1],
                                   scale=float(HD ** -0.5), accum_out=ssum[:, c:c + 1]).then_inc(probs_ready, 1)
                    act.wait_ge(probsT_ps, n + 1)
                    if c >= 1:
                        act.wait_ge(cx_ps, n)
                    act.activation(probsT[:], bank[4][:].rearrange("p (t c) -> p t c", t=TQ)[:, :, 0:CU], ACT.Copy).then_inc(probsT_ready, 1)
                act.wait_ge(cxT_ps, b + 1)
                act.activation(cxT[:], bank[7][:], ACT.Copy).then_inc(cxT_ready, 1)

        @block.gpsimd
        def _(pool):
            with pool.Fori(0, NB) as b:
                pool.wait_ge(rankT_ready, 1)
                pool.wait_ge(y_ready, 1 + b)
                pool.tensor_tensor(q_st[:], of(q_all, b), nil[:], ALU.add).then_inc(q_staged, 1)

        @block.vector
        def _(dve):
            dve.wait_ge(loaded, n_loaded)
            for started in (sc_used, y_ready, hotT_ready):
                dve.sem_inc(started, 1)
            b0 = Steps(dve, idx_steps, 5)
            b0.link(dve.tensor_copy(idx[:], idx_i[:]))
            b0.link(dve.memset(nil[:], 0.0))
            b0.link(dve.tensor_scalar(eq[:, 0:U], idx[:], 0.0, float(L), ALU.is_lt, ALU.mult))
            b0.link(dve.tensor_tensor(idx[:], idx[:], eq[:, 0:U], ALU.add))
            b0.link(dve.tensor_scalar(idx[:], idx[:], 0.0, float(L - 1), ALU.max, ALU.min))
            b0.close()
            for q in range(TQ):
                ins = dve.tensor_scalar(sample[:, q], idx[:], key_no[:, q:q + 1], None, ALU.is_equal)
            ins.then_inc(sample_ready, 1)
            dve.tensor_copy(measT[:], nil[0:H, :]).then_inc(sample_ready, 1)
            dve.wait_ge(sample_ready, 2)

            a = Steps(dve, norm_steps, NORM_STEPS)
            ks = Steps(dve, ks_steps, 1)
            ms = Steps(dve, meas_steps, 2)
            with dve.Fori(0, NB) as b:
                a.turn(b)
                norm_dve(dve, a, batch_view(x_sb, b), xc[:], sq[:], st[:], xn[:], var_ready, seed_ready, b + 1).then_inc(xn_ready, 1)
                a.close()
                dve.wait_ge(xn_ready, b + 1)
                dve.wait_ge(qk_ps, b + 1)
                dve.tensor_scalar(of(kT_all, b), bank[2][:], bqk[:, 1:2], None, ALU.add).then_inc(kT_ready, 1)
                dve.wait_ge(tok_ps, b + 1)
                over = lambda t: t[:].unsqueeze(1).to_broadcast([P, TQ, D])
                dve.tensor_tensor(of(q_all, b).rearrange("p (t d) -> p t d", t=TQ), bank[3][:].rearrange("p (t d) -> p t d", t=TQ),
                                  over(bq), ALU.add)
                dve.tensor_tensor(of(v_all, b).rearrange("p (t d) -> p t d", t=TQ), bank[4][:].rearrange("p (t d) -> p t d", t=TQ),
                                  over(bv), ALU.add).then_inc(tok_ready, 1)
                ks.turn(b)
                dve.wait_ge(ks_ps, b + 1)
                ks.link(dve.tensor_scalar(ksT[:], bank[5][:, 0:U], bqk[:, 1:2], None, ALU.add))
                ks.close()
                dve.tensor_tensor(ks_blocks[:], ksT[:].unsqueeze(1).to_broadcast([P, H, U]),
                                  head_cols[:].unsqueeze(2).to_broadcast([P, H, U]), ALU.mult).then_inc(ks_ready, 1)
                for q in range(TQ):
                    for half in range(2):
                        dve.wait_ge(sc_ps, 8 * b + 2 * q + half + 1)
                        cols = bank[6 + half][:, 0:HALF].rearrange("p (h u) -> p h u", h=HH)
                        dve.reduce_max(top[:, q, half * HH:(half + 1) * HH], cols, AX.X)
                        dve.reduce_sum(tot[:, q, half * HH:(half + 1) * HH], cols, AX.X).then_inc(sc_used, 1)
                ms.turn(b)
                dve.wait_ge(sc_used, 1 + 8 * b + 8)
                ms.link(dve.tensor_scalar(tot[:], tot[:], -float(HD ** -0.5) / U, None, ALU.mult))
                ms.link(dve.tensor_scalar(top[:], top[:], float(HD ** -0.5), None, ALU.mult))
                ms.close()
                dve.tensor_tensor(meas[:], top[:], tot[:], ALU.add).then_inc(meas_ready, 1)
                dve.wait_ge(meas_ready, b + 1)
                dve.wait_ge(mT_ps, b + 1)
                dve.wait_ge(m_stored, DMA * b + DMA)
                dve.tensor_copy(measT[:], bank[0][0:H, :]).then_inc(mT_ready, 1)

            p = Steps(dve, pick_steps, 9 + 11)
            dve.wait_ge(m_loaded, DMA)
            source = m_all
            for r in range((U + 7) // 8):
                p.link(dve.max(best[:], source[:]))
                if r + 1 < (U + 7) // 8:
                    p.link(dve.match_replace(m_left[:], best[:], source[:], -3e38))
                    source = m_left
            last = (U - 1) % 8
            p.link(dve.tensor_scalar(chosen[:], m_all[:], best[:, last:last + 1], None, ALU.is_gt))
            p.link(dve.tensor_scalar(eq[:], m_all[:], best[:, last:last + 1], None, ALU.is_equal))
            p.link(dve.reduce_sum(need[:], chosen[:], AX.X))
            p.link(dve.tensor_scalar(need[:], need[:], -1.0, float(U), ALU.mult, ALU.add))
            p.link(dve.tensor_tensor_scan(cum[:], eq[:], nil[:], 0.0, ALU.add, ALU.add))
            p.link(dve.tensor_scalar(cum[:], cum[:], need[:, 0:1], None, ALU.is_le))
            p.link(dve.tensor_tensor(eq[:], eq[:], cum[:], ALU.mult))
            p.link(dve.tensor_tensor(chosen[:], chosen[:], eq[:], ALU.add))
            p.link(dve.tensor_tensor_scan(cum[:], chosen[:], nil[:], 0.0, ALU.add, ALU.add))
            p.link(dve.tensor_tensor(rank[:], cum[:], chosen[:], ALU.mult))
            p.link(dve.tensor_copy(rank_b[:], rank[:]))
            p.close()
            dve.tensor_copy(best[:], nil[:, 0:8]).then_inc(rank_ready, 1)
            dve.wait_ge(rankT_ps, 1)
            dve.tensor_copy(rankT[:].rearrange("p t r -> p (t r)"), bank[0][:]).then_inc(rankT_ready, 1)
            dve.wait_ge(rankT_ready, 1)

            with dve.Fori(0, NB) as b:
                for q in range(TQ):
                    ins = dve.tensor_tensor(hot[:, q].rearrange("p (h u) -> p h u", h=H),
                                            rankT[:, q, bass.ds(b * H, H)].unsqueeze(2).to_broadcast([P, H, U]),
                                            count_up[:].unsqueeze(1).to_broadcast([P, H, U]), ALU.is_equal)
                ins.then_inc(hot_ready, 1)
                for c in range(NC):
                    dve.wait_ge(hotT_ps, NC * b + c + 1)
                    dve.tensor_scalar(hotT[:, c], bank[6][0:CU, :], row_rank[0:CU, c:c + 1], None, ALU.is_equal).then_inc(hotT_ready, 1)
                dve.wait_ge(qtop_ps, b + 1)
                for half in range(2):
                    part = slice(half * HH, (half + 1) * HH)
                    dve.tensor_tensor(q_blocks[:, part], bank[half][:, 0:HALF].rearrange("p (h u) -> p h u", h=HH),
                                      head_cols[:, part].unsqueeze(2).to_broadcast([P, HH, U]), ALU.mult).then_inc(q_blocks_ready, 1)
                dve.wait_ge(vmean_ps, b + 1)
                dve.tensor_copy(vmean[:], bank[5][:, 0:D]).then_inc(vmean_ready, 1)
                dve.wait_ge(vmean_ready, b + 1)
                cs = Steps(dve, cx_steps, 3 * NC)
                cs.turn(b)

                def lowest(c):
                    dve.wait_ge(s_ps, NC * b + c + 1)
                    cs.link(dve.reduce_max(smax[:, c:c + 1], bank[2 + c % 2][0:CU, :], AX.X))
                    dve.tensor_scalar(smax[:, c:c + 1], smax[:, c:c + 1], -float(HD ** -0.5), None, ALU.mult).then_inc(smax_ready, 1)

                lowest(0)
                for c in range(NC):
                    if c + 1 < NC:
                        lowest(c + 1)
                    dve.wait_ge(cx_ps, NC * b + c + 1)
                    cs.link(dve.reciprocal(ssum[:, c:c + 1], ssum[:, c:c + 1]))
                    dve.tensor_scalar(cxd[:], bank[5][0:CU, 0:D], ssum[:, c:c + 1], None, ALU.mult).then_inc(cxd_ready, 1)
                    dve.wait_ge(cxd_ready, NC * b + c + 1)
                    cs.link(dve.tensor_tensor(cxd[:], cxd[:], vmean[0:CU, :], ALU.subtract))
                    dve.tensor_tensor(cx[:, c], cxd[:], block_mask[0:CU, c], ALU.mult).then_inc(cx_ready, 1)
                    dve.wait_ge(cx_ready, NC * b + c + 1)
                cs.close()
                dve.wait_ge(y_ps, b + 1)
                dve.tensor_tensor(y[:], bank[0][:].rearrange("p (t d) -> p t d", t=TQ), over_tiles(bo[:]), ALU.add).then_inc(y_ready, 1)
                dve.wait_ge(y_ready, 1 + b + 1)
                xb = batch_view(x_sb, b)
                dve.tensor_tensor(xb, xb, y[:], ALU.add).then_inc(x_done, 1)
                dve.wait_ge(x_done, b + 1)


DN, NS, DR, KC = 256, 16, 64, 4
DB = DN // P
DT_MIN, DT_MAX = 0.001, 0.1


def scan_stage(nc, name, x_sb, ident, w):
    with ExitStack() as ctx:
        m = Stage(nc, ctx, name)
        w_in = m.sb("w_in", [P, 4, P])
        w_dtl, w_bc = m.sb("w_dtl", [P, DB, DR]), m.sb("w_bc", [P, DB, 96])
        w_dt, w_out = m.sb("w_dt", [DR, DN]), m.sb("w_out", [P, DB, D])
        conv_w, conv_b, b_dt, d_par = m.sb("conv_w", [P, DB, KC]), m.sb("conv_b", [P, DB]), m.sb("b_dt", [P, DB]), m.sb("d_par", [P, DB])
        log_a, a_neg = m.sb("log_a", [P, DB, NS]), m.sb("a_neg", [P, DB, NS])
        ln_w, ln_b = m.sb("ln_w", [P, D]), m.sb("ln_b", [P, D])
        select = m.sb("select", [96, 2 * NS, P], BF16)
        xc, sq = m.sb("xc", [P, TQ, D]), m.sb("sq", [P, TQ, D])
        st = m.sb("st", [P, 4, TQ])
        xn = m.sb("xn", [P, 2, TQ, D])
        xn2, xn2T = m.sb("xn2", [P, TQ, D]), m.sb("xn2T", [P, L])
        xi, xv = m.sb("xi", [P, DB, KC - 1 + L]), m.sb("xv", [P, DB, L])
        u, zs = m.sb("u", [P, 2, DB, L]), m.sb("zs", [P, 2, DB, L])
        dtl = m.sb("dtl", [DR, L])
        bc_hi, bc_mid, bc_lo = (m.sb(n, [96, L], BF16) for n in ("bc_hi", "bc_mid", "bc_lo"))
        bc_rest, bc = m.sb("bc_rest", [96, L]), m.sb("bc", [96, 2, L], BF16)
        ex, s1, s2 = m.sb("ex", [P, DB, L]), m.sb("s1", [P, DB, L]), m.sb("s2", [P, DB, L])
        dt, dtu = m.sb("dt", [P, 2, DB, L]), m.sb("dtu", [P, 2, DB, L])
        decay, drive, hid, cs, hc = (m.sb(n, [P, 2, DB, L]) for n in ("decay", "drive", "hid", "cs", "hc"))
        y = m.sb("y", [P, DB, L])
        yt = m.sb("yt", [P, TQ, D])
        pA, pB = m.ps("pA", [P, L]), m.ps("pB", [P, L])
        psB = [m.ps(f"psB{i}", [P, L]) for i in range(2)]
        psC = [m.ps(f"psC{i}", [P, L]) for i in range(2)]
        psY = [m.ps(f"psY{i}", [P, L]) for i in range(DB)]
        loads = [(t[:], w[n]) for t, n in (
            (w_in, "w_in"), (w_dtl, "w_dtl"), (w_bc, "w_bc"), (w_dt, "w_dt"), (w_out, "w_out"), (conv_w, "conv_w"),
            (conv_b, "conv_b"), (b_dt, "b_dt"), (d_par, "d_par"), (log_a, "log_a"), (ln_w, "ln_w"), (ln_b, "ln_b"),
            (select, "select"))]
        n_loaded = DMA * len(loads)

        (
            loaded, cleared, a_steps, norm_steps, norm2_steps, conv_steps, bc_steps, dt_steps, out_steps, var_ready, seed_ready,
            xn_ready, var2_ready, seed2_ready, xn2_ready, xn2T_ps, xn2T_ready, xi_ps, xi_ready, conv_ready, z_ps, u_ready, low_ps,
            dtl_ready, bc_read, bc_ready, dt_ps, ex_ready, dt_read, dt_ready, dtu_ready, b_ps, c_ps, decay_ready, drive_ready,
            hid_ready, cs_ready, hc_ready, y_added, y_read, y_ready, out_ps, x_done
        ) = (m.sem(n) for n in (
            "loaded", "cleared", "a_steps", "norm_steps", "norm2_steps", "conv_steps", "bc_steps", "dt_steps", "out_steps", "var_ready",
            "seed_ready", "xn_ready", "var2_ready", "seed2_ready", "xn2_ready", "xn2T_ps", "xn2T_ready", "xi_ps",
            "xi_ready", "conv_ready", "z_ps", "u_ready", "low_ps", "dtl_ready", "bc_read", "bc_ready", "dt_ps", "ex_ready",
            "dt_read", "dt_ready", "dtu_ready", "b_ps", "c_ps", "decay_ready", "drive_ready", "hid_ready", "cs_ready", "hc_ready",
            "y_added", "y_read", "y_ready", "out_ps", "x_done"))
        N_CLEARED = 2

        block = m.block()

        @block.sync
        def _(sp):
            for dst, src in loads:
                sp.dma_start(dst, src).then_inc(loaded, DMA)

        @block.tensor
        def _(pe):
            pe.wait_ge(loaded, n_loaded)

            def emit(t, par, ahead, behind):
                v = t - 1

                def add_up(n):
                    pe.wait_ge(hc_ready, 1 + v * NS + n + 1)
                    if n == 0:
                        pe.wait_ge(y_read, 1 + v)
                    for d in range(DB):
                        ins = pe.matmul(psY[d][:], ident[:], hc[:, n % 2, d], start=(n == 0), stop=(n == NS - 1))
                    ins.then_inc(y_added, 1)

                for n in range(NS):
                    if behind:
                        if n == 0:
                            pe.wait_ge(bc_ready, t)
                        pe.wait_ge(drive_ready, 1 + v * NS + max(n - 1, 0))
                        pe.matmul(psB[n % 2][:], select[:, n], bc[:, 1 - par], start=True, stop=True).then_inc(b_ps, 1)
                        pe.wait_ge(cs_ready, 1 + v * NS + max(n - 1, 0))
                        pe.matmul(psC[n % 2][:], select[:, NS + n], bc[:, 1 - par], start=True, stop=True).then_inc(c_ps, 1)
                        if n >= 2:
                            add_up(n - 2)
                    if ahead and n == 2:
                        pe.wait_ge(xn2_ready, t + 1)
                        if behind:
                            pe.wait_ge(x_done, t)
                        for q in range(TQ):
                            ins = pe.transpose(pA[:, q * P:(q + 1) * P], xn2[:, q], ident[:])
                        ins.then_inc(xn2T_ps, 1)
                    if ahead and n == 4:
                        pe.wait_ge(xn2T_ready, t + 1)
                        pe.matmul(pA[:], w_in[:, 0], xn2T[:], start=True, stop=True)
                        pe.matmul(pB[:], w_in[:, 1], xn2T[:], start=True, stop=True).then_inc(xi_ps, 1)
                    if ahead and n == 6:
                        pe.wait_ge(xi_ready, t + 1)
                        pe.matmul(pA[:], w_in[:, 2], xn2T[:], start=True, stop=True)
                        pe.matmul(pB[:], w_in[:, 3], xn2T[:], start=True, stop=True).then_inc(z_ps, 1)
                    if ahead and n == 8:
                        pe.wait_ge(u_ready, t + 1)
                        for d in range(DB):
                            pe.matmul(pA[0:DR, :], w_dtl[:, d], u[:, par, d], start=(d == 0), stop=(d == DB - 1))
                        for d in range(DB):
                            ins = pe.matmul(pB[0:96, :], w_bc[:, d], u[:, par, d], start=(d == 0), stop=(d == DB - 1))
                        ins.then_inc(low_ps, 1)
                    if ahead and n == 10:
                        pe.wait_ge(dtl_ready, t + 1)
                        pe.wait_ge(bc_read, t + 1)
                        pe.matmul(pA[:], w_dt[:, 0:P], dtl[:], start=True, stop=True)
                        pe.matmul(pB[:], w_dt[:, P:2 * P], dtl[:], start=True, stop=True).then_inc(dt_ps, 1)
                if behind:
                    add_up(NS - 2)
                    add_up(NS - 1)
                    pe.wait_ge(y_ready, t)
                    if ahead:
                        pe.wait_ge(ex_ready, t + 1)
                    for q in range(TQ):
                        for d in range(DB):
                            ins = pe.matmul(pA[:, q * P:(q + 1) * P], y[:, d, q * P:(q + 1) * P], w_out[:, d],
                                            start=(d == 0), stop=(d == DB - 1))
                    ins.then_inc(out_ps, 1)
            turns(pe, emit)

        @block.scalar
        def _(act):
            act.wait_ge(loaded, n_loaded)
            act.wait_ge(cleared, N_CLEARED)
            act.activation(a_neg[:], log_a[:], ACT.Exp).then_inc(a_steps, 1)
            act.wait_ge(a_steps, 2)
            act.sem_inc(cs_ready, 1)
            act.sem_inc(decay_ready, 1)

            def emit(t, par, ahead, behind):
                v = t - 1
                for n in range(NS):
                    if behind:
                        if n == 0:
                            act.wait_ge(dt_ready, t)
                        act.wait_ge(hid_ready, 1 + v * NS + max(n - 1, 0))
                        for d in range(DB):
                            ins = act.activation(decay[:, n % 2, d, 1:L], dt[:, 1 - par, d, 1:L], ACT.Exp, scale=a_neg[:, d, n:n + 1])
                        ins.then_inc(decay_ready, 1)
                        act.wait_ge(c_ps, v * NS + n + 1)
                        act.wait_ge(hc_ready, 1 + v * NS + max(n - 1, 0))
                        act.activation(cs[:, n % 2, 0], psC[n % 2][:], ACT.Copy).then_inc(cs_ready, 1)
                    if ahead and n == 0:
                        norm_act(act, st, var_ready, seed_ready, t + 1)
                    if ahead and n == 1:
                        norm_act(act, st, var2_ready, seed2_ready, t + 1)
                    if ahead and n == 3:
                        act.wait_ge(xn2T_ps, t + 1)
                        act.activation(xn2T[:], pA[:], ACT.Copy).then_inc(xn2T_ready, 1)
                    if ahead and n == 5:
                        act.wait_ge(xi_ps, t + 1)
                        act.activation(xi[:, 0, KC - 1:], pA[:], ACT.Copy)
                        act.activation(xi[:, 1, KC - 1:], pB[:], ACT.Copy).then_inc(xi_ready, 1)
                    if ahead and n == 7:
                        act.wait_ge(z_ps, t + 1)
                        act.activation(zs[:, par, 0], pA[:], ACT.Silu)
                        act.activation(zs[:, par, 1], pB[:], ACT.Silu)
                        act.wait_ge(conv_ready, t + 1)
                        for d in range(DB):
                            ins = act.activation(u[:, par, d], xv[:, d], ACT.Silu, bias=conv_b[:, d:d + 1])
                        ins.then_inc(u_ready, 1)
                    if ahead and n == 9:
                        act.wait_ge(low_ps, t + 1)
                        act.activation(dtl[:], pA[0:DR, :], ACT.Copy).then_inc(dtl_ready, 1)
                    if ahead and n == 11:
                        act.wait_ge(dt_ps, t + 1)
                        act.activation(ex[:, 0], pA[:], ACT.Exp, bias=b_dt[:, 0:1])
                        act.activation(ex[:, 1], pB[:], ACT.Exp, bias=b_dt[:, 1:2]).then_inc(ex_ready, 1)
            turns(act, emit)

        @block.gpsimd
        def _(pool):
            pool.wait_ge(loaded, n_loaded)
            pool.sem_inc(hc_ready, 1)

            def emit(t, par, ahead, behind):
                v = t - 1
                for n in range(NS if behind else 0):
                    pool.wait_ge(hid_ready, 1 + v * NS + n + 1)
                    pool.wait_ge(cs_ready, 1 + v * NS + n + 1)
                    pool.wait_ge(y_added, 1 + v * NS + max(n - 1, 0))
                    pool.tensor_tensor(hc[:, n % 2], hid[:, n % 2], cs[:, n % 2, 0].unsqueeze(1).to_broadcast([P, DB, L]),
                                       ALU.mult).then_inc(hc_ready, 1)
            turns(pool, emit)

        @block.vector
        def _(dve):
            dve.wait_ge(loaded, n_loaded)
            for started in (drive_ready, hid_ready, y_added, y_read, x_done):
                dve.sem_inc(started, 1)
            dve.memset(decay[:], 0.0).then_inc(cleared, 1)
            dve.memset(xi[:], 0.0).then_inc(cleared, 1)
            dve.wait_ge(a_steps, 1)
            dve.tensor_scalar(a_neg[:], a_neg[:], -1.0, None, ALU.mult).then_inc(a_steps, 1)
            a = Steps(dve, norm_steps, NORM_STEPS)
            a2 = Steps(dve, norm2_steps, NORM_STEPS + 2)
            cv = Steps(dve, conv_steps, 3)
            bs = Steps(dve, bc_steps, 3)
            ds = Steps(dve, dt_steps, 8)
            o = Steps(dve, out_steps, 1)

            def prepare(t, par, slot):
                if slot == 0:
                    a.turn(t)
                    norm_dve(dve, a, batch_view(x_sb, t), xc[:], sq[:], st[:], xn[:, par], var_ready, seed_ready, t + 1).then_inc(xn_ready, 1)
                    dve.wait_ge(xn_ready, t + 1)
                    a.close()
                if slot == 1:
                    a2.turn(t)
                    a2.link(norm_dve(dve, a2, xn[:, par], xc[:], sq[:], st[:], xn2[:], var2_ready, seed2_ready, t + 1))
                    a2.link(dve.tensor_tensor(xn2[:], xn2[:], over_tiles(ln_w[:]), ALU.mult))
                    dve.tensor_tensor(xn2[:], xn2[:], over_tiles(ln_b[:]), ALU.add).then_inc(xn2_ready, 1)
                    a2.close()
                if slot == 6:
                    cv.turn(t)
                    dve.wait_ge(xi_ready, t + 1)
                    for d in range(DB):
                        ins = dve.tensor_scalar(xv[:, d], xi[:, d, 0:L], conv_w[:, d, 0:1], None, ALU.mult)
                    cv.link(ins)
                    for k in range(1, KC):
                        for d in range(DB):
                            ins = dve.scalar_tensor_tensor(xv[:, d], xi[:, d, k:k + L], conv_w[:, d, k:k + 1], xv[:, d], ALU.mult, ALU.add)
                        if k < KC - 1:
                            cv.link(ins)
                    ins.then_inc(conv_ready, 1)
                    cv.close()
                if slot == 9:
                    bs.turn(t)
                    dve.wait_ge(low_ps, t + 1)
                    bs.link(dve.tensor_copy(bc_hi[:], pB[0:96, :]))
                    bs.link(dve.tensor_tensor(bc_rest[:], pB[0:96, :], bc_hi[:], ALU.subtract))
                    bs.link(dve.tensor_copy(bc_mid[:], bc_rest[:]))
                    dve.tensor_tensor(bc_lo[:], bc_rest[:], bc_mid[:], ALU.subtract).then_inc(bc_read, 1)
                    dve.wait_ge(bc_read, t + 1)
                    bs.close()
                if slot == 10:
                    dve.tensor_copy(bc[0:32, par], bc_hi[0:32])
                    dve.tensor_copy(bc[32:64, par], bc_mid[32:64])
                    dve.tensor_copy(bc[64:96, par], bc_lo[64:96]).then_inc(bc_ready, 1)
                if slot == 12:
                    ds.turn(t)
                    dve.wait_ge(ex_ready, t + 1)
                    ds.link(dve.tensor_scalar(ex[:], ex[:], 0.2, None, ALU.min))
                    ds.link(dve.tensor_scalar(s1[:], ex[:], 2.0, None, ALU.add))
                    ds.link(dve.reciprocal(s1[:], s1[:]))
                    ds.link(dve.tensor_tensor(s1[:], s1[:], ex[:], ALU.mult))
                if slot == 13:
                    flat = lambda x: x.rearrange("p d l -> p (d l)")
                    ds.link(dve.tensor_tensor(s2[:], s1[:], s1[:], ALU.mult))
                    ds.link(dve.scalar_tensor_tensor(flat(ex[:]), flat(s2[:]), 7.0 / 5.0, flat(s2[:]), ALU.add, ALU.mult))
                    ds.link(dve.scalar_tensor_tensor(flat(ex[:]), flat(ex[:]), 7.0 / 3.0, flat(s2[:]), ALU.add, ALU.mult))
                    ds.link(dve.scalar_tensor_tensor(flat(ex[:]), flat(ex[:]), 7.0, flat(s1[:]), ALU.add, ALU.mult))
                if slot == 14:
                    dve.tensor_scalar(ex[:], ex[:], 2.0 / 7.0, DT_MIN, ALU.mult, ALU.add).then_inc(dt_read, 1)
                    dve.wait_ge(dt_read, t + 1)
                    dve.tensor_scalar(dt[:, par], ex[:], DT_MIN, DT_MAX, ALU.max, ALU.min).then_inc(dt_ready, 1)
                    dve.wait_ge(dt_ready, t + 1)
                    dve.tensor_tensor(dtu[:, par], dt[:, par], u[:, par], ALU.mult).then_inc(dtu_ready, 1)
                    ds.close()

            def emit(t, par, ahead, behind):
                v = t - 1

                def drives(n):
                    dve.wait_ge(b_ps, v * NS + n + 1)
                    if n == 0:
                        dve.wait_ge(dtu_ready, t)
                    dve.wait_ge(hid_ready, 1 + v * NS + max(n - 1, 0))
                    dve.tensor_tensor(drive[:, n % 2], dtu[:, 1 - par], psB[n % 2][:].unsqueeze(1).to_broadcast([P, DB, L]),
                                      ALU.mult).then_inc(drive_ready, 1)

                if behind:
                    drives(0)
                for n in range(NS):
                    if behind:
                        if n + 1 < NS:
                            drives(n + 1)
                        dve.wait_ge(decay_ready, 1 + v * NS + n + 1)
                        dve.wait_ge(drive_ready, 1 + v * NS + n + 1)
                        dve.wait_ge(hc_ready, 1 + v * NS + max(n - 1, 0))
                        dve.tensor_tensor_scan(hid[:, n % 2].rearrange("p d l -> p (d l)"), decay[:, n % 2].rearrange("p d l -> p (d l)"),
                                               drive[:, n % 2].rearrange("p d l -> p (d l)"), 0.0, ALU.mult, ALU.add).then_inc(hid_ready, 1)
                    if ahead:
                        prepare(t, par, n)
                if behind:
                    o.turn(v)
                    dve.wait_ge(y_added, 1 + t * NS)
                    for d in range(DB):
                        ins = dve.scalar_tensor_tensor(y[:, d], u[:, 1 - par, d], d_par[:, d:d + 1], psY[d][:], ALU.mult, ALU.add)
                    ins.then_inc(y_read, 1)
                    dve.wait_ge(y_read, 1 + t)
                    dve.tensor_tensor(y[:], y[:], zs[:, 1 - par], ALU.mult).then_inc(y_ready, 1)
                    dve.wait_ge(out_ps, t)
                    xb = batch_view(x_sb, v)
                    o.link(dve.tensor_tensor(yt[:], pA[:].rearrange("p (t d) -> p t d", t=TQ), xn[:, 1 - par], ALU.add))
                    dve.tensor_tensor(xb, xb, yt[:], ALU.add).then_inc(x_done, 1)
                    dve.wait_ge(x_done, 1 + t)
                    o.close()
            turns(dve, emit)


TREES = "qkvf"
NODES = 256
LW = 16
NBLK = NODES * LW // P
HALVES = NODES // P
DEPTH = 8
OFF = 2.0 ** 60


def tree_stage(nc, name, x_sb, ident, w):
    with ExitStack() as ctx:
        m = Stage(nc, ctx, name)
        w1 = {r: m.sb("w1" + r, [P, NBLK, P]) for r in TREES}
        w2 = {r: m.sb("w2" + r, [P, NBLK, P]) for r in TREES}
        nodes = {r: m.sb("nodes" + r, [P, NODES]) for r in TREES}
        b1 = m.sb("b1", [P, 4, NBLK])
        nb = m.sb("nb", [P, 4, NODES])
        b2 = m.sb("b2", [P, 3, 4, HALVES, D], BF16)
        pen = m.sb("pen", [P, NBLK // HALVES, P], BF16)
        identb = m.sb("identb", [P, P], BF16)
        pp = m.sb("pp", [P, 2, L])
        work = m.sb("work", [P, 2, L])
        xn, y = m.sb("xn", [P, TQ, D]), m.sb("y", [P, TQ, D])
        st = m.sb("st", [P, 4, TQ])
        xnT, yT = m.sb("xnT", [P, L]), m.sb("yT", [P, L])
        qT, kT, outT = m.sb("qT", [P, L]), m.sb("kT", [P, L]), m.sb("outT", [P, L])
        vtok = m.sb("vtok", [P, TQ, D])
        bits = m.sb("bits", [P, TQ, NODES], BF16)
        path = m.sb("path", [P, TQ, 2 * NODES], BF16)
        leafT, offT = m.sb("leafT", [P, 2, HALVES, L], BF16), m.sb("offT", [P, 2, HALVES, L], BF16)
        h = m.sb("h", [P, 2, L])
        smax, ssum = m.sb("smax", [P, TQ]), m.sb("ssum", [P, TQ])
        psH = [m.ps(f"psH{i}", [P, L]) for i in range(2)]
        psN = [m.ps(f"psN{i}", [P, L]) for i in range(2)]
        psA = [m.ps(f"psA{i}", [P, L]) for i in range(2)]
        psO, psR = m.ps("psO", [P, L]), m.ps("psR", [P, L])
        psRb = psR[:].bitcast(BF16).rearrange("p (a l) -> p a l", a=HALVES)
        probs, probsT = pp[:, 0], pp[:, 1].rearrange("p (k q) -> p k q", k=TQ)
        xc, sq = (work[:, i].rearrange("p (t d) -> p t d", t=TQ) for i in range(2))

        loaded, first_steps, norm_steps, att_steps, var_ready, seed_ready, xn_ready, xn_kept = (
            m.sem(n) for n in ("loaded", "first_steps", "norm_steps", "att_steps", "var_ready", "seed_ready",
                               "xn_ready", "xn_kept"))
        xnT_ps, xnT_ready, s_ps, smax_ready, p_ready, pT_ps, pT_ready, ctx_ps, y_ready, x_half, yT_ps, yT_ready = (
            m.sem(n) for n in ("xnT_ps", "xnT_ready", "s_ps", "smax_ready", "p_ready", "pT_ps", "pT_ready",
                               "ctx_ps", "y_ready", "x_half", "yT_ps", "yT_ready"))
        vtok_ps, vtok_ready, f_tok, x_done = (m.sem(n) for n in ("vtok_ps", "vtok_ready", "f_tok", "x_done"))
        w_loaded, node_ps, path_steps, path_ready, leaf_ps, leaf_ready, up_ps, h_ready, out_ps, out_ready = (
            {r: m.sem(n + r) for r in TREES}
            for n in ("w_loaded_", "node_ps_", "path_steps_", "path_ready_", "leaf_ps_", "leaf_ready_", "up_ps_",
                      "h_ready_", "out_ps_", "out_ready_"))

        small = [(nodes[r][:], w[r + "_nodes"]) for r in TREES]
        small += [(b1[:], w["b1"]), (nb[:], w["nb"]), (pp[:].rearrange("p a l -> p (a l)"), w["b2"]), (pen[:], w["pen"]), (identb[:], w["identb"])]
        n_loaded = DMA * len(small)
        side = {r: i % 2 for i, r in enumerate(TREES)}
        FIRST = 6
        SCALE = float(D ** -0.5)

        def turns_of(eng, turn):
            turn(0, True, False, True)
            with eng.Fori(1, NB - 1) as t:
                turn(t, True, True, True)
            turn(NB - 1, True, True, False)
            turn(NB, False, True, False)

        block = m.block()

        @block.sync
        def _(sp):
            for dst, src in small:
                sp.dma_start(dst, src).then_inc(loaded, DMA)
            for r in TREES:
                sp.dma_start(w1[r][:], w[r + "_w1"]).then_inc(w_loaded[r], DMA)
                sp.dma_start(w2[r][:], w[r + "_w2"]).then_inc(w_loaded[r], DMA)

        @block.tensor
        def _(pe):
            pe.wait_ge(loaded, n_loaded)
            pe.wait_ge(first_steps, FIRST)

            def tree(r, b, srcT, extras):
                def down(j):
                    pe.wait_ge(h_ready[r], b * NBLK + j + 1)
                    if j == 0:
                        n = 0
                        for part in range(3):
                            for half in range(HALVES):
                                pe.matmul(psO[:], b2[:, part, TREES.index(r), half], leafT[:, side[r], half],
                                          start=(n == 0), stop=False)
                                n += 1
                    ins = pe.matmul(psO[:], w2[r][:, j], h[:, j % 2], start=False, stop=(j == NBLK - 1))
                    if j == NBLK - 1:
                        ins.then_inc(out_ps[r], 1)

                for j in range(NBLK):
                    if b is not None:
                        if j == 0:
                            pe.wait_ge(w_loaded[r], 2 * DMA)
                            pe.wait_ge(leaf_ready[r], b + 1)
                        pe.matmul(psH[j % 2][:], pen[:, j % (NBLK // HALVES)], offT[:, side[r], j * HALVES // NBLK],
                                  start=True, stop=False)
                        pe.matmul(psH[j % 2][:], w1[r][:, j], srcT[:], start=False, stop=True).then_inc(up_ps[r], 1)
                    if j in extras:
                        extras[j]()
                    if b is not None and j:
                        down(j - 1)
                if b is not None:
                    down(NBLK - 1)

            def transposed(dst, tok, ready):
                for q in range(TQ):
                    ins = pe.transpose(dst[:, q * P:(q + 1) * P], tok[:, q], ident[:])
                ins.then_inc(ready, 1)

            def node_logits(r, srcT):
                for q in range(TQ):
                    ins = pe.matmul(psN[q // 2][:, q % 2 * NODES:(q % 2 + 1) * NODES], srcT[:, q * P:(q + 1) * P],
                                    nodes[r][:], start=True, stop=True)
                ins.then_inc(node_ps[r], 1)

            def leaves(r, b):
                pe.wait_ge(path_ready[r], b + 1)
                for half in range(HALVES):
                    for q in range(TQ):
                        ins = pe.transpose(psRb[:, half, q * P:(q + 1) * P],
                                           path[:, q, NODES + half * P:NODES + (half + 1) * P], identb[:])
                ins.then_inc(leaf_ps[r], 1)

            def xn_transposed(b):
                pe.wait_ge(xn_ready, b + 1)
                transposed(psA[1], xn, xnT_ps)

            xn_transposed(0)
            pe.wait_ge(xnT_ready, 1)
            node_logits("q", xnT)
            leaves("q", 0)

            def turn(t, cur, prev, nxt):
                u = t - 1
                batch = t if cur else None
                behind = u if prev else None

                def scores(i):
                    if i >= 2:
                        pe.wait_ge(p_ready, u * TQ + i - 1)
                    if i == 0:
                        pe.wait_ge(x_done, 1 + u)
                    pe.matmul(psA[i % 2][:], qT[:, i * P:(i + 1) * P], kT[:], start=True, stop=True).then_inc(s_ps, 1)

                def probs_transposed(i):
                    pe.wait_ge(p_ready, u * TQ + i + 1)
                    for k in range(TQ):
                        ins = pe.transpose(psN[1][:, k * P:(k + 1) * P], probs[:, k * P:(k + 1) * P], ident[:])
                    ins.then_inc(pT_ps, 1)

                def contexts(i):
                    pe.wait_ge(pT_ready, u * TQ + i + 1)
                    for k in range(TQ):
                        ins = pe.matmul(psN[0][:, i * P:(i + 1) * P], probsT[:, k], vtok[:, k],
                                        start=(k == 0), stop=(k == TQ - 1))
                    ins.then_inc(ctx_ps, 1)

                def at_q(slot):
                    if slot == 0 and cur:
                        node_logits("k", xnT)
                    if slot == 7 and cur:
                        leaves("k", t)
                    if prev:
                        i, at = divmod(slot - 8, 4)
                        if at == 0:
                            if i >= 1:
                                probs_transposed(i - 1)
                            if 0 <= i < TQ:
                                scores(i)
                        if at == 3 and i >= 1:
                            contexts(i - 1)
                tree("q", batch, xnT, {s: (lambda s=s: at_q(s)) for s in (0, 7, 8, 12, 15, 16, 19, 20, 23, 24, 27)})

                def at_k(slot):
                    if slot == 0 and prev:
                        pe.wait_ge(y_ready, u + 1)
                        transposed(psA[0], y, yT_ps)
                    if slot == 3 and cur:
                        node_logits("v", xnT)
                    if slot == 10 and cur:
                        leaves("v", t)
                tree("k", batch, xnT, {s: (lambda s=s: at_k(s)) for s in (0, 3, 10)})

                def at_v(slot):
                    if slot == 0 and prev:
                        pe.wait_ge(yT_ready, u + 1)
                        node_logits("f", yT)
                    if slot == 8 and prev:
                        leaves("f", u)
                tree("v", batch, xnT, {s: (lambda s=s: at_v(s)) for s in (0, 8)})

                def at_f(slot):
                    if slot == 1 and cur:
                        pe.wait_ge(out_ready["v"], t + 1)
                        transposed(psR, outT[:].rearrange("p (t d) -> p t d", t=TQ), vtok_ps)
                    if slot == 2 and nxt:
                        xn_transposed(t + 1)
                    if slot == 5 and nxt:
                        pe.wait_ge(xnT_ready, t + 2)
                        node_logits("q", xnT)
                    if slot == 12 and nxt:
                        pe.wait_ge(vtok_ready, t + 1)
                        leaves("q", t + 1)
                tree("f", behind, yT, {s: (lambda s=s: at_f(s)) for s in (1, 2, 5, 12)})
                if prev:
                    pe.wait_ge(out_ready["f"], u + 1)
                    transposed(psA[0], outT[:].rearrange("p (t d) -> p t d", t=TQ), f_tok)
            turns_of(pe, turn)

        @block.scalar
        def _(act):
            act.wait_ge(loaded, n_loaded)

            def tree(r, b, dst, extras):
                func = ACT.Gelu if r == "f" else ACT.Relu
                i = TREES.index(r)
                for j in range(NBLK):
                    if b is not None:
                        act.wait_ge(up_ps[r], b * NBLK + j + 1)
                        act.activation(h[:, j % 2], psH[j % 2][:], func, bias=b1[:, i, j:j + 1]).then_inc(h_ready[r], 1)
                    if j in extras:
                        extras[j]()
                if b is not None:
                    act.wait_ge(out_ps[r], b + 1)
                    act.activation(dst[:], psO[:], ACT.Copy).then_inc(out_ready[r], 1)

            def xn_transposed(b):
                act.wait_ge(xnT_ps, b + 1)
                act.activation(xnT[:], psA[1][:], ACT.Copy).then_inc(xnT_ready, 1)

            for i in range(3):
                norm_act(act, st, var_ready, seed_ready, i + 1)
            xn_transposed(0)

            def turn(t, cur, prev, nxt):
                u = t - 1
                batch = t if cur else None
                behind = u if prev else None

                def at_q(slot):
                    i = (slot - 9) // 4
                    act.wait_ge(smax_ready, u * TQ + i + 1)
                    act.activation(probs, psA[i % 2][:], ACT.Exp, bias=smax[:, i:i + 1], scale=SCALE,
                                   accum_out=ssum[:, i:i + 1]).then_inc(p_ready, 1)
                tree("q", batch, qT, {s: (lambda s=s: at_q(s)) for s in (9, 13, 17, 21)} if prev else {})

                def y_transposed():
                    act.wait_ge(yT_ps, u + 1)
                    act.activation(yT[:], psA[0][:], ACT.Copy).then_inc(yT_ready, 1)
                tree("k", batch, kT, {1: y_transposed} if prev else {})
                tree("v", batch, outT, {s: (lambda i=i: norm_act(act, st, var_ready, seed_ready, 3 * (t + 1) + i + 1))
                                        for i, s in enumerate((15, 19, 23))} if nxt else {})
                tree("f", behind, outT, {3: lambda: xn_transposed(t + 1)} if nxt else {})
            turns_of(act, turn)

        @block.vector
        def _(dve):
            dve.wait_ge(loaded, n_loaded)
            dve.sem_inc(x_done, 1)
            first = Steps(dve, first_steps, FIRST)
            raw, rest = (v[:].rearrange("p a l -> p (a l)") for v in (pp, work))
            part = [b2[:, i].rearrange("p r s d -> p (r s d)") for i in range(3)]
            first.link(dve.tensor_copy(part[0], raw))
            first.did(dve.tensor_scalar(nb[:], nb[:], -1.0, None, ALU.mult))
            first.link(dve.tensor_tensor(rest, raw, part[0], ALU.subtract))
            first.link(dve.tensor_copy(part[1], rest))
            first.link(dve.tensor_tensor(part[2], rest, part[1], ALU.subtract))
            first.link(dve.memset(path[:, :, 1:2], 1.0))
            first.close()
            a = Steps(dve, norm_steps, NORM_STEPS + 15)
            rs = {r: Steps(dve, path_steps[r], 2 + 2 * DEPTH - 1) for r in TREES}
            o = Steps(dve, att_steps, TQ + 1 + TQ)

            def norm(b):
                a.turn(b)
                a.link(norm_dve(dve, a, batch_view(x_sb, b), xc, sq, st[:], xn[:], var_ready, seed_ready, 3 * b + 1))
                a.link(dve.reduce_sum(st[:, 0, :], xn[:], AX.X))
                a.link(dve.tensor_scalar(st[:, 0, :], st[:, 0, :], 1.0 / D, None, ALU.mult))
                a.link(dve.tensor_tensor(xc, xn[:], st[:, 0, :].unsqueeze(2).to_broadcast([P, TQ, D]), ALU.subtract))
                a.link(dve.tensor_tensor(sq, xc, xc, ALU.mult))
                a.link(dve.reduce_sum(st[:, 1, :], sq, AX.X))
                dve.tensor_scalar(st[:, 1, :], st[:, 1, :], 1.0 / (D - 1), 1e-36, ALU.mult, ALU.max).then_inc(var_ready, 1)
                dve.wait_ge(seed_ready, 2 * (3 * b + 2))
                rsqrt_polish(dve, a, st[:, 2, :], st[:, 1, :], st[:, 3, :])
                a.link(dve.tensor_tensor(st[:, 1, :], st[:, 1, :], st[:, 2, :], ALU.mult))
                dve.tensor_scalar(st[:, 1, :], st[:, 1, :], EPS, None, ALU.add).then_inc(var_ready, 1)
                dve.wait_ge(seed_ready, 2 * (3 * b + 3))
                rsqrt_polish(dve, a, st[:, 2, :], st[:, 1, :], st[:, 3, :])
                a.close()
                dve.tensor_tensor(xn[:], xc, st[:, 2, :].unsqueeze(2).to_broadcast([P, TQ, D]), ALU.mult).then_inc(xn_ready, 1)
                dve.wait_ge(xn_ready, b + 1)

            def route(r, b):
                s = rs[r]
                s.turn(b)
                dve.wait_ge(node_ps[r], b + 1)
                for i in range(2):
                    s.did(dve.tensor_tensor(bits[:, 2 * i:2 * i + 2], psN[i][:].rearrange("p (t n) -> p t n", t=2),
                                            nb[:, TREES.index(r)].unsqueeze(1).to_broadcast([P, 2, NODES]), ALU.is_gt))
                s.wait()
                for level in range(DEPTH):
                    n = 2 ** level
                    children = path[:, :, 2 * n:4 * n].rearrange("p t (n two) -> p t n two", two=2)
                    s.link(dve.tensor_tensor(children[:, :, :, 1], path[:, :, n:2 * n], bits[:, :, n - 1:2 * n - 1], ALU.mult))
                    ins = dve.tensor_tensor(children[:, :, :, 0], path[:, :, n:2 * n], children[:, :, :, 1], ALU.subtract)
                    if level + 1 < DEPTH:
                        s.link(ins)
                ins.then_inc(path_ready[r], 1)
                s.close()
                dve.wait_ge(path_ready[r], b + 1)
                dve.wait_ge(leaf_ps[r], b + 1)
                dve.tensor_copy(leafT[:, side[r]], psRb)
                dve.tensor_scalar(offT[:, side[r]], psRb, -1.0, 1.0, ALU.mult, ALU.add).then_inc(leaf_ready[r], 1)

            norm(0)
            route("q", 0)

            def turn(t, cur, prev, nxt):
                u = t - 1
                if cur:
                    route("k", t)
                if prev:
                    o.turn(u)
                    for i in range(TQ):
                        dve.wait_ge(s_ps, u * TQ + i + 1)
                        o.link(dve.reduce_max(smax[:, i:i + 1], psA[i % 2][:], AX.X))
                        dve.tensor_scalar(smax[:, i:i + 1], smax[:, i:i + 1], -SCALE, None, ALU.mult).then_inc(smax_ready, 1)
                        dve.wait_ge(pT_ps, u * TQ + i + 1)
                        dve.tensor_copy(probsT, psN[1][:].rearrange("p (k q) -> p k q", k=TQ)).then_inc(pT_ready, 1)
                    o.link(dve.reciprocal(ssum[:], ssum[:]))
                    dve.wait_ge(ctx_ps, u * TQ + TQ)
                    for i in range(TQ):
                        o.did(dve.scalar_tensor_tensor(y[:, i], psN[0][:, i * P:(i + 1) * P], ssum[:, i:i + 1], y[:, i],
                                                       ALU.mult, ALU.add))
                    o.wait()
                    o.close()
                    dve.sem_inc(y_ready, 1)
                    xb = batch_view(x_sb, u)
                    dve.tensor_tensor(xb, xb, y[:], ALU.add).then_inc(x_half, 1)
                    dve.wait_ge(x_half, u + 1)
                if cur:
                    route("v", t)
                if prev:
                    route("f", u)
                if cur:
                    dve.tensor_copy(y[:], xn[:]).then_inc(xn_kept, 1)
                    dve.wait_ge(xn_kept, t + 1)
                if nxt:
                    norm(t + 1)
                if cur:
                    dve.wait_ge(vtok_ps, t + 1)
                    dve.tensor_copy(vtok[:], psR[:].rearrange("p (t d) -> p t d", t=TQ)).then_inc(vtok_ready, 1)
                if nxt:
                    route("q", t + 1)
                if prev:
                    dve.wait_ge(f_tok, u + 1)
                    xb = batch_view(x_sb, u)
                    dve.tensor_tensor(xb, xb, psA[0][:].rearrange("p (t d) -> p t d", t=TQ), ALU.add).then_inc(x_done, 1)
                    dve.wait_ge(x_done, 1 + u + 1)
            turns_of(dve, turn)


def program(nc, a, out):
    with ExitStack() as ctx:
        x_sb = ctx.enter_context(nc.sbuf_tensor("x_sb", [P, NB * TQ * D], F32))
        ident = ctx.enter_context(nc.sbuf_tensor("ident", [P, P], F32))
        x_loaded = ctx.enter_context(nc.semaphore("x_loaded"))
        x_stored = ctx.enter_context(nc.semaphore("x_stored"))
        qk_scratch = nc.dram_tensor("qk_scratch", (3, 2, P, L), BF16, kind="Internal").ap()
        mx_scratch = nc.dram_tensor("mx_scratch", (3, 64, P), BF16, kind="Internal").ap()
        m_scratch = nc.dram_tensor("m_scratch", (P, L), F32, kind="Internal").ap()
        with nc.Block() as block:
            @block.sync
            def _(sp):
                sp.dma_start(x_sb[:], a["x"]).then_inc(x_loaded, DMA)
                sp.dma_start(ident[:], a["ident"]).then_inc(x_loaded, DMA)
                sp.wait_ge(x_loaded, 2 * DMA)

        def some(prefix):
            return {k[len(prefix):]: v for k, v in a.items() if k.startswith(prefix)}

        if 0 in PHASES:
            attention_stage(nc, "l0", x_sb, ident, some("l0_"), qk_scratch, mx_scratch, causal=False)
        if 1 in PHASES:
            experts_stage(nc, "l1", x_sb, ident, some("l1_"), "linear")
        if 2 in PHASES:
            sparse_attention_stage(nc, "l2", x_sb, ident, some("l2_"), m_scratch)
        if 3 in PHASES:
            experts_stage(nc, "l3", x_sb, ident, some("l3_"), "swiglu")
        if 4 in PHASES:
            scan_stage(nc, "l4", x_sb, ident, some("l4_"))
        if 5 in PHASES:
            tree_stage(nc, "l5", x_sb, ident, some("l5_"))
        if 6 in PHASES:
            attention_stage(nc, "l6", x_sb, ident, some("l6_"), qk_scratch, mx_scratch, causal=True)
        if 7 in PHASES:
            experts_stage(nc, "l7", x_sb, ident, some("l7_"), "gelu")
        with nc.Block() as block:
            @block.sync
            def _(sp):
                sp.dma_start(out, x_sb[:]).then_inc(x_stored, DMA)
                sp.wait_ge(x_stored, DMA)


def attention_rows(slopes):
    q = np.zeros((R_MAX - NSLOT * HD, H, L), np.float32)
    k = np.zeros((R_ALL - NSLOT * HD, H, L), np.float32)
    at, n = R_EXT - NSLOT * HD, np.arange(L)
    if slopes is None:
        q[at] = 1.0
    else:
        q[at] = q[at + 1] = slopes[:, None]
        k[at], k[at + 1] = n - n % 2, n % 2
        whole = -slopes[:, None] * n
        high = whole.astype(mybir.dt.np(BF16)).astype(np.float32)
        q[at + 2], q[at + 3] = high, whole - high
        k[at + 2] = k[at + 3] = 1.0
    k[at + 4:] = 1.0
    return q.astype(mybir.dt.np(BF16)), k.astype(mybir.dt.np(BF16))


def layout(i):
    bf16 = mybir.dt.np(BF16)
    i = {k: np.asarray(v) for k, v in i.items()}

    def rows(v):
        return np.ascontiguousarray(np.broadcast_to(v.reshape(1, -1), (P, v.size)))

    a = {"x": np.ascontiguousarray(i["L0_attn_x"].reshape(NB * TQ, P, D).transpose(1, 0, 2).reshape(P, -1)),
         "ident": np.eye(P, dtype=np.float32)}
    for n, w, b in (("wq", "Wq", "bq"), ("wk", "Wk", "bk"), ("wv", "Wv", "bv"), ("wo", "Wo", "bo")):
        a["l0_" + n] = i["L0_attn_" + w].T
    a["l0_bqk"] = np.stack([i["L0_attn_bq"], i["L0_attn_bk"]], 1)
    a["l0_bv"], a["l0_bo"] = rows(i["L0_attn_bv"]), rows(i["L0_attn_bo"])
    a["l0_gamma"], a["l0_beta"] = rows(i["L0_attn_gamma"]), rows(i["L0_attn_beta"])
    a["l0_band"] = i["L0_attn_band_importance"]
    a["l0_qext"], a["l0_kext"] = attention_rows(None)

    for n, wt in (("wq", "Wq"), ("wk", "Wk"), ("wv", "Wv"), ("wo", "Wo")):
        a["l2_" + n] = i["L1_attn_" + wt].T
    for n in ("bq", "bv", "bo"):
        a["l2_" + n] = rows(i["L1_attn_" + n])
    a["l2_bqk"] = np.stack([i["L1_attn_bq"], i["L1_attn_bk"]], 1)
    a["l2_idx"] = rows(i["L1_attn_idx_k"])
    a["l2_key_no"] = np.arange(L, dtype=np.float32).reshape(TQ, P).T
    a["l2_head_cols"] = (np.arange(P)[:, None] // HD == np.arange(H)).astype(np.float32)
    a["l2_count_up"] = rows(np.arange(1, U + 1, dtype=np.float32))
    row = np.arange(NC * P) % P + np.arange(NC * P) // P * CU
    a["l2_row_rank"] = (row % U + 1).astype(np.float32).reshape(NC, P).T
    a["l2_block_mask"] = (row[:, None] // U == np.arange(D) // HD).astype(np.float32).reshape(NC, P, D).transpose(1, 0, 2)
    a["l2_spread"] = (np.arange(P)[:, None, None] == np.arange(NB)[:, None] * H + np.arange(HU) // U).astype(bf16)
    a["l2_mean_w"] = np.full((P, P), 1.0 / L, np.float32)
    a["l2_ones"] = np.ones((1, L), np.float32)

    def blocks(v):
        return v.reshape((DB, P) + v.shape[1:]).swapaxes(0, 1)

    a["l4_w_in"] = i["L2_attn_W_in"].T.reshape(P, 4, P)
    wx = i["L2_attn_W_x"].T
    a["l4_w_dtl"] = blocks(wx[:, :DR])
    a["l4_w_bc"] = blocks(np.tile(wx[:, DR:], (1, 3)))
    a["l4_w_dt"], a["l4_w_out"] = i["L2_attn_W_dt"].T, blocks(i["L2_attn_W_out"].T)
    a["l4_conv_w"] = blocks(i["L2_attn_conv_w"][:, 0])
    for n, v in (("conv_b", "conv_b"), ("b_dt", "b_dt"), ("d_par", "D_param"), ("log_a", "log_A")):
        a["l4_" + n] = blocks(i["L2_attn_" + v])
    a["l4_ln_w"], a["l4_ln_b"] = rows(i["L2_attn_ln_w"]), rows(i["L2_attn_ln_b"])
    a["l4_select"] = np.broadcast_to((np.arange(96)[:, None] % 32 == np.arange(2 * NS))[:, :, None], (96, 2 * NS, P)).astype(bf16)

    tree = {r: {n: i[f"L2_ffn_{r}_{n}"] for n in ("nw", "nb", "w1", "b1", "w2", "b2")} for r in TREES}
    for r in TREES:
        v = tree[r]
        a[f"l5_{r}_nodes"] = np.pad(v["nw"], ((0, 1), (0, 0))).T
        a[f"l5_{r}_w1"] = v["w1"].transpose(1, 0, 2).reshape(D, NBLK, P)
        a[f"l5_{r}_w2"] = v["w2"].reshape(NBLK, P, D).transpose(1, 0, 2)
    a["l5_b1"] = np.stack([tree[r]["b1"].reshape(NBLK, P).T for r in TREES], 1)
    a["l5_nb"] = rows(np.stack([np.pad(tree[r]["nb"], (0, 1)) for r in TREES])).reshape(P, 4, NODES)
    a["l5_b2"] = np.stack([tree[r]["b2"].reshape(HALVES, P, D) for r in TREES]).transpose(2, 0, 1, 3).reshape(P, -1)
    leaf = np.arange(NBLK // HALVES)[:, None] * (P // LW) + np.arange(P) // LW
    a["l5_pen"] = (-OFF * (np.arange(P)[:, None, None] == leaf)).astype(bf16)
    a["l5_identb"] = np.eye(P).astype(bf16)

    kv, kvb = i["L3_attn_kv_w"], i["L3_attn_kv_b"]
    a["l6_wq"], a["l6_wk"], a["l6_wv"], a["l6_wo"] = i["L3_attn_q_w"], kv[:, :D], kv[:, D:], i["L3_attn_o_w"]
    a["l6_bqk"] = np.stack([i["L3_attn_q_b"], kvb[:D]], 1)
    a["l6_bv"], a["l6_bo"] = rows(kvb[D:]), rows(i["L3_attn_o_b"])
    a["l6_qext"], a["l6_kext"] = attention_rows(np.arange(1, H + 1, dtype=np.float32) / H)
    a["l6_identb"] = np.eye(P).astype(bf16)
    later = np.triu(np.ones((P, P), np.float32), 1)
    a["l6_above"] = np.stack([-BIG * later.T, -BIG * later], 1).astype(bf16)

    def experts(n, wg, bg, up, b_up, down, b_down):
        ne = down.shape[0]
        a[n + "wg"], a[n + "bg"] = wg, rows(bg)
        a[n + "before"] = np.broadcast_to(np.tril(np.ones((NEG, NEG), np.float32), -1), (P, NEG, NEG))
        a[n + "identb"] = np.eye(P).astype(bf16)
        part, expert = np.divmod(np.arange(3 * ne), ne)
        a[n + "select"] = np.broadcast_to((expert[:, None] == np.arange(ne))[:, :, None], (3 * ne, ne, P)).astype(bf16)
        a[n + "w_down"] = down.reshape(ne, -1, P, D).transpose(2, 0, 1, 3)
        if up is not None:
            a[n + "w_up"] = up.reshape(ne, P, -1, P).transpose(1, 0, 2, 3)
        if b_up is not None:
            a[n + "b_up"] = b_up.reshape(ne, -1, P).transpose(2, 0, 1)
        if b_down is not None:
            a[n + "b_down"] = np.tile(b_down, (3, 1))

    experts("l1_", i["L0_ffn_Wg"], i["L0_ffn_bg"], None, None, i["L0_ffn_We"].transpose(0, 2, 1), i["L0_ffn_be"])
    w1, w3 = (np.concatenate([i["L1_ffn_We" + c], i["L1_ffn_Ws" + c][None]]) for c in "13")
    experts("l3_", i["L1_ffn_Wg"], np.zeros(NEG, np.float32), np.concatenate([w1, w3], 2), None,
            np.concatenate([i["L1_ffn_We2"], i["L1_ffn_Ws2"][None]]), None)
    experts("l7_", i["L3_ffn_gate_w"], i["L3_ffn_gate_b"], i["L3_ffn_w1"], i["L3_ffn_b1"], i["L3_ffn_w2"], i["L3_ffn_b2"])
    a["l7_gamma"], a["l7_beta"] = rows(i["L3_ffn_ln_g"]), rows(i["L3_ffn_ln_b"])
    return {k: np.ascontiguousarray(v) for k, v in a.items() if k[:2] in ("x", "id") or int(k[1]) in PHASES}


def kernel(**inputs):
    import concourse.bacc as bacc
    from concourse.bass_utils import run_bass_kernel_spmd

    nc = bacc.Bacc("TRN2", target_bir_lowering=False, num_devices=1)
    arrays = {f"in_{k}": v for k, v in layout(inputs).items()}
    args = {k[3:]: nc.dram_tensor(k, v.shape, mybir.dt.from_np(v.dtype), kind="ExternalInput").ap() for k, v in arrays.items()}
    out = nc.dram_tensor("out", (P, NB * TQ * D), F32, kind="ExternalOutput").ap()
    program(nc, args, out)
    got = run_bass_kernel_spmd(nc, [arrays], core_ids=[0]).results[0]["out"]
    return np.ascontiguousarray(got.reshape(P, NB * TQ, D).transpose(1, 0, 2)).reshape(NB, L, D)
```

```python
from contextlib import ExitStack

import numpy as np
import concourse.bass as bass
from concourse import mybir
from concourse.alu_op_type import AluOpType as ALU

F32, BF16 = mybir.dt.float32, mybir.dt.bfloat16
ACT = mybir.ActivationFunctionType
AX = mybir.AxisListType

P = 128
D = 128
NB, L = 8, 512
TQ = L // P
H, HD = 16, 8
HG = 4
EPS = 1e-5
BIG = 1e30
DMA = 16

Q_PART = (0, 0, 1, 1, 0, 2)
K_PART = (0, 1, 0, 1, 2, 0)
NSLOT = len(Q_PART)
R_EXT = 64
R_MAX = 68
R_ALL = 71


class Steps:

    def __init__(self, eng, sem, per_turn):
        self.eng, self.sem, self.per_turn, self.n, self.base = eng, sem, per_turn, 0, 0

    def turn(self, t):
        self.base, self.n = t * self.per_turn, 0

    def did(self, ins):
        ins.then_inc(self.sem, 1)
        self.n += 1

    def wait(self):
        self.eng.wait_ge(self.sem, self.base + self.n)

    def link(self, ins):
        self.did(ins)
        self.wait()

    def close(self):
        assert self.n == self.per_turn, (self.n, self.per_turn)


def batch_view(x_sb, t):
    return x_sb[:, bass.ds(t * (TQ * D), TQ * D)].rearrange("p (t d) -> p t d", d=D)


NORM_STEPS = 9


def rsqrt_polish(dve, s, y, v, tmp):
    s.link(dve.tensor_tensor(tmp, y, y, ALU.mult))
    s.link(dve.tensor_tensor(tmp, tmp, v, ALU.mult))
    s.link(dve.tensor_scalar(tmp, tmp, -0.5, 1.5, ALU.mult, ALU.add))
    s.link(dve.tensor_tensor(y, y, tmp, ALU.mult))


def norm_dve(dve, s, src, xc, sq, st, out, var_ready, seed_ready, k, eps=EPS):
    s.link(dve.reduce_sum(st[:, 0, :], src, AX.X))
    s.link(dve.tensor_scalar(st[:, 0, :], st[:, 0, :], 1.0 / D, None, ALU.mult))
    s.link(dve.tensor_tensor(xc, src, st[:, 0, :].unsqueeze(2).to_broadcast([P, TQ, D]), ALU.subtract))
    s.link(dve.tensor_tensor(sq, xc, xc, ALU.mult))
    s.link(dve.reduce_sum(st[:, 1, :], sq, AX.X))
    dve.tensor_scalar(st[:, 1, :], st[:, 1, :], 1.0 / D, eps, ALU.mult, ALU.add).then_inc(var_ready, 1)
    dve.wait_ge(seed_ready, 2 * k)
    rsqrt_polish(dve, s, st[:, 2, :], st[:, 1, :], st[:, 3, :])
    return dve.tensor_tensor(out, xc, st[:, 2, :].unsqueeze(2).to_broadcast([P, TQ, D]), ALU.mult)


def norm_act(act, st, var_ready, seed_ready, k):
    act.wait_ge(var_ready, k)
    act.activation(st[:, 2, :], st[:, 1, :], ACT.Ln).then_inc(seed_ready, 1)
    act.wait_ge(seed_ready, 2 * k - 1)
    act.activation(st[:, 2, :], st[:, 2, :], ACT.Exp, scale=-0.5).then_inc(seed_ready, 1)


def over_tiles(row):
    return row.unsqueeze(1).to_broadcast([P, TQ, D])


def turns(eng, emit):
    emit(0, 0, True, False)
    with eng.Fori(0, NB // 2 - 1) as k:
        emit(2 * k + 1, 1, True, True)
        emit(2 * k + 2, 0, True, True)
    emit(NB - 1, 1, True, True)
    emit(NB, 0, False, True)


def turns_but_two(eng, emit):
    emit(0, 0, True, False)
    with eng.Fori(0, NB // 2 - 2) as k:
        emit(2 * k + 1, 1, True, True)
        emit(2 * k + 2, 0, True, True)
    for t in range(NB - 3, NB):
        emit(t, t % 2, True, True)
    emit(NB, 0, False, True)


def has_after_next(t, ahead):
    return ahead and not (isinstance(t, int) and t >= NB - 2)


def has_next(t, ahead):
    return ahead and not (isinstance(t, int) and t == NB - 1)


class Stage:

    def __init__(self, nc, ctx, name):
        self.nc, self.ctx, self.name, self.sems = nc, ctx, name, []

    def sb(self, name, shape, dt=F32):
        return self.ctx.enter_context(self.nc.sbuf_tensor(f"{self.name}_{name}", shape, dt))

    def ps(self, name, shape, dt=F32):
        return self.ctx.enter_context(self.nc.psum_tensor(f"{self.name}_{name}", shape, dt))

    def sem(self, name):
        self.sems.append(self.ctx.enter_context(self.nc.semaphore(f"{self.name}_{name}")))
        return self.sems[-1]

    def block(self):
        self.ctx.callback(self.clear)
        return self.ctx.enter_context(self.nc.Block())

    def clear(self):
        with self.nc.Block() as block:
            @block.gpsimd
            def _(pool):
                for sem in self.sems:
                    pool.sem_clear(sem)


def attention_stage(nc, name, x_sb, ident, w, qk_scratch, mx_scratch, causal):
    with ExitStack() as ctx:
        m = Stage(nc, ctx, name)
        wq, wk, wv, wo = (m.sb(n, [P, D]) for n in ("wq", "wk", "wv", "wo"))
        bqk = m.sb("bqk", [P, 2])
        bv, bo = m.sb("bv", [P, D]), m.sb("bo", [P, D])
        xc, sq, xn = (m.sb(n, [P, TQ, D]) for n in ("xc", "sq", "xn"))
        st = m.sb("st", [P, 4, TQ])
        xnT = m.sb("xnT", [P, L])
        zeros = m.sb("zeros", [P, TQ * HG * (HD + 1)])
        qk32, rest = m.sb("qk32", [P, 2, L]), m.sb("rest", [P, 2, L])
        parts = m.sb("parts", [P, 3, 2, L], BF16)
        QS = m.sb("QS", [R_ALL, 2, H, L], BF16)
        KS = m.sb("KS", [R_ALL, 2, H, L], BF16)
        vhold = m.sb("vhold", [P, TQ, H, HD])
        vaug = m.sb("vaug", [P, 2, TQ, H, HD + 1])
        mxs, mx = m.sb("mxs", [P, HG, TQ]), m.sb("mx", [P, P])
        mneg, mrest = m.sb("mneg", [64, P]), m.sb("mrest", [64, P])
        mparts = m.sb("mparts", [64, 3, P], BF16)
        probs = m.sb("probs", [P, 2, TQ, L])
        vstage = m.sb("vstage", [P, TQ, HG, 32])
        oT = m.sb("oT", [P, L])
        rden = m.sb("rden", [P, TQ, HG])
        cx = m.sb("cx", [P, TQ, D])
        cxT = m.sb("cxT", [P, L])
        if causal:
            identb = m.sb("identb", [P, P], BF16)
            above = m.sb("above", [P, 2, P], BF16)
        else:
            yres = m.sb("yres", [P, 2, TQ, D])
            gamma, beta = m.sb("gamma", [P, D]), m.sb("beta", [P, D])
            band = m.sb("band", [1, 256])
            btop, bsel, beq, bcum = m.sb("btop", [1, 16]), m.sb("bsel", [1, 256]), m.sb("beq", [1, 256]), m.sb("bcum", [1, 256])
            bzero = m.sb("bzero", [1, 256])
            brow = m.sb("brow", [1, H, L], BF16)
        psT, psU = m.ps("psT", [P, L]), m.ps("psU", [P, L])
        psM = [m.ps(f"psM{i}", [P, L]) for i in range(2)]
        psS = [m.ps(f"psS{i}", [P, L]) for i in range(3)]
        psO = m.ps("psO", [P, L])

        (
            loaded, ones_set, norm_steps, m_steps, out_steps, xn_ready, yres_ready, var_ready, seed_ready,
            var2_ready, seed2_ready, xnT_ps, xnT_ready, q_ps, k_ps, q_evac, v_ps, v_ready, hi_ready, rest_ready,
            mid_ready, parts_ready, parts_stored, qk_loaded, sc_ready, sc_used, mx_ready, mT_ps, mparts_ready,
            mrow_stored, mrow_loaded, s_ready, p_ready, pv_done, oT_ps, o_used, cx_ready, cxT_ps, cxT_ready, y_ps,
            x_done, mask_row, band_steps, rden_ready, vstage_ready
        ) = (m.sem(n) for n in (
            "loaded", "ones_set", "norm_steps", "m_steps", "out_steps", "xn_ready", "yres_ready", "var_ready",
            "seed_ready", "var2_ready", "seed2_ready", "xnT_ps", "xnT_ready", "q_ps", "k_ps", "q_evac", "v_ps",
            "v_ready", "hi_ready", "rest_ready", "mid_ready", "parts_ready", "parts_stored", "qk_loaded",
            "sc_ready", "sc_used", "mx_ready", "mT_ps", "mparts_ready", "mrow_stored", "mrow_loaded", "s_ready",
            "p_ready", "pv_done", "oT_ps", "o_used", "cx_ready", "cxT_ps", "cxT_ready", "y_ps", "x_done",
            "mask_row", "band_steps", "rden_ready", "vstage_ready"))
        v_held, k_evac = m.sem("v_held"), m.sem("k_evac")

        loads = [(wq[:], w["wq"]), (wk[:], w["wk"]), (wv[:], w["wv"]), (wo[:], w["wo"]), (bqk[:], w["bqk"]),
                 (bv[:], w["bv"]), (bo[:], w["bo"])]
        for par in range(2):
            loads += [(QS[NSLOT * HD:R_MAX, par], w["qext"]), (KS[NSLOT * HD:R_ALL, par], w["kext"])]
        if causal:
            loads += [(identb[:], w["identb"]), (above[:], w["above"])]
        else:
            loads += [(gamma[:], w["gamma"]), (beta[:], w["beta"]), (band[:], w["band"])]
        n_loaded = DMA * len(loads)
        norms = 1 if causal else 2
        width = [(q + 1) * P if causal else L for q in range(TQ)]
        NG = H // HG
        first_q = [k * P if causal else 0 for k in range(TQ)]

        block = m.block()

        @block.sync
        def _(sp):
            for dst, src in loads:
                sp.dma_start(dst, src).then_inc(loaded, DMA)
            if not causal:
                sp.wait_ge(loaded, n_loaded)
                sp.wait_ge(band_steps, 12)
                for par in range(2):
                    sp.dma_start(KS[R_EXT:R_EXT + 1, par], brow[:]).then_inc(mask_row, DMA)

            sp.wait_ge(parts_ready, 1)
            sp.dma_start(qk_scratch.rearrange("a b p l -> p a b l"), parts[:]).then_inc(parts_stored, DMA)

            def emit(t, par, ahead, behind):
                if ahead:
                    sp.wait_ge(parts_stored, t * DMA + DMA)
                    for dst, side, part in ((QS, 0, Q_PART), (KS, 1, K_PART)):
                        for slot in range(NSLOT):
                            sp.dma_start(dst[slot * HD:(slot + 1) * HD, par],
                                         qk_scratch[part[slot], side].rearrange("(h e) l -> e h l", e=HD)
                                         ).then_inc(qk_loaded, DMA)
                    if has_next(t, ahead):
                        sp.wait_ge(parts_ready, t + 2)
                        sp.dma_start(qk_scratch.rearrange("a b p l -> p a b l"), parts[:]).then_inc(parts_stored, DMA)
                    sp.wait_ge(mparts_ready, t + 1)
                    sp.dma_start(mx_scratch.rearrange("a p l -> p a l"), mparts[:]).then_inc(mrow_stored, DMA)
                    sp.wait_ge(mrow_stored, t * DMA + DMA)
                    sp.dma_start(QS[R_MAX:R_ALL, par].rearrange("e h l -> e (h l)"),
                                 mx_scratch.rearrange("a p l -> a (p l)")).then_inc(mrow_loaded, DMA)
            turns(sp, emit)

        @block.tensor
        def _(pe):
            pe.wait_ge(loaded, n_loaded)
            pe.wait_ge(ones_set, 4)
            pe.sem_inc(pv_done, 2)

            def project(b):
                pe.wait_ge(xn_ready, b + 1)
                for q in range(TQ):
                    ins = pe.transpose(psT[:, q * P:(q + 1) * P], xn[:, q], ident[:])
                ins.then_inc(xnT_ps, 1)
                pe.wait_ge(xnT_ready, b + 1)
                pe.matmul(psU[:], wq[:], xnT[:], start=True, stop=True).then_inc(q_ps, 1)
                pe.matmul(psT[:], wk[:], xnT[:], start=True, stop=True).then_inc(k_ps, 1)
                pe.wait_ge(q_evac, b + 1)
                for q in range(TQ):
                    if q == TQ - 1:
                        pe.wait_ge(k_evac, b + 1)
                    ins = pe.matmul(psU[:, q * P:(q + 1) * P], xnT[:, q * P:(q + 1) * P], wv[:], start=True, stop=True)
                ins.then_inc(v_ps, 1)

            project(0)

            def emit(t, par, ahead, behind):
                if not causal:
                    pe.wait_ge(mask_row, 2 * DMA)
                u = t - 1

                def scores(g, j, k):
                    i = j * TQ + k
                    if i == 0:
                        pe.wait_ge(mrow_loaded, t * DMA)
                    bank = psS[i % 3]
                    pe.wait_ge(p_ready, 1 + (u * H + g * HG) * TQ + max(i - 2, 0))
                    if causal:
                        pe.matmul(bank[:, k * P:(k + 1) * P], identb[:], above[:, 0], start=True, stop=False,
                                  skip_group_check=True)
                    pe.matmul(bank[:, first_q[k]:L], KS[:, 1 - par, bass.ds(g * HG + j, 1), k * P:(k + 1) * P].rearrange("e h l -> e (h l)"),
                              QS[:, 1 - par, bass.ds(g * HG + j, 1), first_q[k]:L].rearrange("e h l -> e (h l)"),
                              start=not causal, stop=True, skip_group_check=True).then_inc(s_ready, 1)

                def for_maxima(g, j, q):
                    i = j * TQ + q
                    if i == 0:
                        pe.wait_ge(qk_loaded, (t + 1) * (2 * NSLOT * DMA))
                    bank = psM[i % 2]
                    pe.wait_ge(sc_used, 1 + (t * H + g * HG) * TQ + max(i - 1, 0))
                    if causal:
                        pe.matmul(bank[:, q * P:(q + 1) * P], identb[:], above[:, 1], start=True, stop=False,
                                  skip_group_check=True)
                    pe.matmul(bank[:, 0:width[q]], QS[0:R_MAX, par, bass.ds(g * HG + j, 1), q * P:(q + 1) * P].rearrange("e h l -> e (h l)"),
                              KS[0:R_MAX, par, bass.ds(g * HG + j, 1), 0:width[q]].rearrange("e h l -> e (h l)"),
                              start=not causal, stop=True, skip_group_check=True).then_inc(sc_ready, 1)

                def contexts(g, j, k):
                    pe.wait_ge(p_ready, 1 + (u * H + g * HG + j) * TQ + k + 1)
                    if j == 0 and k == 0:
                        pe.wait_ge(o_used, 1 + u * NG + g)
                        pe.wait_ge(vstage_ready, u * NG + g + 1)
                    ins = pe.matmul(psO[32 * j:32 * (j + 1), first_q[k]:L], vstage[:, k, j], probs[:, j % 2, k, first_q[k]:L],
                                    start=(k == 0), stop=(k == TQ - 1))
                    if k == TQ - 1:
                        ins.then_inc(pv_done, 1)

                def group(g):
                    for j in range(HG + 1):
                        if behind and j == 1 and not (isinstance(g, int) and g == 0):
                            turned(g - 1)
                        for i in range(TQ):
                            if behind and j < HG:
                                scores(g, j, i)
                            if ahead and j:
                                for_maxima(g, j - 1, i)
                            if behind and j:
                                contexts(g, j - 1, i)

                def turned(g):
                    pe.wait_ge(o_used, 1 + u * NG + g + 1)
                    for q in range(TQ):
                        ins = pe.transpose(psT[:, q * P:(q + 1) * P], oT[:, q * P:(q + 1) * P], ident[:])
                    ins.then_inc(oT_ps, 1)

                group(0)
                group(1)
                if has_next(t, ahead):
                    if behind:
                        pe.wait_ge(cx_ready, u * NG + 1)
                    project(t + 1)
                with pe.Fori(2, NG) as g:
                    group(g)
                if ahead:
                    pe.wait_ge(mx_ready, 1 + t * NG + NG)
                    pe.transpose(psM[0][:, 0:P], mx[:], ident[:]).then_inc(mT_ps, 1)
                if behind:
                    turned(NG - 1)
                    pe.wait_ge(cx_ready, t * NG)
                if behind:
                    for q in range(TQ):
                        ins = pe.transpose(psT[:, q * P:(q + 1) * P], cx[:, q], ident[:])
                    ins.then_inc(cxT_ps, 1)
                    pe.wait_ge(cxT_ready, t)
                    for q in range(TQ):
                        ins = pe.matmul(psU[:, q * P:(q + 1) * P], cxT[:, q * P:(q + 1) * P], wo[:], start=True, stop=True)
                    ins.then_inc(y_ps, 1)

            turns(pe, emit)

        @block.vector
        def _(dve):
            dve.memset(vaug[:], 1.0).then_inc(ones_set, 1)
            dve.memset(mx[:], 0.0).then_inc(ones_set, 1)
            dve.memset(vstage[:], 0.0).then_inc(ones_set, 1)
            dve.memset(zeros[:], 0.0).then_inc(ones_set, 1)
            dve.wait_ge(ones_set, 4)
            for started in (sc_used, mx_ready, o_used):
                dve.sem_inc(started, 1)
            a = Steps(dve, norm_steps, NORM_STEPS)

            def norm(b):
                a.turn(b)
                norm_dve(dve, a, batch_view(x_sb, b), xc[:], sq[:], st[:], xn[:], var_ready, seed_ready, b + 1).then_inc(xn_ready, 1)
                a.close()
                dve.wait_ge(xn_ready, b + 1)

            norm(0)
            dve.wait_ge(loaded, n_loaded)
            if not causal:
                b = Steps(dve, band_steps, 12)
                b.link(dve.memset(bzero[:], 0.0))
                b.link(dve.memset(brow[:], 0.0))
                b.link(dve.max(btop[:, 0:8], band[:]))
                b.link(dve.tensor_scalar(bsel[:], band[:], btop[:, 2:3], None, ALU.is_gt))
                b.link(dve.tensor_scalar(beq[:], band[:], btop[:, 2:3], None, ALU.is_equal))
                b.link(dve.reduce_sum(btop[:, 8:9], bsel[:], AX.X))
                b.link(dve.tensor_scalar(btop[:, 8:9], btop[:, 8:9], -1.0, 3.0, ALU.mult, ALU.add))
                b.link(dve.tensor_tensor_scan(bcum[:], beq[:], bzero[:], 0.0, ALU.add, ALU.add))
                b.link(dve.tensor_scalar(bcum[:], bcum[:], btop[:, 8:9], None, ALU.is_le))
                b.link(dve.tensor_tensor(beq[:], beq[:], bcum[:], ALU.mult))
                b.link(dve.tensor_tensor(bsel[:], bsel[:], beq[:], ALU.add))
                b.link(dve.tensor_scalar(brow[:, :, 0:256], bsel[:].unsqueeze(1).to_broadcast([1, H, 256]), -BIG, None, ALU.mult))
                b.close()
            mm = Steps(dve, m_steps, 4)
            o = Steps(dve, out_steps, 1 if causal else 4 + NORM_STEPS)

            def project(b):
                dve.wait_ge(q_ps, b + 1)
                dve.tensor_scalar(qk32[:, 0], psU[:], bqk[:, 0:1], float(HD ** -0.5), ALU.add, ALU.mult).then_inc(q_evac, 1)
                dve.wait_ge(k_ps, b + 1)
                dve.tensor_scalar(qk32[:, 1], psT[:], bqk[:, 1:2], None, ALU.add).then_inc(k_evac, 1)
                dve.wait_ge(v_ps, b + 1)
                dve.tensor_tensor(vhold[:], psU[:].rearrange("p (t h e) -> p t h e", t=TQ, h=H),
                                  bv[:].rearrange("p (h e) -> p h e", h=H).unsqueeze(1).to_broadcast([P, TQ, H, HD]),
                                  ALU.add).then_inc(v_held, 1)

            project(0)
            if causal:
                norm(1)

            def emit(t, par, ahead, behind):
                if ahead:
                    dve.wait_ge(v_held, t + 1)
                    dve.tensor_copy(vaug[:, par, :, :, 0:HD], vhold[:]).then_inc(v_ready, 1)
                    dve.wait_ge(v_ready, t + 1)
                    if not causal:
                        dve.tensor_tensor(yres[:, par], xn[:],
                                          over_tiles(bo[:]), ALU.add).then_inc(yres_ready, 1)
                        dve.wait_ge(yres_ready, t + 1)

                def group(g):
                    if ahead:
                        dve.wait_ge(mx_ready, 1 + t * NG + g)
                    for j in range(HG):
                        if ahead:
                            for q in range(TQ):
                                i = j * TQ + q
                                dve.wait_ge(sc_ready, (t * H + g * HG) * TQ + i + 1)
                                dve.reduce_max(mxs[:, j, q:q + 1], psM[i % 2][:, 0:width[q]], AX.X).then_inc(sc_used, 1)
                    if ahead:
                        dve.wait_ge(sc_used, 1 + (t * H + g * HG + HG) * TQ)
                        dve.tensor_scalar(mx[:, bass.ds(g * (HG * TQ), HG * TQ)], mxs[:].rearrange("p a b -> p (a b)"),
                                          1.0, None, ALU.mult).then_inc(mx_ready, 1)
                    if behind:
                        dve.wait_ge(pv_done, 2 + (t - 1) * H + g * HG + HG)
                        dve.tensor_copy(oT[:], psO[:]).then_inc(o_used, 1)

                def divide(g):
                    dve.wait_ge(oT_ps, (t - 1) * NG + g + 1)
                    turned = psT[:].rearrange("p (t j e) -> p t j e", t=TQ, j=HG)
                    dve.reciprocal(rden[:], turned[:, :, :, HD]).then_inc(rden_ready, 1)
                    dve.wait_ge(rden_ready, (t - 1) * NG + g + 1)
                    dve.tensor_tensor(cx[:, :, bass.ds(g * (HG * HD), HG * HD)].rearrange("p t (j e) -> p t j e", j=HG),
                                      turned[:, :, :, 0:HD], rden[:].unsqueeze(3).to_broadcast([P, TQ, HG, HD]),
                                      ALU.mult).then_inc(cx_ready, 1)

                def minus_maxima():
                    mm.turn(t)
                    dve.wait_ge(mT_ps, t + 1)
                    mm.link(dve.tensor_scalar(mneg[:], psM[0][0:64, 0:P], -1.0, None, ALU.mult))
                    mm.link(dve.tensor_copy(mparts[:, 0], mneg[:]))
                    mm.link(dve.tensor_tensor(mrest[:], mneg[:], mparts[:, 0], ALU.subtract))
                    mm.link(dve.tensor_copy(mparts[:, 1], mrest[:]))
                    dve.tensor_tensor(mparts[:, 2], mrest[:], mparts[:, 1], ALU.subtract).then_inc(mparts_ready, 1)
                    dve.wait_ge(mparts_ready, t + 1)
                    mm.close()

                for g in range(NG):
                    if g and behind:
                        dve.wait_ge(cx_ready, (t - 1) * NG + g)
                    group(g)
                    if g == 0 and not causal and has_next(t, ahead):
                        norm(t + 1)
                    if g == 1 and has_next(t, ahead):
                        project(t + 1)
                    if g == NG - 1 and ahead:
                        minus_maxima()
                    if behind:
                        divide(g)
                if causal and has_after_next(t, ahead):
                    norm(t + 2)
                if behind:
                    o.turn(t - 1)
                    dve.wait_ge(y_ps, t)
                    xb = batch_view(x_sb, t - 1)
                    y3 = psU[:].rearrange("p (t d) -> p t d", t=TQ)
                    if causal:
                        o.link(dve.tensor_tensor(xc[:], y3, over_tiles(bo[:]), ALU.add))
                        dve.tensor_tensor(xb, xb, xc[:], ALU.add).then_inc(x_done, 1)
                    else:
                        o.link(dve.tensor_tensor(cx[:], y3, yres[:, 1 - par], ALU.add))
                        o.link(norm_dve(dve, o, cx[:], xc[:], sq[:], st[:], cx[:], var2_ready, seed2_ready, t))
                        o.link(dve.tensor_tensor(cx[:], cx[:], over_tiles(gamma[:]), ALU.mult))
                        o.link(dve.tensor_tensor(cx[:], cx[:], over_tiles(beta[:]), ALU.add))
                        dve.tensor_tensor(xb, xb, cx[:], ALU.add).then_inc(x_done, 1)
                    dve.wait_ge(x_done, t)
                    o.close()
            (turns_but_two if causal else turns)(dve, emit)

        @block.gpsimd
        def _(pool):
            pool.wait_ge(ones_set, 4)

            def split(b):
                pool.wait_ge(hi_ready, b + 1)
                pool.tensor_tensor(rest[:], qk32[:], parts[:, 0], ALU.subtract).then_inc(rest_ready, 1)
                pool.wait_ge(mid_ready, b + 1)
                pool.tensor_tensor(parts[:, 2], rest[:], parts[:, 1], ALU.subtract).then_inc(parts_ready, 1)

            split(0)

            def emit(t, par, ahead, behind):
                for g in range(NG):
                    if g == 3 and has_next(t, ahead):
                        split(t + 1)
                    if behind:
                        pool.wait_ge(v_ready, t)
                        pool.wait_ge(pv_done, 2 + (t - 1) * H + g * HG)
                        pool.tensor_tensor(vstage[:, :, :, 0:HD + 1], vaug[:, 1 - par, :, g * HG:(g + 1) * HG, :],
                                           zeros[:].rearrange("p (a b c) -> p a b c", a=TQ, b=HG),
                                           ALU.add).then_inc(vstage_ready, 1)
            turns(pool, emit)

        @block.scalar
        def _(act):
            act.sem_inc(p_ready, 1)

            act.preload_act_table_set("natural_log_exp_and_others")

            def project(b):
                act.wait_ge(xnT_ps, b + 1)
                act.activation(xnT[:], psT[:], ACT.Copy).then_inc(xnT_ready, 1)
                act.wait_ge(k_evac, b + 1)
                if not (isinstance(b, int) and b == 0):
                    act.wait_ge(parts_stored, b * DMA)
                act.activation(parts[:, 0], qk32[:], ACT.Copy).then_inc(hi_ready, 1)
                act.wait_ge(rest_ready, b + 1)
                act.activation(parts[:, 1], rest[:], ACT.Copy).then_inc(mid_ready, 1)

            norm_act(act, st, var_ready, seed_ready, 1)
            project(0)
            if causal:
                norm_act(act, st, var_ready, seed_ready, 2)

            def emit(t, par, ahead, behind):
                u = t - 1

                def group(g):
                    for j in range(HG if behind else 0):
                        for k in range(TQ):
                            act.wait_ge(s_ready, (u * H + g * HG + j) * TQ + k + 1)
                            if k == 0:
                                act.wait_ge(pv_done, u * H + g * HG + j + 1)
                            act.activation(probs[:, j % 2, k, first_q[k]:L], psS[(j * TQ + k) % 3][:, first_q[k]:L],
                                           ACT.Exp).then_inc(p_ready, 1)

                group(0)
                if not causal and has_next(t, ahead):
                    norm_act(act, st, var_ready, seed_ready, t + 2)
                group(1)
                if has_next(t, ahead):
                    project(t + 1)
                if behind:
                    with act.Fori(2, NG) as g:
                        group(g)
                    act.wait_ge(cxT_ps, t)
                    act.activation(cxT[:], psT[:], ACT.Copy).then_inc(cxT_ready, 1)
                    if not causal:
                        norm_act(act, st, var2_ready, seed2_ready, t)
                if causal and has_after_next(t, ahead):
                    norm_act(act, st, var_ready, seed_ready, t + 3)
            (turns_but_two if causal else turns)(act, emit)


NEG = 8


def experts_stage(nc, name, x_sb, ident, w, kind):
    shared = kind == "swiglu"
    NE = NEG + shared
    F = {"linear": P, "swiglu": 256, "gelu": 512}[kind]
    NF = F // P
    post_norm = kind == "gelu"
    has_bias = kind != "swiglu"
    out_scale = 1.0 / 3.0 if shared else 1.0
    gate_scale = 1.0 / 0.9 if kind == "gelu" else 1.0
    with ExitStack() as ctx:
        m = Stage(nc, ctx, name)
        wg, bg = m.sb("wg", [P, NEG]), m.sb("bg", [P, NEG])
        w_down = m.sb("w_down", [P, NE, NF, D])
        select = m.sb("select", [3 * NE, NE, P], BF16)
        before = m.sb("before", [P, NEG, NEG])
        identb = m.sb("identb", [P, P], BF16)
        xc, sq, xn = (m.sb(n, [P, TQ, D]) for n in ("xc", "sq", "xn"))
        st = m.sb("st", [P, 4, TQ])
        xnT = m.sb("xnT", [P, 2, L])
        logit, rank, gexp, gate = (m.sb(n, [P, TQ, NEG]) for n in ("logit", "rank", "gexp", "gate"))
        above, equal = m.sb("above", [P, TQ * NEG, NEG]), m.sb("equal", [P, TQ * NEG, NEG])
        gsum = m.sb("gsum", [P, TQ])
        gparts = m.sb("gparts", [P, TQ, 3, NE], BF16)
        gT = m.sb("gT", [3 * NE, 2, L], BF16)
        hw = m.sb("hw", [P, 2, NF, L])
        outT = m.sb("outT", [P, L])
        y = m.sb("y", [P, TQ, D])
        loads = [(wg[:], w["wg"]), (bg[:], w["bg"]), (select[:], w["select"]), (before[:], w["before"]),
                 (identb[:], w["identb"])]
        weights = [(w_down[:], w["w_down"])]
        if kind != "linear":
            h = m.sb("h", [P, NF, L])
            w_up = m.sb("w_up", [P, NE, (2 if shared else 1) * NF, P])
            weights.insert(0, (w_up[:], w["w_up"]))
        if kind == "swiglu":
            hh = m.sb("hh", [P, NF, L])
        if kind == "gelu":
            b_up, gamma, beta = m.sb("b_up", [P, NE, NF]), m.sb("gamma", [P, D]), m.sb("beta", [P, D])
            loads += [(b_up[:], w["b_up"]), (gamma[:], w["gamma"]), (beta[:], w["beta"])]
        if has_bias:
            b_down = m.sb("b_down", [3 * NE, 3, D], BF16)
            b32, brest = m.sb("b32", [3 * NE, D]), m.sb("brest", [3 * NE, D])
            loads.append((b32[:], w["b_down"]))
        n_loaded = DMA * len(loads)
        psT, psO = m.ps("psT", [P, L]), m.ps("psO", [P, L])
        psW = [m.ps(f"psW{i}", [P, L]) for i in range(2)]
        psF = [m.ps(f"psF{i}", [P, L]) for i in range(4)]
        gT_bank = psT[:].bitcast(BF16)[0:3 * NE, 0:L]

        (
            loaded, bias_steps, norm_steps, gate_steps, out_steps, var_ready, seed_ready, xn_ready, xnT_ps, xnT_ready,
            logit_ps, top_ready, exp_ready, gparts_ready, gT_ps, gT_ready, w_ps, up_ps, act_done, first_mult, hw_ready,
            down_done, out_ps, outT_ready, out_tok, var2_ready, seed2_ready, x_done, ones_set
        ) = (m.sem(n) for n in (
            "loaded", "bias_steps", "norm_steps", "gate_steps", "out_steps", "var_ready", "seed_ready", "xn_ready", "xnT_ps",
            "xnT_ready", "logit_ps", "top_ready", "exp_ready", "gparts_ready", "gT_ps", "gT_ready", "w_ps", "up_ps",
            "act_done", "first_mult", "hw_ready", "down_done", "out_ps", "outT_ready", "out_tok", "var2_ready",
            "seed2_ready", "x_done", "ones_set"))
        w_loaded = m.sem("w_loaded")
        BIAS_STEPS = 5 if has_bias else 0
        S0 = 2 if post_norm else 0

        block = m.block()

        @block.sync
        def _(sp):
            for dst, src in loads:
                sp.dma_start(dst, src).then_inc(loaded, DMA)
            for dst, src in weights:
                sp.dma_start(dst, src).then_inc(w_loaded, DMA)

        @block.tensor
        def _(pe):
            pe.wait_ge(loaded, n_loaded)
            pe.sem_inc(down_done, 1)
            if has_bias:
                pe.wait_ge(bias_steps, BIAS_STEPS)

            def emit(t, par, ahead, behind):
                u = t - 1

                def up(e):
                    if e == 0:
                        pe.wait_ge(gT_ready, u + 1)
                    pe.wait_ge(hw_ready, 1 + u * (NE * NF) + max(e - 1, 0) * NF)
                    pe.matmul(psW[e % 2][:], select[:, e], gT[:, 1 - par], start=True, stop=True).then_inc(w_ps, 1)
                    for f in range(NF if kind != "linear" else 0):
                        if kind == "gelu":
                            pe.wait_ge(act_done, 1 + u * (NE * NF) + ((e - 1) * NF + f + 1 if e else 0))
                            pe.matmul(psF[f][:], w_up[:, e, f], xnT[:, 1 - par], start=True, stop=True).then_inc(up_ps, 1)
                        else:
                            pe.wait_ge(first_mult, 1 + u * (NE * NF) + ((e - 1) * NF + f + 1 if e else 0))
                            pe.matmul(psF[2 * f][:], w_up[:, e, f], xnT[:, 1 - par], start=True, stop=True)
                            pe.matmul(psF[2 * f + 1][:], w_up[:, e, NF + f], xnT[:, 1 - par], start=True, stop=True).then_inc(up_ps, 1)

                def down(e):
                    if e == 0:
                        pe.wait_ge(outT_ready, 1 + u)
                        for i in range(3 if has_bias else 0):
                            pe.matmul(psO[:], b_down[:, i], gT[:, 1 - par], start=(i == 0), stop=False)
                    for f in range(NF):
                        pe.wait_ge(hw_ready, 1 + u * (NE * NF) + e * NF + f + 1)
                        ins = pe.matmul(psO[:], w_down[:, e, f], hw[:, e % 2, f], start=(e == f == 0 and not has_bias),
                                        stop=(e == NE - 1 and f == NF - 1))
                    ins.then_inc(down_done, 1)

                for e in range(NE):
                    if behind:
                        up(e)
                        if e:
                            down(e - 1)
                    if ahead and e == S0:
                        pe.wait_ge(xn_ready, t + 1)
                        if behind:
                            pe.wait_ge(x_done, t)
                        for q in range(TQ):
                            ins = pe.transpose(psT[:, q * P:(q + 1) * P], xn[:, q], ident[:])
                        ins.then_inc(xnT_ps, 1)
                    if ahead and e == S0 + 2:
                        pe.wait_ge(xnT_ready, t + 1)
                        for q in range(TQ):
                            ins = pe.matmul(psT[:, q * NEG:(q + 1) * NEG], xnT[:, par, q * P:(q + 1) * P], wg[:], start=True, stop=True)
                        ins.then_inc(logit_ps, 1)
                    if ahead and e == S0 + 5:
                        pe.wait_ge(gparts_ready, t + 1)
                        for q in range(TQ):
                            ins = pe.transpose(gT_bank[:, q * P:(q + 1) * P], gparts[:, q].rearrange("p a b -> p (a b)"), identb[:])
                        ins.then_inc(gT_ps, 1)
                if not behind:
                    pe.wait_ge(w_loaded, DMA * len(weights))
                if behind:
                    down(NE - 1)
                    if ahead:
                        pe.wait_ge(gT_ready, t + 1)
                    pe.wait_ge(outT_ready, 2 + u)
                    for q in range(TQ):
                        ins = pe.transpose(psT[:, q * P:(q + 1) * P], outT[:, q * P:(q + 1) * P], ident[:])
                    ins.then_inc(out_tok, 1)
            turns(pe, emit)

        @block.scalar
        def _(act):
            act.sem_inc(outT_ready, 1)
            act.sem_inc(act_done, 1)

            def norm_seed(b):
                act.preload_act_table_set("natural_log_exp_and_others")
                norm_act(act, st, var_ready, seed_ready, b + 1)

            norm_seed(0)
            act.wait_ge(loaded, n_loaded)

            def emit(t, par, ahead, behind):
                u = t - 1
                for e in range(NE):
                    if behind and kind != "linear":
                        for f in range(NF):
                            n = u * (NE * NF) + e * NF + f
                            act.wait_ge(up_ps, n + 1)
                            if kind == "gelu":
                                act.wait_ge(hw_ready, 1 + u * (NE * NF) + ((e - 1) * NF + f + 1 if e else 0))
                                act.activation(h[:, f], psF[f][:], ACT.Gelu, bias=b_up[:, e, f:f + 1]).then_inc(act_done, 1)
                            else:
                                act.wait_ge(first_mult, 1 + u * (NE * NF) + ((e - 1) * NF + f + 1 if e else 0))
                                act.activation(h[:, f], psF[2 * f][:], ACT.Silu).then_inc(act_done, 1)
                    if ahead and e == S0 + 1:
                        act.wait_ge(xnT_ps, t + 1)
                        act.activation(xnT[:, par], psT[:], ACT.Copy).then_inc(xnT_ready, 1)
                    if ahead and e == S0 + 3:
                        act.wait_ge(top_ready, t + 1)
                        act.activation(gexp[:], logit[:], ACT.Exp, scale=-1.0 if shared else 1.0).then_inc(exp_ready, 1)
                if has_next(t, ahead):
                    norm_seed(t + 1)
                if behind:
                    act.wait_ge(down_done, 1 + t * NE)
                    act.activation(outT[:], psO[:], ACT.Copy, scale=out_scale).then_inc(outT_ready, 1)
                    if post_norm:
                        norm_act(act, st, var2_ready, seed2_ready, t)
            turns(act, emit)

        @block.vector
        def _(dve):
            for started in (hw_ready, first_mult, x_done):
                dve.sem_inc(started, 1)
            if shared:
                dve.memset(gparts[:], 0.0).then_inc(ones_set, 1)
                dve.wait_ge(ones_set, 1)
                dve.memset(gparts[:, :, 0, NEG], 1.0).then_inc(ones_set, 1)

            def bias_parts():
                b = Steps(dve, bias_steps, BIAS_STEPS)
                b.link(dve.tensor_copy(b_down[:, 0], b32[:]))
                b.link(dve.tensor_tensor(brest[:], b32[:], b_down[:, 0], ALU.subtract))
                b.link(dve.tensor_copy(b_down[:, 1], brest[:]))
                b.link(dve.tensor_tensor(brest[:], brest[:], b_down[:, 1], ALU.subtract))
                b.link(dve.tensor_copy(b_down[:, 2], brest[:]))
                b.close()

            a = Steps(dve, norm_steps, NORM_STEPS)
            g = Steps(dve, gate_steps, 21 if shared else 22)
            o = Steps(dve, out_steps, 3 + NORM_STEPS)

            def per_token(v):
                return v.unsqueeze(2).to_broadcast([P, TQ, NEG])

            def norm(b):
                a.turn(b)
                norm_dve(dve, a, batch_view(x_sb, b), xc[:], sq[:], st[:], xn[:], var_ready, seed_ready, b + 1).then_inc(xn_ready, 1)
                dve.wait_ge(xn_ready, b + 1)
                a.close()

            norm(0)
            dve.wait_ge(loaded, n_loaded)
            if has_bias:
                bias_parts()

            def prepare(t, par, slot):
                if slot == S0 + 2:
                    g.turn(t)
                    dve.wait_ge(logit_ps, t + 1)
                    g.link(dve.tensor_tensor(logit[:], psT[:, 0:TQ * NEG].rearrange("p (t e) -> p t e", t=TQ),
                                             bg[:].unsqueeze(1).to_broadcast([P, TQ, NEG]), ALU.add))
                    flat = logit[:].rearrange("p t e -> p (t e)")
                    mine = flat.unsqueeze(2).to_broadcast([P, TQ * NEG, NEG])
                    for q in range(TQ):
                        part = slice(q * NEG, (q + 1) * NEG)
                        other = logit[:, q].unsqueeze(1).to_broadcast([P, NEG, NEG])
                        g.did(dve.tensor_tensor(above[:, part], other, mine[:, part], ALU.is_gt))
                        g.did(dve.tensor_tensor(equal[:, part], other, mine[:, part], ALU.is_equal))
                    g.wait()
                    for q in range(TQ):
                        part = slice(q * NEG, (q + 1) * NEG)
                        ins = dve.tensor_tensor(equal[:, part], equal[:, part], before[:], ALU.mult)
                    g.link(ins)
                    g.link(dve.tensor_tensor(above[:], above[:], equal[:], ALU.add))
                    g.link(dve.reduce_sum(rank[:].rearrange("p t e -> p (t e)"), above[:], AX.X))
                    if shared:
                        dve.tensor_scalar(rank[:], rank[:], 2.0, None, ALU.is_lt).then_inc(top_ready, 1)
                    else:
                        g.link(dve.tensor_scalar(rank[:], rank[:], 2.0, None, ALU.is_lt))
                        g.link(dve.reduce_max(gsum[:], logit[:], AX.X))
                        g.link(dve.tensor_tensor(logit[:], logit[:], per_token(gsum[:]), ALU.subtract))
                        dve.tensor_scalar(logit[:], logit[:], gate_scale, None, ALU.mult).then_inc(top_ready, 1)
                if slot == S0 + 4:
                    dve.wait_ge(exp_ready, t + 1)
                    if shared:
                        g.link(dve.tensor_scalar(gexp[:], gexp[:], 1.0, None, ALU.add))
                        g.link(dve.reciprocal(gexp[:], gexp[:]))
                    g.link(dve.tensor_tensor(gate[:], gexp[:], rank[:], ALU.mult))
                    g.link(dve.reduce_sum(gsum[:], gate[:], AX.X))
                    g.link(dve.reciprocal(gsum[:], gsum[:]))
                    g.link(dve.tensor_tensor(gate[:], gate[:], per_token(gsum[:]), ALU.mult))
                    g.link(dve.tensor_copy(gparts[:, :, 0, 0:NEG], gate[:]))
                    g.link(dve.tensor_tensor(gate[:], gate[:], gparts[:, :, 0, 0:NEG], ALU.subtract))
                    g.link(dve.tensor_copy(gparts[:, :, 1, 0:NEG], gate[:]))
                    dve.tensor_tensor(gparts[:, :, 2, 0:NEG], gate[:], gparts[:, :, 1, 0:NEG], ALU.subtract).then_inc(gparts_ready, 1)
                    dve.wait_ge(gparts_ready, t + 1)
                if slot == S0 + 5:
                    dve.wait_ge(gT_ps, t + 1)
                    dve.tensor_copy(gT[:, par], gT_bank).then_inc(gT_ready, 1)

            def emit(t, par, ahead, behind):
                u = t - 1
                for e in range(NE):
                    if behind:
                        dve.wait_ge(w_ps, u * NE + e + 1)
                        for f in range(NF):
                            n = u * (NE * NF) + e * NF + f
                            if f == 0:
                                dve.wait_ge(down_done, 1 + u * NE + max(e - 1, 0))
                            if kind == "linear":
                                src = xnT[:, 1 - par]
                            elif kind == "gelu":
                                dve.wait_ge(act_done, 1 + n + 1)
                                src = h[:, f]
                            else:
                                dve.wait_ge(act_done, 1 + n + 1)
                                dve.wait_ge(hw_ready, 1 + u * (NE * NF) + ((e - 1) * NF + f + 1 if e else 0))
                                dve.tensor_tensor(hh[:, f], h[:, f], psF[2 * f + 1][:], ALU.mult).then_inc(first_mult, 1)
                                dve.wait_ge(first_mult, 1 + n + 1)
                                src = hh[:, f]
                            dve.tensor_tensor(hw[:, e % 2, f], src, psW[e % 2][:], ALU.mult).then_inc(hw_ready, 1)
                    if ahead:
                        prepare(t, par, e)
                if ahead:
                    g.close()
                if has_next(t, ahead):
                    norm(t + 1)
                if behind:
                    xb = batch_view(x_sb, u)
                    tok = psT[:].rearrange("p (t d) -> p t d", t=TQ)
                    dve.wait_ge(out_tok, t)
                    if post_norm:
                        o.turn(u)
                        o.link(dve.tensor_copy(y[:], tok))
                        o.link(norm_dve(dve, o, y[:], xc[:], sq[:], st[:], y[:], var2_ready, seed2_ready, t))
                        o.link(dve.tensor_tensor(y[:], y[:], over_tiles(gamma[:]), ALU.mult))
                        dve.tensor_tensor(y[:], y[:], over_tiles(beta[:]), ALU.add).then_inc(ones_set, 1)
                        dve.wait_ge(ones_set, t)
                        dve.tensor_tensor(xb, xb, y[:], ALU.add).then_inc(x_done, 1)
                        dve.wait_ge(x_done, 1 + t)
                        o.close()
                    else:
                        dve.tensor_tensor(xb, xb, tok, ALU.add).then_inc(x_done, 1)
            turns(dve, emit)


U = 35
HU = H * U
NC, CU = 5, HU // 5
assert NC * CU == HU and CU <= P


def sparse_attention_stage(nc, name, x_sb, ident, w, m_scratch):
    with ExitStack() as ctx:
        m = Stage(nc, ctx, name)
        wq, wk, wv, wo = (m.sb(n, [P, D]) for n in ("wq", "wk", "wv", "wo"))
        bqk = m.sb("bqk", [P, 2])
        bq, bv, bo = (m.sb(n, [P, D]) for n in ("bq", "bv", "bo"))
        idx_i, idx, key_no, sample = m.sb("idx_i", [P, U], mybir.dt.int32), m.sb("idx", [P, U]), m.sb("key_no", [P, TQ]), m.sb("sample", [P, TQ, U])
        head_cols = m.sb("head_cols", [P, H])
        count_up = m.sb("count_up", [P, U])
        row_rank = m.sb("row_rank", [P, NC])
        block_mask = m.sb("block_mask", [P, NC, D])
        spread = m.sb("spread", [P, NB, HU], BF16)
        mean_w, ones = m.sb("mean_w", [P, P]), m.sb("ones", [1, L])
        xc, sq, xn = (m.sb(n, [P, TQ, D]) for n in ("xc", "sq", "xn"))
        st = m.sb("st", [P, 4, TQ])
        xnT, qT, kT = m.sb("xnT", [P, L]), m.sb("qT", [P, L]), m.sb("kT", [P, L])
        xsT, ksT, ks_blocks = m.sb("xsT", [P, U]), m.sb("ksT", [P, U]), m.sb("ks_blocks", [P, H, U])
        kT_all, q_all, v_all = (m.sb(n, [P, NB * L]) for n in ("kT_all", "q_all", "v_all"))
        top, tot, meas = m.sb("top", [P, TQ, H]), m.sb("tot", [P, TQ, H]), m.sb("meas", [P, TQ, H])
        measT = m.sb("measT", [H, L])
        chosen, eq, cum, best = m.sb("chosen", [P, L]), m.sb("eq", [P, L]), m.sb("cum", [P, L]), m.sb("best", [P, 8])
        m_all, m_left, need = m.sb("m_all", [P, L]), m.sb("m_left", [P, L]), m.sb("need", [P, 1])
        nil = m.sb("nil", [P, L])
        rank, rank_b = m.sb("rank", [P, L]), m.sb("rank_b", [P, L], BF16)
        rankT = m.sb("rankT", [P, TQ, P])
        q_st, hot, hotT = m.sb("q_st", [P, L]), m.sb("hot", [P, TQ, HU]), m.sb("hotT", [CU, NC, L])
        q_blocks = m.sb("q_blocks", [P, H, U])
        vmean = m.sb("vmean", [P, D])
        smax, ssum, probs = m.sb("smax", [CU, NC]), m.sb("ssum", [CU, NC]), m.sb("probs", [CU, 2, L])
        probsT, cxd, cx = m.sb("probsT", [P, TQ, CU]), m.sb("cxd", [CU, D]), m.sb("cx", [CU, NC, D])
        cxT = m.sb("cxT", [P, L])
        y = m.sb("y", [P, TQ, D])
        bank = [m.ps(f"bank{i}", [P, L]) for i in range(8)]
        loads = [(t[:], w[n]) for t, n in (
            (wq, "wq"), (wk, "wk"), (wv, "wv"), (wo, "wo"), (bqk, "bqk"), (bq, "bq"), (bv, "bv"), (bo, "bo"), (idx_i, "idx"),
            (key_no, "key_no"), (head_cols, "head_cols"), (count_up, "count_up"), (row_rank, "row_rank"),
            (block_mask, "block_mask"), (spread, "spread"), (mean_w, "mean_w"), (ones, "ones"))]
        n_loaded = DMA * len(loads)
        HALF = HU // 2
        HH = H // 2

        (
            loaded, idx_steps, sample_ready, norm_steps, var_ready, seed_ready, xn_ready, xnT_ps, xnT_ready, qk_ps, qT_ready,
            kT_ready, tok_ps, tok_ready, xs_ps, xs_ready, ks_ps, ks_steps, ks_ready, sc_ps, sc_used, meas_steps, meas_ready, mT_ps,
            mT_ready, m_stored, m_loaded, pick_steps, rank_ready, rankT_ps, rankT_ready, q_staged, hot_ready, hotT_ps,
            hotT_ready, qtop_ps, q_blocks_ready, vmean_ps, vmean_ready, s_ps, smax_ready, probs_ready, probsT_ps,
            probsT_ready, cx_ps, cxd_ready, cx_steps, cx_ready, cxT_ps, cxT_ready, y_ps, y_ready, x_done
        ) = (m.sem(n) for n in (
            "loaded", "idx_steps", "sample_ready", "norm_steps", "var_ready", "seed_ready", "xn_ready", "xnT_ps", "xnT_ready",
            "qk_ps", "qT_ready", "kT_ready", "tok_ps", "tok_ready", "xs_ps", "xs_ready", "ks_ps", "ks_steps", "ks_ready", "sc_ps",
            "sc_used", "meas_steps", "meas_ready", "mT_ps", "mT_ready", "m_stored", "m_loaded", "pick_steps",
            "rank_ready", "rankT_ps", "rankT_ready", "q_staged", "hot_ready", "hotT_ps", "hotT_ready", "qtop_ps",
            "q_blocks_ready", "vmean_ps", "vmean_ready", "s_ps", "smax_ready", "probs_ready", "probsT_ps",
            "probsT_ready", "cx_ps", "cxd_ready", "cx_steps", "cx_ready", "cxT_ps", "cxT_ready", "y_ps", "y_ready", "x_done"))

        def of(all_, b, q=None):
            return all_[:, bass.ds(b * L, L)] if q is None else all_[:, bass.ds(b * L + q * P, P)]

        block = m.block()

        @block.sync
        def _(sp):
            for dst, src in loads:
                sp.dma_start(dst, src).then_inc(loaded, DMA)
            sp.sem_inc(m_stored, DMA)
            with sp.Fori(0, NB) as b:
                sp.wait_ge(mT_ready, 1 + b + 1)
                sp.dma_start(m_scratch[bass.ds(b * H, H), :], measT[:]).then_inc(m_stored, DMA)
            sp.wait_ge(m_stored, DMA + NB * DMA)
            sp.dma_start(m_all[:], m_scratch).then_inc(m_loaded, DMA)

        @block.tensor
        def _(pe):
            pe.wait_ge(loaded, n_loaded)
            pe.wait_ge(sample_ready, 2)
            with pe.Fori(0, NB) as b:
                pe.wait_ge(xn_ready, b + 1)
                pe.wait_ge(mT_ready, 1 + b)
                for q in range(TQ):
                    pe.transpose(bank[0][:, q * P:(q + 1) * P], xn[:, q], ident[:])
                for q in range(TQ):
                    ins = pe.matmul(bank[5][:, 0:U], xn[:, q], sample[:, q], start=(q == 0), stop=(q == TQ - 1))
                ins.then_inc(xnT_ps, 1)
                pe.wait_ge(xnT_ready, b + 1)
                pe.matmul(bank[1][:], wq[:], xnT[:], start=True, stop=True)
                pe.matmul(bank[2][:], wk[:], xnT[:], start=True, stop=True).then_inc(qk_ps, 1)
                for dst, wt in ((bank[3], wq), (bank[4], wv)):
                    for q in range(TQ):
                        ins = pe.matmul(dst[:, q * P:(q + 1) * P], xnT[:, q * P:(q + 1) * P], wt[:], start=True, stop=True)
                ins.then_inc(tok_ps, 1)
                pe.wait_ge(xs_ready, b + 1)
                pe.matmul(bank[5][:, 0:U], wk[:], xsT[:], start=True, stop=True).then_inc(ks_ps, 1)
                pe.wait_ge(ks_ready, b + 1)
                pe.wait_ge(qT_ready, b + 1)
                for q in range(TQ):
                    for half in range(2):
                        pe.wait_ge(sc_used, 1 + 8 * b + max(2 * q + half - 1, 0))
                        pe.matmul(bank[6 + half][:, 0:HALF], qT[:, q * P:(q + 1) * P],
                                  ks_blocks[:, half * HH:(half + 1) * HH].rearrange("p h u -> p (h u)"),
                                  start=True, stop=True).then_inc(sc_ps, 1)
                pe.wait_ge(meas_ready, b + 1)
                for q in range(TQ):
                    ins = pe.transpose(bank[0][0:H, q * P:(q + 1) * P], meas[:, q], ident[:])
                ins.then_inc(mT_ps, 1)

            pe.wait_ge(rank_ready, 1)
            for q in range(TQ):
                ins = pe.transpose(bank[0][:, q * P:(q + 1) * P], rank[:, q * P:(q + 1) * P], ident[:])
            ins.then_inc(rankT_ps, 1)

            def choose(b):
                pe.wait_ge(hot_ready, b + 1)
                pe.wait_ge(q_staged, b + 1)
                for half in range(2):
                    for q in range(TQ):
                        ins = pe.matmul(bank[half][:, 0:HALF], q_st[:, q * P:(q + 1) * P],
                                        hot[:, q, half * HALF:(half + 1) * HALF], start=(q == 0), stop=(q == TQ - 1))
                ins.then_inc(qtop_ps, 1)
                for q in range(TQ):
                    ins = pe.matmul(bank[1][:, L - D:], mean_w[:], of(v_all, b, q), start=(q == 0), stop=(q == TQ - 1),
                                    skip_group_check=True)
                ins.then_inc(vmean_ps, 1)

            def attend(b, more):
                pe.wait_ge(q_blocks_ready, 2 * b + 2)
                flat = q_blocks[:].rearrange("p h u -> p (h u)")

                def scores(c):
                    if c >= 2:
                        pe.wait_ge(probs_ready, NC * b + c - 1)
                    pe.matmul(bank[2 + c % 2][0:CU, :], flat[:, c * CU:(c + 1) * CU], of(kT_all, b), start=True, stop=True).then_inc(s_ps, 1)

                scores(0)
                for c in range(NC):
                    if c + 1 < NC:
                        scores(c + 1)
                    if c == 0:
                        pe.wait_ge(y_ready, 1 + b)
                    pe.wait_ge(hotT_ready, 1 + NC * b + c)
                    pe.matmul(bank[6][0:CU, :], spread[:, bass.ds(b, 1), c * CU:(c + 1) * CU].rearrange("p a c -> p (a c)"),
                              rank_b[:], start=True, stop=True).then_inc(hotT_ps, 1)
                    if c == NC - 1:
                        pe.wait_ge(vmean_ready, b + 1)
                        if more:
                            choose(b + 1)
                    pe.wait_ge(probs_ready, NC * b + c + 1)
                    if c:
                        pe.wait_ge(probsT_ready, NC * b + c)
                    for k in range(TQ):
                        ins = pe.transpose(bank[4][:, k * P:k * P + CU], probs[:, c % 2, k * P:(k + 1) * P], ident[0:CU, 0:CU])
                    ins.then_inc(probsT_ps, 1)
                    pe.wait_ge(probsT_ready, NC * b + c + 1)
                    if c:
                        pe.wait_ge(cxd_ready, NC * b + c)
                    for k in range(TQ):
                        ins = pe.matmul(bank[5][0:CU, 0:D], probsT[:, k], of(v_all, b, k), start=(k == 0), stop=(k == TQ - 1))
                    ins.then_inc(cx_ps, 1)
                pe.wait_ge(hotT_ready, 1 + NC * b + NC)
                pe.matmul(bank[7][:], vmean[0:1, :], ones[:], start=True, stop=False)
                for c in range(NC):
                    pe.wait_ge(cx_ready, NC * b + c + 1)
                    ins = pe.matmul(bank[7][:], cx[:, c], hotT[:, c], start=False, stop=(c == NC - 1))
                ins.then_inc(cxT_ps, 1)
                pe.wait_ge(cxT_ready, b + 1)
                for q in range(TQ):
                    ins = pe.matmul(bank[6][:, q * P:(q + 1) * P], cxT[:, q * P:(q + 1) * P], wo[:], start=True, stop=True)
                ins.then_inc(y_ps, 1)

            choose(0)
            with pe.Fori(0, NB - 1) as b:
                attend(b, True)
            attend(NB - 1, False)

        @block.scalar
        def _(act):
            act.preload_act_table_set("natural_log_exp_and_others")
            norm_act(act, st, var_ready, seed_ready, 1)
            act.wait_ge(loaded, n_loaded)

            def measure(b, more):
                act.wait_ge(xnT_ps, b + 1)
                act.activation(xnT[:], bank[0][:], ACT.Copy).then_inc(xnT_ready, 1)
                act.activation(xsT[:], bank[5][:, 0:U], ACT.Copy).then_inc(xs_ready, 1)
                act.wait_ge(qk_ps, b + 1)
                act.activation(qT[:], bank[1][:], ACT.Identity, bias=bqk[:, 0:1]).then_inc(qT_ready, 1)
                if more:
                    norm_act(act, st, var_ready, seed_ready, b + 2)

            with act.Fori(0, NB - 1) as b:
                measure(b, True)
            measure(NB - 1, False)
            with act.Fori(0, NB) as b:
                for c in range(NC):
                    n = NC * b + c
                    act.wait_ge(smax_ready, n + 1)
                    if c >= 1:
                        act.wait_ge(probsT_ps, n)
                    act.activation(probs[:, c % 2], bank[2 + c % 2][0:CU, :], ACT.Exp, bias=smax[:, c:c + 1],
                                   scale=float(HD ** -0.5), accum_out=ssum[:, c:c + 1]).then_inc(probs_ready, 1)
                    act.wait_ge(probsT_ps, n + 1)
                    if c >= 1:
                        act.wait_ge(cx_ps, n)
                    act.activation(probsT[:], bank[4][:].rearrange("p (t c) -> p t c", t=TQ)[:, :, 0:CU], ACT.Copy).then_inc(probsT_ready, 1)
                act.wait_ge(cxT_ps, b + 1)
                act.activation(cxT[:], bank[7][:], ACT.Copy).then_inc(cxT_ready, 1)

        @block.gpsimd
        def _(pool):
            pool.wait_ge(rankT_ready, 1)
            pool.tensor_tensor(q_st[:], q_all[:, 0:L], nil[:], ALU.add).then_inc(q_staged, 1)
            with pool.Fori(1, NB) as b:
                pool.wait_ge(qtop_ps, b)
                pool.tensor_tensor(q_st[:], of(q_all, b), nil[:], ALU.add).then_inc(q_staged, 1)

        @block.vector
        def _(dve):
            a = Steps(dve, norm_steps, NORM_STEPS)

            def norm(b):
                a.turn(b)
                norm_dve(dve, a, batch_view(x_sb, b), xc[:], sq[:], st[:], xn[:], var_ready, seed_ready, b + 1).then_inc(xn_ready, 1)
                a.close()
                dve.wait_ge(xn_ready, b + 1)

            norm(0)
            dve.wait_ge(loaded, n_loaded)
            for started in (sc_used, y_ready, hotT_ready, mT_ready):
                dve.sem_inc(started, 1)
            b0 = Steps(dve, idx_steps, 5)
            b0.link(dve.tensor_copy(idx[:], idx_i[:]))
            b0.link(dve.memset(nil[:], 0.0))
            b0.link(dve.tensor_scalar(eq[:, 0:U], idx[:], 0.0, float(L), ALU.is_lt, ALU.mult))
            b0.link(dve.tensor_tensor(idx[:], idx[:], eq[:, 0:U], ALU.add))
            b0.link(dve.tensor_scalar(idx[:], idx[:], 0.0, float(L - 1), ALU.max, ALU.min))
            b0.close()
            for q in range(TQ):
                ins = dve.tensor_scalar(sample[:, q], idx[:], key_no[:, q:q + 1], None, ALU.is_equal)
            ins.then_inc(sample_ready, 1)
            dve.tensor_copy(measT[:], nil[0:H, :]).then_inc(sample_ready, 1)
            dve.wait_ge(sample_ready, 2)

            ks = Steps(dve, ks_steps, 1)
            ms = Steps(dve, meas_steps, 2)

            def measure(b, more):
                if more:
                    dve.wait_ge(xnT_ps, b + 1)
                    norm(b + 1)
                dve.wait_ge(qk_ps, b + 1)
                dve.tensor_scalar(of(kT_all, b), bank[2][:], bqk[:, 1:2], None, ALU.add).then_inc(kT_ready, 1)
                dve.wait_ge(tok_ps, b + 1)
                over = lambda t: t[:].unsqueeze(1).to_broadcast([P, TQ, D])
                dve.tensor_tensor(of(q_all, b).rearrange("p (t d) -> p t d", t=TQ), bank[3][:].rearrange("p (t d) -> p t d", t=TQ),
                                  over(bq), ALU.add)
                dve.tensor_tensor(of(v_all, b).rearrange("p (t d) -> p t d", t=TQ), bank[4][:].rearrange("p (t d) -> p t d", t=TQ),
                                  over(bv), ALU.add).then_inc(tok_ready, 1)
                ks.turn(b)
                dve.wait_ge(ks_ps, b + 1)
                ks.link(dve.tensor_scalar(ksT[:], bank[5][:, 0:U], bqk[:, 1:2], None, ALU.add))
                ks.close()
                dve.tensor_tensor(ks_blocks[:], ksT[:].unsqueeze(1).to_broadcast([P, H, U]),
                                  head_cols[:].unsqueeze(2).to_broadcast([P, H, U]), ALU.mult).then_inc(ks_ready, 1)
                for q in range(TQ):
                    for half in range(2):
                        dve.wait_ge(sc_ps, 8 * b + 2 * q + half + 1)
                        cols = bank[6 + half][:, 0:HALF].rearrange("p (h u) -> p h u", h=HH)
                        dve.reduce_max(top[:, q, half * HH:(half + 1) * HH], cols, AX.X)
                        dve.reduce_sum(tot[:, q, half * HH:(half + 1) * HH], cols, AX.X).then_inc(sc_used, 1)
                ms.turn(b)
                dve.wait_ge(sc_used, 1 + 8 * b + 8)
                ms.link(dve.tensor_scalar(tot[:], tot[:], -float(HD ** -0.5) / U, None, ALU.mult))
                ms.link(dve.tensor_scalar(top[:], top[:], float(HD ** -0.5), None, ALU.mult))
                ms.close()
                dve.tensor_tensor(meas[:], top[:], tot[:], ALU.add).then_inc(meas_ready, 1)
                dve.wait_ge(meas_ready, b + 1)
                dve.wait_ge(mT_ps, b + 1)
                dve.wait_ge(m_stored, DMA * b + DMA)
                dve.tensor_copy(measT[:], bank[0][0:H, :]).then_inc(mT_ready, 1)

            with dve.Fori(0, NB - 1) as b:
                measure(b, True)
            measure(NB - 1, False)

            p = Steps(dve, pick_steps, 9 + 11)
            dve.wait_ge(m_loaded, DMA)
            source = m_all
            for r in range((U + 7) // 8):
                p.link(dve.max(best[:], source[:]))
                if r + 1 < (U + 7) // 8:
                    p.link(dve.match_replace(m_left[:], best[:], source[:], -3e38))
                    source = m_left
            last = (U - 1) % 8
            p.link(dve.tensor_scalar(chosen[:], m_all[:], best[:, last:last + 1], None, ALU.is_gt))
            p.link(dve.tensor_scalar(eq[:], m_all[:], best[:, last:last + 1], None, ALU.is_equal))
            p.link(dve.reduce_sum(need[:], chosen[:], AX.X))
            p.link(dve.tensor_scalar(need[:], need[:], -1.0, float(U), ALU.mult, ALU.add))
            p.link(dve.tensor_tensor_scan(cum[:], eq[:], nil[:], 0.0, ALU.add, ALU.add))
            p.link(dve.tensor_scalar(cum[:], cum[:], need[:, 0:1], None, ALU.is_le))
            p.link(dve.tensor_tensor(eq[:], eq[:], cum[:], ALU.mult))
            p.link(dve.tensor_tensor(chosen[:], chosen[:], eq[:], ALU.add))
            p.link(dve.tensor_tensor_scan(cum[:], chosen[:], nil[:], 0.0, ALU.add, ALU.add))
            p.link(dve.tensor_tensor(rank[:], cum[:], chosen[:], ALU.mult))
            p.link(dve.tensor_copy(rank_b[:], rank[:]))
            p.close()
            dve.tensor_copy(best[:], nil[:, 0:8]).then_inc(rank_ready, 1)
            dve.wait_ge(rankT_ps, 1)
            dve.tensor_copy(rankT[:].rearrange("p t r -> p (t r)"), bank[0][:]).then_inc(rankT_ready, 1)
            dve.wait_ge(rankT_ready, 1)

            cs = Steps(dve, cx_steps, 3 * NC)

            def choose(b):
                for q in range(TQ):
                    ins = dve.tensor_tensor(hot[:, q].rearrange("p (h u) -> p h u", h=H),
                                            rankT[:, q, bass.ds(b * H, H)].unsqueeze(2).to_broadcast([P, H, U]),
                                            count_up[:].unsqueeze(1).to_broadcast([P, H, U]), ALU.is_equal)
                ins.then_inc(hot_ready, 1)

            def blocks(b):
                dve.wait_ge(vmean_ps, b + 1)
                for half in range(2):
                    part = slice(half * HH, (half + 1) * HH)
                    dve.tensor_tensor(q_blocks[:, part], bank[half][:, 0:HALF].rearrange("p (h u) -> p h u", h=HH),
                                      head_cols[:, part].unsqueeze(2).to_broadcast([P, HH, U]), ALU.mult).then_inc(q_blocks_ready, 1)

            def attend(b, more):
                dve.wait_ge(vmean_ps, b + 1)
                dve.tensor_copy(vmean[:], bank[1][:, L - D:]).then_inc(vmean_ready, 1)
                dve.wait_ge(vmean_ready, b + 1)
                cs.turn(b)

                def lowest(c):
                    dve.wait_ge(s_ps, NC * b + c + 1)
                    cs.link(dve.reduce_max(smax[:, c:c + 1], bank[2 + c % 2][0:CU, :], AX.X))
                    dve.tensor_scalar(smax[:, c:c + 1], smax[:, c:c + 1], -float(HD ** -0.5), None, ALU.mult).then_inc(smax_ready, 1)

                lowest(0)
                if more:
                    choose(b + 1)
                for c in range(NC):
                    if c + 1 < NC:
                        lowest(c + 1)
                    dve.wait_ge(hotT_ps, NC * b + c + 1)
                    dve.tensor_scalar(hotT[:, c], bank[6][0:CU, :], row_rank[0:CU, c:c + 1], None, ALU.is_equal).then_inc(hotT_ready, 1)
                    dve.wait_ge(cx_ps, NC * b + c + 1)
                    cs.link(dve.reciprocal(ssum[:, c:c + 1], ssum[:, c:c + 1]))
                    dve.tensor_scalar(cxd[:], bank[5][0:CU, 0:D], ssum[:, c:c + 1], None, ALU.mult).then_inc(cxd_ready, 1)
                    dve.wait_ge(cxd_ready, NC * b + c + 1)
                    cs.link(dve.tensor_tensor(cxd[:], cxd[:], vmean[0:CU, :], ALU.subtract))
                    dve.tensor_tensor(cx[:, c], cxd[:], block_mask[0:CU, c], ALU.mult).then_inc(cx_ready, 1)
                    dve.wait_ge(cx_ready, NC * b + c + 1)
                cs.close()
                if more:
                    blocks(b + 1)
                dve.wait_ge(y_ps, b + 1)
                dve.tensor_tensor(y[:], bank[6][:].rearrange("p (t d) -> p t d", t=TQ), over_tiles(bo[:]), ALU.add).then_inc(y_ready, 1)
                dve.wait_ge(y_ready, 1 + b + 1)
                xb = batch_view(x_sb, b)
                dve.tensor_tensor(xb, xb, y[:], ALU.add).then_inc(x_done, 1)
                dve.wait_ge(x_done, b + 1)

            choose(0)
            blocks(0)
            with dve.Fori(0, NB - 1) as b:
                attend(b, True)
            attend(NB - 1, False)


DN, NS, DR, KC = 256, 16, 64, 4
DB = DN // P
DT_MIN, DT_MAX = 0.001, 0.1


def scan_stage(nc, name, x_sb, ident, w):
    with ExitStack() as ctx:
        m = Stage(nc, ctx, name)
        w_in = m.sb("w_in", [P, 4, P])
        w_dtl, w_bc = m.sb("w_dtl", [P, DB, DR]), m.sb("w_bc", [P, DB, 96])
        w_dt, w_out = m.sb("w_dt", [DR, DN]), m.sb("w_out", [P, DB, D])
        conv_w, conv_b, b_dt, d_par = m.sb("conv_w", [P, DB, KC]), m.sb("conv_b", [P, DB]), m.sb("b_dt", [P, DB]), m.sb("d_par", [P, DB])
        log_a, a_neg = m.sb("log_a", [P, DB, NS]), m.sb("a_neg", [P, DB, NS])
        ln_w, ln_b = m.sb("ln_w", [P, D]), m.sb("ln_b", [P, D])
        select = m.sb("select", [96, 2 * NS, P], BF16)
        xc, sq = m.sb("xc", [P, TQ, D]), m.sb("sq", [P, TQ, D])
        st = m.sb("st", [P, 4, TQ])
        xn = m.sb("xn", [P, TQ, D])
        xn2, xn2T = m.sb("xn2", [P, TQ, D]), m.sb("xn2T", [P, L])
        xi = m.sb("xi", [P, DB, KC - 1 + L])
        conv_diag = m.sb("conv_diag", [P, DB, KC, P])
        u, zs = m.sb("u", [P, 2, DB, L]), m.sb("zs", [P, 2, DB, L])
        dtl = m.sb("dtl", [DR, L])
        bc_hi, bc_mid, bc_lo = (m.sb(n, [96, L], BF16) for n in ("bc_hi", "bc_mid", "bc_lo"))
        bc_rest, bc = m.sb("bc_rest", [96, L]), m.sb("bc", [96, 2, L], BF16)
        ex, s1, s2 = m.sb("ex", [P, DB, L]), m.sb("s1", [P, DB, L]), m.sb("s2", [P, DB, L])
        dt, dtu = m.sb("dt", [P, 2, DB, L]), m.sb("dtu", [P, 2, DB, L])
        decay, drive, hid, cs, hc = (m.sb(n, [P, 2, DB, L]) for n in ("decay", "drive", "hid", "cs", "hc"))
        y = m.sb("y", [P, DB, L])
        pA, pB = m.ps("pA", [P, L]), m.ps("pB", [P, L])
        psB = [m.ps(f"psB{i}", [P, L]) for i in range(2)]
        psC = [m.ps(f"psC{i}", [P, L]) for i in range(2)]
        psY = [m.ps(f"psY{i}", [P, L]) for i in range(DB)]
        loads = [(t[:], w[n]) for t, n in (
            (w_in, "w_in"), (w_dtl, "w_dtl"), (w_bc, "w_bc"), (w_dt, "w_dt"), (w_out, "w_out"), (conv_w, "conv_w"),
            (conv_b, "conv_b"), (b_dt, "b_dt"), (d_par, "d_par"), (log_a, "log_a"), (ln_w, "ln_w"), (ln_b, "ln_b"),
            (select, "select"))]
        n_loaded = DMA * len(loads)

        (
            loaded, cleared, a_steps, norm_steps, norm2_steps, diag_ready, bc_steps, dt_steps, out_steps, var_ready, seed_ready,
            xn_ready, var2_ready, seed2_ready, xn2_ready, xn2T_ps, xn2T_ready, xi_ps, xi_ready, conv_ps, z_ps, u_ready, low_ps,
            dtl_ready, bc_read, bc_ready, dt_ps, ex_ready, dt_read, dt_ready, dtu_ready, b_ps, c_ps, decay_ready, drive_ready,
            hid_ready, cs_ready, hc_ready, y_added, y_read, y_ready, out_ps, x_done
        ) = (m.sem(n) for n in (
            "loaded", "cleared", "a_steps", "norm_steps", "norm2_steps", "diag_ready", "bc_steps", "dt_steps", "out_steps", "var_ready",
            "seed_ready", "xn_ready", "var2_ready", "seed2_ready", "xn2_ready", "xn2T_ps", "xn2T_ready", "xi_ps",
            "xi_ready", "conv_ps", "z_ps", "u_ready", "low_ps", "dtl_ready", "bc_read", "bc_ready", "dt_ps", "ex_ready",
            "dt_read", "dt_ready", "dtu_ready", "b_ps", "c_ps", "decay_ready", "drive_ready", "hid_ready", "cs_ready", "hc_ready",
            "y_added", "y_read", "y_ready", "out_ps", "x_done"))
        den_ready, inv_ready, zs_ready = (m.sem(n) for n in ("den_ready", "inv_ready", "zs_ready"))
        N_CLEARED = 2

        block = m.block()

        @block.sync
        def _(sp):
            for dst, src in loads:
                sp.dma_start(dst, src).then_inc(loaded, DMA)

        @block.tensor
        def _(pe):
            pe.wait_ge(loaded, n_loaded)

            def emit(t, par, ahead, behind):
                v = t - 1

                def add_up(n):
                    pe.wait_ge(hc_ready, 1 + v * NS + n + 1)
                    if n == 0:
                        pe.wait_ge(y_read, 1 + v)
                    for d in range(DB):
                        ins = pe.matmul(psY[d][:], ident[:], hc[:, n % 2, d], start=(n == 0), stop=(n == NS - 1))
                    ins.then_inc(y_added, 1)

                def spread(n):
                    pe.wait_ge(drive_ready, 1 + v * NS + max(n - 1, 0))
                    pe.matmul(psB[n % 2][:], select[:, n], bc[:, 1 - par], start=True, stop=True).then_inc(b_ps, 1)
                    pe.wait_ge(cs_ready, 1 + v * NS + max(n - 1, 0))
                    pe.matmul(psC[n % 2][:], select[:, NS + n], bc[:, 1 - par], start=True, stop=True).then_inc(c_ps, 1)

                if behind:
                    pe.wait_ge(bc_ready, t)
                    spread(0)
                for n in range(NS):
                    if behind:
                        if n + 1 < NS:
                            spread(n + 1)
                        if n >= 2:
                            add_up(n - 2)
                    if ahead and n == 1:
                        pe.wait_ge(xn2_ready, t + 1)
                        if behind:
                            pe.wait_ge(x_done, t)
                        for q in range(TQ):
                            ins = pe.transpose(pA[:, q * P:(q + 1) * P], xn2[:, q], ident[:])
                        ins.then_inc(xn2T_ps, 1)
                    if ahead and n == 3:
                        pe.wait_ge(xn2T_ready, t + 1)
                        pe.matmul(pA[:], w_in[:, 0], xn2T[:], start=True, stop=True)
                        pe.matmul(pB[:], w_in[:, 1], xn2T[:], start=True, stop=True).then_inc(xi_ps, 1)
                    if ahead and n in (5, 6):
                        if not behind:
                            pe.wait_ge(diag_ready, 1)
                        pe.wait_ge(xi_ready, t + 1)
                        d, dst = n - 5, (pA, pB)[n - 5]
                        for k in range(KC):
                            ins = pe.matmul(dst[:], conv_diag[:, d, k], xi[:, d, k:k + L], start=(k == 0), stop=(k == KC - 1))
                        ins.then_inc(conv_ps, 1)
                    if ahead and n == 8:
                        pe.wait_ge(u_ready, t + 1)
                        for d in range(DB):
                            pe.matmul(pA[0:DR, :], w_dtl[:, d], u[:, par, d], start=(d == 0), stop=(d == DB - 1))
                        for d in range(DB):
                            ins = pe.matmul(pB[0:96, :], w_bc[:, d], u[:, par, d], start=(d == 0), stop=(d == DB - 1))
                        ins.then_inc(low_ps, 1)
                    if ahead and n == 10:
                        pe.wait_ge(dtl_ready, t + 1)
                        pe.wait_ge(bc_read, t + 1)
                        pe.matmul(pA[:], w_dt[:, 0:P], dtl[:], start=True, stop=True)
                        pe.matmul(pB[:], w_dt[:, P:2 * P], dtl[:], start=True, stop=True).then_inc(dt_ps, 1)
                    if ahead and n == 12:
                        pe.wait_ge(ex_ready, t + 1)
                        pe.matmul(pA[:], w_in[:, 2], xn2T[:], start=True, stop=True)
                        pe.matmul(pB[:], w_in[:, 3], xn2T[:], start=True, stop=True).then_inc(z_ps, 1)
                if behind:
                    add_up(NS - 2)
                    add_up(NS - 1)
                    pe.wait_ge(y_ready, t)
                    if ahead:
                        pe.wait_ge(zs_ready, t + 1)
                    for q in range(TQ):
                        for d in range(DB):
                            ins = pe.matmul(pA[:, q * P:(q + 1) * P], y[:, d, q * P:(q + 1) * P], w_out[:, d],
                                            start=(d == 0), stop=(d == DB - 1))
                    ins.then_inc(out_ps, 1)
            turns(pe, emit)

        @block.scalar
        def _(act):
            act.preload_act_table_set("natural_log_exp_and_others")
            act.sem_inc(cs_ready, 1)
            act.sem_inc(decay_ready, 1)

            def norm_seeds(b):
                norm_act(act, st, var_ready, seed_ready, b + 1)
                norm_act(act, st, var2_ready, seed2_ready, b + 1)

            norm_seeds(0)
            act.wait_ge(loaded, n_loaded)
            act.wait_ge(cleared, N_CLEARED)
            act.activation(a_neg[:], log_a[:], ACT.Exp).then_inc(a_steps, 1)
            act.wait_ge(a_steps, 2)

            def emit(t, par, ahead, behind):
                v = t - 1
                for n in range(NS):
                    if behind:
                        if n == 0:
                            act.wait_ge(dt_ready, t)
                        act.wait_ge(hid_ready, 1 + v * NS + max(n - 1, 0))
                        for d in range(DB):
                            ins = act.activation(decay[:, n % 2, d, 1:L], dt[:, 1 - par, d, 1:L], ACT.Exp, scale=a_neg[:, d, n:n + 1])
                        ins.then_inc(decay_ready, 1)
                        act.wait_ge(c_ps, v * NS + n + 1)
                        act.wait_ge(hc_ready, 1 + v * NS + max(n - 1, 0))
                        act.activation(cs[:, n % 2, 0], psC[n % 2][:], ACT.Copy).then_inc(cs_ready, 1)
                    if ahead and n == 2:
                        act.wait_ge(xn2T_ps, t + 1)
                        act.activation(xn2T[:], pA[:], ACT.Copy).then_inc(xn2T_ready, 1)
                    if ahead and n == 4:
                        act.wait_ge(xi_ps, t + 1)
                        act.activation(xi[:, 0, KC - 1:], pA[:], ACT.Copy)
                        act.activation(xi[:, 1, KC - 1:], pB[:], ACT.Copy).then_inc(xi_ready, 1)
                    if ahead and n == 7:
                        act.wait_ge(conv_ps, 2 * t + 2)
                        for d, src in enumerate((pA, pB)):
                            ins = act.activation(u[:, par, d], src[:], ACT.Silu, bias=conv_b[:, d:d + 1])
                        ins.then_inc(u_ready, 1)
                        act.preload_act_table_set("natural_log_exp_and_others")
                    if ahead and n == 9:
                        act.wait_ge(low_ps, t + 1)
                        act.activation(dtl[:], pA[0:DR, :], ACT.Copy).then_inc(dtl_ready, 1)
                    if ahead and n == 11:
                        act.wait_ge(dt_ps, t + 1)
                        act.activation(ex[:, 0], pA[:], ACT.Exp, bias=b_dt[:, 0:1])
                        act.activation(ex[:, 1], pB[:], ACT.Exp, bias=b_dt[:, 1:2]).then_inc(ex_ready, 1)
                    if ahead and n == 12:
                        act.wait_ge(den_ready, t + 1)
                        act.activation(s2[:], s1[:], ACT.Ln).then_inc(inv_ready, 1)
                        act.wait_ge(inv_ready, 2 * t + 1)
                        act.activation(s2[:], s2[:], ACT.Exp, scale=-1.0).then_inc(inv_ready, 1)
                    if ahead and n == 13:
                        act.wait_ge(z_ps, t + 1)
                        act.activation(zs[:, par, 0], pA[:], ACT.Silu)
                        act.activation(zs[:, par, 1], pB[:], ACT.Silu).then_inc(zs_ready, 1)
                        act.preload_act_table_set("natural_log_exp_and_others")
                if has_next(t, ahead):
                    norm_seeds(t + 1)
            turns(act, emit)

        @block.gpsimd
        def _(pool):
            pool.wait_ge(loaded, n_loaded)
            pool.sem_inc(hc_ready, 1)

            def emit(t, par, ahead, behind):
                v = t - 1
                for n in range(NS if behind else 0):
                    pool.wait_ge(hid_ready, 1 + v * NS + n + 1)
                    pool.wait_ge(cs_ready, 1 + v * NS + n + 1)
                    pool.wait_ge(y_added, 1 + v * NS + max(n - 1, 0))
                    pool.tensor_tensor(hc[:, n % 2], hid[:, n % 2], cs[:, n % 2, 0].unsqueeze(1).to_broadcast([P, DB, L]),
                                       ALU.mult).then_inc(hc_ready, 1)
            turns(pool, emit)

        @block.vector
        def _(dve):
            for started in (drive_ready, hid_ready, y_added, y_read, x_done):
                dve.sem_inc(started, 1)
            dve.memset(decay[:], 0.0).then_inc(cleared, 1)
            dve.memset(xi[:], 0.0).then_inc(cleared, 1)
            a = Steps(dve, norm_steps, NORM_STEPS + 1)
            a2 = Steps(dve, norm2_steps, NORM_STEPS + 2)
            bs = Steps(dve, bc_steps, 3)
            ds = Steps(dve, dt_steps, 8)

            def outer_norm(b):
                a.turn(b)
                a.link(norm_dve(dve, a, batch_view(x_sb, b), xc[:], sq[:], st[:], xn[:], var_ready, seed_ready, b + 1))
                xb = batch_view(x_sb, b)
                dve.tensor_tensor(xb, xb, xn[:], ALU.add).then_inc(xn_ready, 1)
                dve.wait_ge(xn_ready, b + 1)
                a.close()

            def inner_norm(b):
                a2.turn(b)
                a2.link(norm_dve(dve, a2, xn[:], xc[:], sq[:], st[:], xn2[:], var2_ready, seed2_ready, b + 1))
                a2.link(dve.tensor_tensor(xn2[:], xn2[:], over_tiles(ln_w[:]), ALU.mult))
                dve.tensor_tensor(xn2[:], xn2[:], over_tiles(ln_b[:]), ALU.add).then_inc(xn2_ready, 1)
                dve.wait_ge(xn2_ready, b + 1)
                a2.close()

            outer_norm(0)
            dve.wait_ge(loaded, n_loaded)
            inner_norm(0)
            dve.wait_ge(a_steps, 1)
            dve.tensor_scalar(a_neg[:], a_neg[:], -1.0, None, ALU.mult).then_inc(a_steps, 1)
            for d in range(DB):
                for k in range(KC):
                    ins = dve.tensor_scalar(conv_diag[:, d, k], ident[:], conv_w[:, d, k:k + 1], None, ALU.mult)
            ins.then_inc(diag_ready, 1)

            def prepare(t, par, slot):
                if slot == 9:
                    bs.turn(t)
                    dve.wait_ge(low_ps, t + 1)
                    bs.link(dve.tensor_copy(bc_hi[:], pB[0:96, :]))
                    bs.link(dve.tensor_tensor(bc_rest[:], pB[0:96, :], bc_hi[:], ALU.subtract))
                    bs.link(dve.tensor_copy(bc_mid[:], bc_rest[:]))
                    dve.tensor_tensor(bc_lo[:], bc_rest[:], bc_mid[:], ALU.subtract).then_inc(bc_read, 1)
                    dve.wait_ge(bc_read, t + 1)
                    bs.close()
                if slot == 10:
                    dve.tensor_copy(bc[0:32, par], bc_hi[0:32])
                    dve.tensor_copy(bc[32:64, par], bc_mid[32:64])
                    dve.tensor_copy(bc[64:96, par], bc_lo[64:96]).then_inc(bc_ready, 1)
                if slot == 12:
                    ds.turn(t)
                    dve.wait_ge(ex_ready, t + 1)
                    ds.link(dve.tensor_scalar(ex[:], ex[:], 0.2, None, ALU.min))
                    dve.tensor_scalar(s1[:], ex[:], 2.0, None, ALU.add).then_inc(den_ready, 1)
                if slot == 13:
                    flat = lambda x: x.rearrange("p d l -> p (d l)")
                    dve.wait_ge(inv_ready, 2 * t + 2)
                    ds.link(dve.tensor_tensor(s1[:], s1[:], s2[:], ALU.mult))
                    ds.link(dve.scalar_tensor_tensor(flat(s2[:]), flat(s1[:]), -2.0, flat(s2[:]), ALU.add, ALU.mult))
                    ds.link(dve.tensor_tensor(s1[:], s2[:], ex[:], ALU.mult))
                    ds.link(dve.tensor_tensor(s2[:], s1[:], s1[:], ALU.mult))
                    ds.link(dve.scalar_tensor_tensor(flat(ex[:]), flat(s2[:]), 7.0 / 5.0, flat(s2[:]), ALU.add, ALU.mult))
                    ds.link(dve.scalar_tensor_tensor(flat(ex[:]), flat(ex[:]), 7.0 / 3.0, flat(s2[:]), ALU.add, ALU.mult))
                    ds.link(dve.scalar_tensor_tensor(flat(ex[:]), flat(ex[:]), 7.0, flat(s1[:]), ALU.add, ALU.mult))
                if slot == 14:
                    dve.tensor_scalar(ex[:], ex[:], -2.0 / 7.0, DT_MIN, ALU.mult, ALU.add).then_inc(dt_read, 1)
                    dve.wait_ge(dt_read, t + 1)
                    dve.tensor_scalar(dt[:, par], ex[:], DT_MIN, DT_MAX, ALU.max, ALU.min).then_inc(dt_ready, 1)
                    dve.wait_ge(dt_ready, t + 1)
                    dve.tensor_tensor(dtu[:, par], dt[:, par], u[:, par], ALU.mult).then_inc(dtu_ready, 1)
                    ds.close()

            def emit(t, par, ahead, behind):
                v = t - 1

                def drives(n):
                    dve.wait_ge(b_ps, v * NS + n + 1)
                    if n == 0:
                        dve.wait_ge(dtu_ready, t)
                    dve.wait_ge(hid_ready, 1 + v * NS + max(n - 1, 0))
                    dve.tensor_tensor(drive[:, n % 2], dtu[:, 1 - par], psB[n % 2][:].unsqueeze(1).to_broadcast([P, DB, L]),
                                      ALU.mult).then_inc(drive_ready, 1)

                if behind:
                    drives(0)
                for n in range(NS):
                    if behind:
                        if n + 1 < NS:
                            drives(n + 1)
                        dve.wait_ge(decay_ready, 1 + v * NS + n + 1)
                        dve.wait_ge(drive_ready, 1 + v * NS + n + 1)
                        dve.wait_ge(hc_ready, 1 + v * NS + max(n - 1, 0))
                        dve.tensor_tensor_scan(hid[:, n % 2].rearrange("p d l -> p (d l)"), decay[:, n % 2].rearrange("p d l -> p (d l)"),
                                               drive[:, n % 2].rearrange("p d l -> p (d l)"), 0.0, ALU.mult, ALU.add).then_inc(hid_ready, 1)
                    if ahead:
                        prepare(t, par, n)
                if has_next(t, ahead):
                    outer_norm(t + 1)
                if behind:
                    dve.wait_ge(y_added, 1 + t * NS)
                    for d in range(DB):
                        ins = dve.scalar_tensor_tensor(y[:, d], u[:, 1 - par, d], d_par[:, d:d + 1], psY[d][:], ALU.mult, ALU.add)
                    ins.then_inc(y_read, 1)
                    dve.wait_ge(y_read, 1 + t)
                    dve.wait_ge(zs_ready, t)
                    dve.tensor_tensor(y[:], y[:], zs[:, 1 - par], ALU.mult).then_inc(y_ready, 1)
                if has_next(t, ahead):
                    inner_norm(t + 1)
                if behind:
                    dve.wait_ge(out_ps, t)
                    xb = batch_view(x_sb, v)
                    dve.tensor_tensor(xb, xb, pA[:].rearrange("p (t d) -> p t d", t=TQ), ALU.add).then_inc(x_done, 1)
                    dve.wait_ge(x_done, 1 + t)
            turns(dve, emit)


TREES = "qkvf"
NODES = 256
LW = 16
NBLK = NODES * LW // P
HALVES = NODES // P
DEPTH = 8
OFF = 2.0 ** 60


def tree_stage(nc, name, x_sb, ident, w):
    with ExitStack() as ctx:
        m = Stage(nc, ctx, name)
        w1 = {r: m.sb("w1" + r, [P, NBLK, P]) for r in TREES}
        w2 = {r: m.sb("w2" + r, [P, NBLK, P]) for r in TREES}
        nodes = {r: m.sb("nodes" + r, [P, NODES]) for r in TREES}
        b1 = m.sb("b1", [P, 4, NBLK])
        nb = m.sb("nb", [P, 4, NODES])
        b2 = m.sb("b2", [P, 3, 4, HALVES, D], BF16)
        pen = m.sb("pen", [P, NBLK // HALVES, P], BF16)
        identb = m.sb("identb", [P, P], BF16)
        pp = m.sb("pp", [P, 2, L])
        work = m.sb("work", [P, 2, L])
        xn, y = m.sb("xn", [P, TQ, D]), m.sb("y", [P, TQ, D])
        st = m.sb("st", [P, 4, TQ])
        xnT, yT = m.sb("xnT", [P, L]), m.sb("yT", [P, L])
        qT, kT, outT = m.sb("qT", [P, L]), m.sb("kT", [P, L]), m.sb("outT", [P, L])
        vtok = m.sb("vtok", [P, TQ, D])
        bits = m.sb("bits", [P, TQ, NODES], BF16)
        path = m.sb("path", [P, TQ, 2 * NODES], BF16)
        leafT, offT = m.sb("leafT", [P, 2, HALVES, L], BF16), m.sb("offT", [P, 2, HALVES, L], BF16)
        h = m.sb("h", [P, 2, L])
        smax, ssum = m.sb("smax", [P, TQ]), m.sb("ssum", [P, TQ])
        psH = [m.ps(f"psH{i}", [P, L]) for i in range(2)]
        psN = [m.ps(f"psN{i}", [P, L]) for i in range(2)]
        psA = [m.ps(f"psA{i}", [P, L]) for i in range(2)]
        psO, psR = m.ps("psO", [P, L]), m.ps("psR", [P, L])
        psRb = psR[:].bitcast(BF16).rearrange("p (a l) -> p a l", a=HALVES)
        probs, probsT = pp[:, 0], pp[:, 1].rearrange("p (k q) -> p k q", k=TQ)
        xc, sq = (work[:, i].rearrange("p (t d) -> p t d", t=TQ) for i in range(2))

        loaded, first_steps, norm_steps, att_steps, var_ready, seed_ready, xn_ready, xn_kept = (
            m.sem(n) for n in ("loaded", "first_steps", "norm_steps", "att_steps", "var_ready", "seed_ready",
                               "xn_ready", "xn_kept"))
        xnT_ps, xnT_ready, s_ps, smax_ready, p_ready, pT_ps, pT_ready, ctx_ps, y_ready, x_half, yT_ps, yT_ready = (
            m.sem(n) for n in ("xnT_ps", "xnT_ready", "s_ps", "smax_ready", "p_ready", "pT_ps", "pT_ready",
                               "ctx_ps", "y_ready", "x_half", "yT_ps", "yT_ready"))
        vtok_ps, vtok_ready, f_tok, x_done = (m.sem(n) for n in ("vtok_ps", "vtok_ready", "f_tok", "x_done"))
        w_loaded, node_ps, path_steps, path_ready, leaf_ps, leaf_ready, up_ps, h_ready, out_ps, out_ready = (
            {r: m.sem(n + r) for r in TREES}
            for n in ("w_loaded_", "node_ps_", "path_steps_", "path_ready_", "leaf_ps_", "leaf_ready_", "up_ps_",
                      "h_ready_", "out_ps_", "out_ready_"))

        small = [(nodes[r][:], w[r + "_nodes"]) for r in TREES]
        small += [(b1[:], w["b1"]), (nb[:], w["nb"]), (pp[:].rearrange("p a l -> p (a l)"), w["b2"]), (pen[:], w["pen"]), (identb[:], w["identb"])]
        n_loaded = DMA * len(small)
        side = {r: i % 2 for i, r in enumerate(TREES)}
        FIRST = 6
        SCALE = float(D ** -0.5)

        def turns_of(eng, turn):
            turn(0, True, False, True)
            with eng.Fori(1, NB - 1) as t:
                turn(t, True, True, True)
            turn(NB - 1, True, True, False)
            turn(NB, False, True, False)

        block = m.block()

        @block.sync
        def _(sp):
            for dst, src in small:
                sp.dma_start(dst, src).then_inc(loaded, DMA)
            for r in TREES:
                sp.dma_start(w1[r][:], w[r + "_w1"]).then_inc(w_loaded[r], DMA)
                sp.dma_start(w2[r][:], w[r + "_w2"]).then_inc(w_loaded[r], DMA)

        @block.tensor
        def _(pe):
            pe.wait_ge(loaded, n_loaded)
            pe.wait_ge(first_steps, FIRST)

            def tree(r, b, srcT, extras):
                def down(j):
                    pe.wait_ge(h_ready[r], b * NBLK + j + 1)
                    if j == 0:
                        n = 0
                        for part in range(3):
                            for half in range(HALVES):
                                pe.matmul(psO[:], b2[:, part, TREES.index(r), half], leafT[:, side[r], half],
                                          start=(n == 0), stop=False)
                                n += 1
                    ins = pe.matmul(psO[:], w2[r][:, j], h[:, j % 2], start=False, stop=(j == NBLK - 1))
                    if j == NBLK - 1:
                        ins.then_inc(out_ps[r], 1)

                for j in range(NBLK):
                    if b is not None:
                        if j == 0:
                            pe.wait_ge(w_loaded[r], 2 * DMA)
                            pe.wait_ge(leaf_ready[r], b + 1)
                        pe.matmul(psH[j % 2][:], pen[:, j % (NBLK // HALVES)], offT[:, side[r], j * HALVES // NBLK],
                                  start=True, stop=False)
                        pe.matmul(psH[j % 2][:], w1[r][:, j], srcT[:], start=False, stop=True).then_inc(up_ps[r], 1)
                    if j in extras:
                        extras[j]()
                    if b is not None and j:
                        down(j - 1)
                if b is not None:
                    down(NBLK - 1)

            def transposed(dst, tok, ready):
                for q in range(TQ):
                    ins = pe.transpose(dst[:, q * P:(q + 1) * P], tok[:, q], ident[:])
                ins.then_inc(ready, 1)

            def node_logits(r, srcT):
                for q in range(TQ):
                    ins = pe.matmul(psN[q // 2][:, q % 2 * NODES:(q % 2 + 1) * NODES], srcT[:, q * P:(q + 1) * P],
                                    nodes[r][:], start=True, stop=True)
                ins.then_inc(node_ps[r], 1)

            def leaves(r, b):
                pe.wait_ge(path_ready[r], b + 1)
                for half in range(HALVES):
                    for q in range(TQ):
                        ins = pe.transpose(psRb[:, half, q * P:(q + 1) * P],
                                           path[:, q, NODES + half * P:NODES + (half + 1) * P], identb[:])
                ins.then_inc(leaf_ps[r], 1)

            def xn_transposed(b):
                pe.wait_ge(xn_ready, b + 1)
                transposed(psA[1], xn, xnT_ps)

            xn_transposed(0)
            pe.wait_ge(xnT_ready, 1)
            node_logits("q", xnT)
            leaves("q", 0)

            def turn(t, cur, prev, nxt):
                u = t - 1
                batch = t if cur else None
                behind = u if prev else None

                def scores(i):
                    if i >= 2:
                        pe.wait_ge(p_ready, u * TQ + i - 1)
                    if i == 0:
                        pe.wait_ge(x_done, 1 + u)
                    pe.matmul(psA[i % 2][:], qT[:, i * P:(i + 1) * P], kT[:], start=True, stop=True).then_inc(s_ps, 1)

                def probs_transposed(i):
                    pe.wait_ge(p_ready, u * TQ + i + 1)
                    for k in range(TQ):
                        ins = pe.transpose(psN[1][:, k * P:(k + 1) * P], probs[:, k * P:(k + 1) * P], ident[:])
                    ins.then_inc(pT_ps, 1)

                def contexts(i):
                    pe.wait_ge(pT_ready, u * TQ + i + 1)
                    for k in range(TQ):
                        ins = pe.matmul(psN[0][:, i * P:(i + 1) * P], probsT[:, k], vtok[:, k],
                                        start=(k == 0), stop=(k == TQ - 1))
                    ins.then_inc(ctx_ps, 1)

                def at_q(slot):
                    if slot == 0 and cur:
                        node_logits("k", xnT)
                    if slot == 7 and cur:
                        leaves("k", t)
                    if prev:
                        i, at = divmod(slot - 8, 4)
                        if at == 0:
                            if i >= 1:
                                probs_transposed(i - 1)
                            if 0 <= i < TQ:
                                scores(i)
                        if at == 3 and i >= 1:
                            contexts(i - 1)
                tree("q", batch, xnT, {s: (lambda s=s: at_q(s)) for s in (0, 7, 8, 12, 15, 16, 19, 20, 23, 24, 27)})

                def at_k(slot):
                    if slot == 0 and prev:
                        pe.wait_ge(y_ready, u + 1)
                        transposed(psA[0], y, yT_ps)
                    if slot == 3 and cur:
                        node_logits("v", xnT)
                    if slot == 10 and cur:
                        leaves("v", t)
                tree("k", batch, xnT, {s: (lambda s=s: at_k(s)) for s in (0, 3, 10)})

                def at_v(slot):
                    if slot == 0 and prev:
                        pe.wait_ge(yT_ready, u + 1)
                        node_logits("f", yT)
                    if slot == 8 and prev:
                        leaves("f", u)
                tree("v", batch, xnT, {s: (lambda s=s: at_v(s)) for s in (0, 8)})

                def at_f(slot):
                    if slot == 1 and cur:
                        pe.wait_ge(out_ready["v"], t + 1)
                        transposed(psR, outT[:].rearrange("p (t d) -> p t d", t=TQ), vtok_ps)
                    if slot == 2 and nxt:
                        xn_transposed(t + 1)
                    if slot == 5 and nxt:
                        pe.wait_ge(xnT_ready, t + 2)
                        node_logits("q", xnT)
                    if slot == 12 and nxt:
                        pe.wait_ge(vtok_ready, t + 1)
                        leaves("q", t + 1)
                tree("f", behind, yT, {s: (lambda s=s: at_f(s)) for s in (1, 2, 5, 12)})
                if prev:
                    pe.wait_ge(out_ready["f"], u + 1)
                    transposed(psA[0], outT[:].rearrange("p (t d) -> p t d", t=TQ), f_tok)
            turns_of(pe, turn)

        @block.scalar
        def _(act):

            def tree(r, b, dst, extras):
                func = ACT.Gelu if r == "f" else ACT.Relu
                i = TREES.index(r)
                for j in range(NBLK):
                    if b is not None:
                        act.wait_ge(up_ps[r], b * NBLK + j + 1)
                        act.activation(h[:, j % 2], psH[j % 2][:], func, bias=b1[:, i, j:j + 1]).then_inc(h_ready[r], 1)
                    if j in extras:
                        extras[j]()
                if b is not None:
                    act.wait_ge(out_ps[r], b + 1)
                    act.activation(dst[:], psO[:], ACT.Copy).then_inc(out_ready[r], 1)

            def xn_transposed(b):
                act.wait_ge(xnT_ps, b + 1)
                act.activation(xnT[:], psA[1][:], ACT.Copy).then_inc(xnT_ready, 1)

            act.preload_act_table_set("natural_log_exp_and_others")
            for i in range(3):
                norm_act(act, st, var_ready, seed_ready, i + 1)
            act.wait_ge(loaded, n_loaded)
            xn_transposed(0)

            def turn(t, cur, prev, nxt):
                u = t - 1
                batch = t if cur else None
                behind = u if prev else None

                def at_q(slot):
                    i = (slot - 9) // 4
                    act.wait_ge(smax_ready, u * TQ + i + 1)
                    act.activation(probs, psA[i % 2][:], ACT.Exp, bias=smax[:, i:i + 1], scale=SCALE,
                                   accum_out=ssum[:, i:i + 1]).then_inc(p_ready, 1)
                tree("q", batch, qT, {s: (lambda s=s: at_q(s)) for s in (9, 13, 17, 21)} if prev else {})

                def y_transposed():
                    act.wait_ge(yT_ps, u + 1)
                    act.activation(yT[:], psA[0][:], ACT.Copy).then_inc(yT_ready, 1)
                tree("k", batch, kT, {1: y_transposed} if prev else {})
                if nxt:
                    act.preload_act_table_set("natural_log_exp_and_others")
                tree("v", batch, outT, {s: (lambda i=i: norm_act(act, st, var_ready, seed_ready, 3 * (t + 1) + i + 1))
                                        for i, s in enumerate((15, 19, 23))} if nxt else {})
                tree("f", behind, outT, {3: lambda: xn_transposed(t + 1)} if nxt else {})
            turns_of(act, turn)

        @block.vector
        def _(dve):
            dve.sem_inc(x_done, 1)
            a = Steps(dve, norm_steps, NORM_STEPS + 15)
            rs = {r: Steps(dve, path_steps[r], 2 + 2 * DEPTH - 1) for r in TREES}
            o = Steps(dve, att_steps, TQ + 1 + TQ)

            def norm(b):
                a.turn(b)
                a.link(norm_dve(dve, a, batch_view(x_sb, b), xc, sq, st[:], xn[:], var_ready, seed_ready, 3 * b + 1))
                a.link(dve.reduce_sum(st[:, 0, :], xn[:], AX.X))
                a.link(dve.tensor_scalar(st[:, 0, :], st[:, 0, :], 1.0 / D, None, ALU.mult))
                a.link(dve.tensor_tensor(xc, xn[:], st[:, 0, :].unsqueeze(2).to_broadcast([P, TQ, D]), ALU.subtract))
                a.link(dve.tensor_tensor(sq, xc, xc, ALU.mult))
                a.link(dve.reduce_sum(st[:, 1, :], sq, AX.X))
                dve.tensor_scalar(st[:, 1, :], st[:, 1, :], 1.0 / (D - 1), 1e-36, ALU.mult, ALU.max).then_inc(var_ready, 1)
                dve.wait_ge(seed_ready, 2 * (3 * b + 2))
                rsqrt_polish(dve, a, st[:, 2, :], st[:, 1, :], st[:, 3, :])
                a.link(dve.tensor_tensor(st[:, 1, :], st[:, 1, :], st[:, 2, :], ALU.mult))
                dve.tensor_scalar(st[:, 1, :], st[:, 1, :], EPS, None, ALU.add).then_inc(var_ready, 1)
                dve.wait_ge(seed_ready, 2 * (3 * b + 3))
                rsqrt_polish(dve, a, st[:, 2, :], st[:, 1, :], st[:, 3, :])
                a.close()
                dve.tensor_tensor(xn[:], xc, st[:, 2, :].unsqueeze(2).to_broadcast([P, TQ, D]), ALU.mult).then_inc(xn_ready, 1)
                dve.wait_ge(xn_ready, b + 1)

            def route(r, b):
                s = rs[r]
                s.turn(b)
                dve.wait_ge(node_ps[r], b + 1)
                for i in range(2):
                    s.did(dve.tensor_tensor(bits[:, 2 * i:2 * i + 2], psN[i][:].rearrange("p (t n) -> p t n", t=2),
                                            nb[:, TREES.index(r)].unsqueeze(1).to_broadcast([P, 2, NODES]), ALU.is_gt))
                s.wait()
                for level in range(DEPTH):
                    n = 2 ** level
                    children = path[:, :, 2 * n:4 * n].rearrange("p t (n two) -> p t n two", two=2)
                    s.link(dve.tensor_tensor(children[:, :, :, 1], path[:, :, n:2 * n], bits[:, :, n - 1:2 * n - 1], ALU.mult))
                    ins = dve.tensor_tensor(children[:, :, :, 0], path[:, :, n:2 * n], children[:, :, :, 1], ALU.subtract)
                    if level + 1 < DEPTH:
                        s.link(ins)
                ins.then_inc(path_ready[r], 1)
                s.close()
                dve.wait_ge(path_ready[r], b + 1)
                dve.wait_ge(leaf_ps[r], b + 1)
                dve.tensor_copy(leafT[:, side[r]], psRb)
                dve.tensor_scalar(offT[:, side[r]], psRb, -1.0, 1.0, ALU.mult, ALU.add).then_inc(leaf_ready[r], 1)

            norm(0)
            dve.wait_ge(loaded, n_loaded)
            first = Steps(dve, first_steps, FIRST)
            raw, rest = (v[:].rearrange("p a l -> p (a l)") for v in (pp, work))
            part = [b2[:, i].rearrange("p r s d -> p (r s d)") for i in range(3)]
            first.link(dve.tensor_copy(part[0], raw))
            first.did(dve.tensor_scalar(nb[:], nb[:], -1.0, None, ALU.mult))
            first.link(dve.tensor_tensor(rest, raw, part[0], ALU.subtract))
            first.link(dve.tensor_copy(part[1], rest))
            first.link(dve.tensor_tensor(part[2], rest, part[1], ALU.subtract))
            first.link(dve.memset(path[:, :, 1:2], 1.0))
            first.close()
            route("q", 0)

            def turn(t, cur, prev, nxt):
                u = t - 1
                if cur:
                    route("k", t)
                if prev:
                    o.turn(u)
                    for i in range(TQ):
                        dve.wait_ge(s_ps, u * TQ + i + 1)
                        o.link(dve.reduce_max(smax[:, i:i + 1], psA[i % 2][:], AX.X))
                        dve.tensor_scalar(smax[:, i:i + 1], smax[:, i:i + 1], -SCALE, None, ALU.mult).then_inc(smax_ready, 1)
                        dve.wait_ge(pT_ps, u * TQ + i + 1)
                        dve.tensor_copy(probsT, psN[1][:].rearrange("p (k q) -> p k q", k=TQ)).then_inc(pT_ready, 1)
                    o.link(dve.reciprocal(ssum[:], ssum[:]))
                    dve.wait_ge(ctx_ps, u * TQ + TQ)
                    for i in range(TQ):
                        o.did(dve.scalar_tensor_tensor(y[:, i], psN[0][:, i * P:(i + 1) * P], ssum[:, i:i + 1], y[:, i],
                                                       ALU.mult, ALU.add))
                    o.wait()
                    o.close()
                    dve.sem_inc(y_ready, 1)
                    xb = batch_view(x_sb, u)
                    dve.tensor_tensor(xb, xb, y[:], ALU.add).then_inc(x_half, 1)
                    dve.wait_ge(x_half, u + 1)
                if cur:
                    route("v", t)
                if prev:
                    route("f", u)
                if cur:
                    dve.tensor_copy(y[:], xn[:]).then_inc(xn_kept, 1)
                    dve.wait_ge(xn_kept, t + 1)
                if nxt:
                    norm(t + 1)
                if cur:
                    dve.wait_ge(vtok_ps, t + 1)
                    dve.tensor_copy(vtok[:], psR[:].rearrange("p (t d) -> p t d", t=TQ)).then_inc(vtok_ready, 1)
                if nxt:
                    route("q", t + 1)
                if prev:
                    dve.wait_ge(f_tok, u + 1)
                    xb = batch_view(x_sb, u)
                    dve.tensor_tensor(xb, xb, psA[0][:].rearrange("p (t d) -> p t d", t=TQ), ALU.add).then_inc(x_done, 1)
                    dve.wait_ge(x_done, 1 + u + 1)
            turns_of(dve, turn)


def program(nc, a, out):
    with ExitStack() as ctx:
        x_sb = ctx.enter_context(nc.sbuf_tensor("x_sb", [P, NB * TQ * D], F32))
        ident = ctx.enter_context(nc.sbuf_tensor("ident", [P, P], F32))
        x_loaded = ctx.enter_context(nc.semaphore("x_loaded"))
        x_stored = ctx.enter_context(nc.semaphore("x_stored"))
        qk_scratch = nc.dram_tensor("qk_scratch", (3, 2, P, L), BF16, kind="Internal").ap()
        mx_scratch = nc.dram_tensor("mx_scratch", (3, 64, P), BF16, kind="Internal").ap()
        m_scratch = nc.dram_tensor("m_scratch", (P, L), F32, kind="Internal").ap()
        with nc.Block() as block:
            @block.sync
            def _(sp):
                sp.dma_start(x_sb[:], a["x"]).then_inc(x_loaded, DMA)
                sp.dma_start(ident[:], a["ident"]).then_inc(x_loaded, DMA)
                sp.wait_ge(x_loaded, 2 * DMA)

        def some(prefix):
            return {k[len(prefix):]: v for k, v in a.items() if k.startswith(prefix)}

        attention_stage(nc, "l0", x_sb, ident, some("l0_"), qk_scratch, mx_scratch, causal=False)
        experts_stage(nc, "l1", x_sb, ident, some("l1_"), "linear")
        sparse_attention_stage(nc, "l2", x_sb, ident, some("l2_"), m_scratch)
        experts_stage(nc, "l3", x_sb, ident, some("l3_"), "swiglu")
        scan_stage(nc, "l4", x_sb, ident, some("l4_"))
        tree_stage(nc, "l5", x_sb, ident, some("l5_"))
        attention_stage(nc, "l6", x_sb, ident, some("l6_"), qk_scratch, mx_scratch, causal=True)
        experts_stage(nc, "l7", x_sb, ident, some("l7_"), "gelu")
        with nc.Block() as block:
            @block.sync
            def _(sp):
                sp.dma_start(out, x_sb[:]).then_inc(x_stored, DMA)
                sp.wait_ge(x_stored, DMA)


def attention_rows(slopes):
    q = np.zeros((R_MAX - NSLOT * HD, H, L), np.float32)
    k = np.zeros((R_ALL - NSLOT * HD, H, L), np.float32)
    at, n = R_EXT - NSLOT * HD, np.arange(L)
    if slopes is None:
        q[at] = 1.0
    else:
        q[at] = q[at + 1] = slopes[:, None]
        k[at], k[at + 1] = n - n % 2, n % 2
        whole = -slopes[:, None] * n
        high = whole.astype(mybir.dt.np(BF16)).astype(np.float32)
        q[at + 2], q[at + 3] = high, whole - high
        k[at + 2] = k[at + 3] = 1.0
    k[at + 4:] = 1.0
    return q.astype(mybir.dt.np(BF16)), k.astype(mybir.dt.np(BF16))


def layout(i):
    bf16 = mybir.dt.np(BF16)
    i = {k: np.asarray(v) for k, v in i.items()}

    def rows(v):
        return np.ascontiguousarray(np.broadcast_to(v.reshape(1, -1), (P, v.size)))

    a = {"x": np.ascontiguousarray(i["L0_attn_x"].reshape(NB * TQ, P, D).transpose(1, 0, 2).reshape(P, -1)),
         "ident": np.eye(P, dtype=np.float32)}
    for n, w, b in (("wq", "Wq", "bq"), ("wk", "Wk", "bk"), ("wv", "Wv", "bv"), ("wo", "Wo", "bo")):
        a["l0_" + n] = i["L0_attn_" + w].T
    a["l0_bqk"] = np.stack([i["L0_attn_bq"], i["L0_attn_bk"]], 1)
    a["l0_bv"], a["l0_bo"] = rows(i["L0_attn_bv"]), rows(i["L0_attn_bo"])
    a["l0_gamma"], a["l0_beta"] = rows(i["L0_attn_gamma"]), rows(i["L0_attn_beta"])
    a["l0_band"] = i["L0_attn_band_importance"]
    a["l0_qext"], a["l0_kext"] = attention_rows(None)

    for n, wt in (("wq", "Wq"), ("wk", "Wk"), ("wv", "Wv"), ("wo", "Wo")):
        a["l2_" + n] = i["L1_attn_" + wt].T
    for n in ("bq", "bv", "bo"):
        a["l2_" + n] = rows(i["L1_attn_" + n])
    a["l2_bqk"] = np.stack([i["L1_attn_bq"], i["L1_attn_bk"]], 1)
    a["l2_idx"] = rows(i["L1_attn_idx_k"])
    a["l2_key_no"] = np.arange(L, dtype=np.float32).reshape(TQ, P).T
    a["l2_head_cols"] = (np.arange(P)[:, None] // HD == np.arange(H)).astype(np.float32)
    a["l2_count_up"] = rows(np.arange(1, U + 1, dtype=np.float32))
    row = np.arange(NC * P) % P + np.arange(NC * P) // P * CU
    a["l2_row_rank"] = (row % U + 1).astype(np.float32).reshape(NC, P).T
    a["l2_block_mask"] = (row[:, None] // U == np.arange(D) // HD).astype(np.float32).reshape(NC, P, D).transpose(1, 0, 2)
    a["l2_spread"] = (np.arange(P)[:, None, None] == np.arange(NB)[:, None] * H + np.arange(HU) // U).astype(bf16)
    a["l2_mean_w"] = np.full((P, P), 1.0 / L, np.float32)
    a["l2_ones"] = np.ones((1, L), np.float32)

    def blocks(v):
        return v.reshape((DB, P) + v.shape[1:]).swapaxes(0, 1)

    a["l4_w_in"] = i["L2_attn_W_in"].T.reshape(P, 4, P)
    wx = i["L2_attn_W_x"].T
    a["l4_w_dtl"] = blocks(wx[:, :DR])
    a["l4_w_bc"] = blocks(np.tile(wx[:, DR:], (1, 3)))
    a["l4_w_dt"], a["l4_w_out"] = i["L2_attn_W_dt"].T, blocks(i["L2_attn_W_out"].T)
    a["l4_conv_w"] = blocks(i["L2_attn_conv_w"][:, 0])
    for n, v in (("conv_b", "conv_b"), ("b_dt", "b_dt"), ("d_par", "D_param"), ("log_a", "log_A")):
        a["l4_" + n] = blocks(i["L2_attn_" + v])
    a["l4_ln_w"], a["l4_ln_b"] = rows(i["L2_attn_ln_w"]), rows(i["L2_attn_ln_b"])
    a["l4_select"] = np.broadcast_to((np.arange(96)[:, None] % 32 == np.arange(2 * NS))[:, :, None], (96, 2 * NS, P)).astype(bf16)

    tree = {r: {n: i[f"L2_ffn_{r}_{n}"] for n in ("nw", "nb", "w1", "b1", "w2", "b2")} for r in TREES}
    for r in TREES:
        v = tree[r]
        a[f"l5_{r}_nodes"] = np.pad(v["nw"], ((0, 1), (0, 0))).T
        a[f"l5_{r}_w1"] = v["w1"].transpose(1, 0, 2).reshape(D, NBLK, P)
        a[f"l5_{r}_w2"] = v["w2"].reshape(NBLK, P, D).transpose(1, 0, 2)
    a["l5_b1"] = np.stack([tree[r]["b1"].reshape(NBLK, P).T for r in TREES], 1)
    a["l5_nb"] = rows(np.stack([np.pad(tree[r]["nb"], (0, 1)) for r in TREES])).reshape(P, 4, NODES)
    a["l5_b2"] = np.stack([tree[r]["b2"].reshape(HALVES, P, D) for r in TREES]).transpose(2, 0, 1, 3).reshape(P, -1)
    leaf = np.arange(NBLK // HALVES)[:, None] * (P // LW) + np.arange(P) // LW
    a["l5_pen"] = (-OFF * (np.arange(P)[:, None, None] == leaf)).astype(bf16)
    a["l5_identb"] = np.eye(P).astype(bf16)

    kv, kvb = i["L3_attn_kv_w"], i["L3_attn_kv_b"]
    a["l6_wq"], a["l6_wk"], a["l6_wv"], a["l6_wo"] = i["L3_attn_q_w"], kv[:, :D], kv[:, D:], i["L3_attn_o_w"]
    a["l6_bqk"] = np.stack([i["L3_attn_q_b"], kvb[:D]], 1)
    a["l6_bv"], a["l6_bo"] = rows(kvb[D:]), rows(i["L3_attn_o_b"])
    a["l6_qext"], a["l6_kext"] = attention_rows(np.arange(1, H + 1, dtype=np.float32) / H)
    a["l6_identb"] = np.eye(P).astype(bf16)
    later = np.triu(np.ones((P, P), np.float32), 1)
    a["l6_above"] = np.stack([-BIG * later.T, -BIG * later], 1).astype(bf16)

    def experts(n, wg, bg, up, b_up, down, b_down):
        ne = down.shape[0]
        a[n + "wg"], a[n + "bg"] = wg, rows(bg)
        a[n + "before"] = np.broadcast_to(np.tril(np.ones((NEG, NEG), np.float32), -1), (P, NEG, NEG))
        a[n + "identb"] = np.eye(P).astype(bf16)
        part, expert = np.divmod(np.arange(3 * ne), ne)
        a[n + "select"] = np.broadcast_to((expert[:, None] == np.arange(ne))[:, :, None], (3 * ne, ne, P)).astype(bf16)
        a[n + "w_down"] = down.reshape(ne, -1, P, D).transpose(2, 0, 1, 3)
        if up is not None:
            a[n + "w_up"] = up.reshape(ne, P, -1, P).transpose(1, 0, 2, 3)
        if b_up is not None:
            a[n + "b_up"] = b_up.reshape(ne, -1, P).transpose(2, 0, 1)
        if b_down is not None:
            a[n + "b_down"] = np.tile(b_down, (3, 1))

    experts("l1_", i["L0_ffn_Wg"], i["L0_ffn_bg"], None, None, i["L0_ffn_We"].transpose(0, 2, 1), i["L0_ffn_be"])
    w1, w3 = (np.concatenate([i["L1_ffn_We" + c], i["L1_ffn_Ws" + c][None]]) for c in "13")
    experts("l3_", i["L1_ffn_Wg"], np.zeros(NEG, np.float32), np.concatenate([w1, w3], 2), None,
            np.concatenate([i["L1_ffn_We2"], i["L1_ffn_Ws2"][None]]), None)
    experts("l7_", i["L3_ffn_gate_w"], i["L3_ffn_gate_b"], i["L3_ffn_w1"], i["L3_ffn_b1"], i["L3_ffn_w2"], i["L3_ffn_b2"])
    a["l7_gamma"], a["l7_beta"] = rows(i["L3_ffn_ln_g"]), rows(i["L3_ffn_ln_b"])
    return {k: np.ascontiguousarray(v) for k, v in a.items()}


def kernel(**inputs):
    import concourse.bacc as bacc
    from concourse.bass_utils import run_bass_kernel_spmd

    nc = bacc.Bacc("TRN2", target_bir_lowering=False, num_devices=1)
    arrays = {f"in_{k}": v for k, v in layout(inputs).items()}
    args = {k[3:]: nc.dram_tensor(k, v.shape, mybir.dt.from_np(v.dtype), kind="ExternalInput").ap() for k, v in arrays.items()}
    out = nc.dram_tensor("out", (P, NB * TQ * D), F32, kind="ExternalOutput").ap()
    program(nc, args, out)
    got = run_bass_kernel_spmd(nc, [arrays], core_ids=[0]).results[0]["out"]
    return np.ascontiguousarray(got.reshape(P, NB * TQ, D).transpose(1, 0, 2)).reshape(NB, L, D)
```
